# Optimizing a Trainium2 kernel written in Bass

```python
import numpy as np
import jax
import jax.numpy as jnp

def _softmax(x, axis=-1):
    return jax.nn.softmax(x, axis=axis)

def _gelu(x):
    return jax.nn.gelu(x, approximate=True)

def _silu(x):
    return jax.nn.silu(x)

def _sigmoid(x):
    return jax.nn.sigmoid(x)

def _layernorm(x, axis=-1, eps=1e-05):
    m = jnp.mean(x, axis=axis, keepdims=True)
    v = jnp.var(x, axis=axis, keepdims=True)
    return (x - m) / jnp.sqrt(v + eps)

def _scatter_add(tgt, idx, src, axis=0):
    return tgt.at[idx].add(src)

def _segment_sum(src, seg, n):
    return jax.ops.segment_sum(src, seg, n)
kernel_name = 'mk_adaln_d2_jaxref_r8_f7acf5'

def setup_inputs(seed: int=0):
    np.random.seed(seed)
    _w = jnp.asarray

    def _L0_attn_setup():
        import jax, jax.numpy as jnp
        import numpy as np
        B, T, C = (8, 256, 256)
        HEAD = 256
        key = jax.random.key(seed)
        ks = jax.random.split(key, 4)
        s = 1.0 / np.sqrt(C)
        return {'x': jax.random.normal(ks[0], (B, T, C), dtype=jnp.float32), 'Wq': jax.random.normal(ks[1], (C, HEAD), dtype=jnp.float32) * s, 'bq': jnp.zeros((HEAD,), dtype=jnp.float32), 'Wk': jax.random.normal(ks[2], (C, HEAD), dtype=jnp.float32) * s, 'bk': jnp.zeros((HEAD,), dtype=jnp.float32), 'Wv': jax.random.normal(ks[3], (C, HEAD), dtype=jnp.float32) * s, 'bv': jnp.zeros((HEAD,), dtype=jnp.float32)}
    _L0_attn_in = _L0_attn_setup()

    def _L0_ffn_setup():
        import jax, jax.numpy as jnp
        import numpy as np
        H = 256
        E = 64
        I = 64
        SI = 64
        TOP_K = 8
        B, T = (2, 64)
        key = jax.random.key(seed)
        ks = jax.random.split(key, 8)
        s = 0.02
        return {'h': jax.random.normal(ks[0], (B, T, H), jnp.float32), 'gate_w': jax.random.normal(ks[1], (E, H), jnp.float32) * s, 'gu_w': jax.random.normal(ks[2], (E, 2 * I, H), jnp.float32) * s, 'dp_w': jax.random.normal(ks[3], (E, H, I), jnp.float32) * s, 'sh_gate_w': jax.random.normal(ks[4], (SI, H), jnp.float32) * s, 'sh_up_w': jax.random.normal(ks[5], (SI, H), jnp.float32) * s, 'sh_down_w': jax.random.normal(ks[6], (H, SI), jnp.float32) * s, 'sh_gate1_w': jax.random.normal(ks[7], (1, H), jnp.float32) * s}
    _L0_ffn_in = _L0_ffn_setup()
    _L0_c = _w((lambda *s: np.random.randn(*s).astype(np.float32) * 0.05)(2, 256))
    _L0_wmod = _w((lambda *s: np.random.randn(*s).astype(np.float32) * 0.05)(256, 6 * 256) * 256 ** (-0.5))

    def _L1_attn_setup():
        import jax, jax.numpy as jnp
        import numpy as np
        B, S, D_IN = (4, 256, 256)
        D_OUT, NUM_HEADS = (256, 16)
        HEAD_DIM = D_OUT // NUM_HEADS
        key = jax.random.key(seed)
        ks = jax.random.split(key, 6)
        s = 0.02
        return {'x': jax.random.normal(ks[0], (B, S, D_IN), dtype=jnp.float32), 'W_query': jax.random.normal(ks[1], (D_IN, D_OUT), dtype=jnp.float32) * s, 'W_key': jax.random.normal(ks[2], (D_IN, D_OUT), dtype=jnp.float32) * s, 'W_value': jax.random.normal(ks[3], (D_IN, D_OUT), dtype=jnp.float32) * s, 'W_out': jax.random.normal(ks[4], (D_OUT, D_OUT), dtype=jnp.float32) * s, 'b_out': jax.random.normal(ks[5], (D_OUT,), dtype=jnp.float32) * s}
    _L1_attn_in = _L1_attn_setup()

    def _L1_ffn_setup():
        import jax, jax.numpy as jnp
        import numpy as np
        HIDDEN = 256
        INTER = 1024
        RETRIEVAL = 128
        NUM_EXPERTS = 512
        NUM_KEYS = 64
        TOP_K = 8
        B, S = (4, 256)
        key = jax.random.key(seed)
        ks = jax.random.split(key, 8)
        sc = 0.02
        return {'hidden_states': jax.random.normal(ks[0], (B, S, HIDDEN), jnp.float32), 'W_q': jax.random.normal(ks[1], (HIDDEN, RETRIEVAL), jnp.float32) * sc, 'keys': jax.random.normal(ks[2], (2, RETRIEVAL // 2, NUM_KEYS), jnp.float32) * sc, 'down_embed': jax.random.normal(ks[3], (NUM_EXPERTS, HIDDEN), jnp.float32) * sc, 'up_embed': jax.random.normal(ks[4], (NUM_EXPERTS, HIDDEN), jnp.float32) * sc, 'gate_w': jax.random.normal(ks[5], (HIDDEN, INTER), jnp.float32) * sc, 'up_w': jax.random.normal(ks[6], (HIDDEN, INTER), jnp.float32) * sc, 'down_w': jax.random.normal(ks[7], (INTER, HIDDEN), jnp.float32) * sc}
    _L1_ffn_in = _L1_ffn_setup()
    _L1_c = _w((lambda *s: np.random.randn(*s).astype(np.float32) * 0.05)(2, 256))
    _L1_wmod = _w((lambda *s: np.random.randn(*s).astype(np.float32) * 0.05)(256, 6 * 256) * 256 ** (-0.5))
    _d = {'L0_attn_x': _L0_attn_in['x'], 'L0_attn_Wq': _L0_attn_in['Wq'], 'L0_attn_bq': _L0_attn_in['bq'], 'L0_attn_Wk': _L0_attn_in['Wk'], 'L0_attn_bk': _L0_attn_in['bk'], 'L0_attn_Wv': _L0_attn_in['Wv'], 'L0_attn_bv': _L0_attn_in['bv'], 'L0_ffn_gate_w': _L0_ffn_in['gate_w'], 'L0_ffn_gu_w': _L0_ffn_in['gu_w'], 'L0_ffn_dp_w': _L0_ffn_in['dp_w'], 'L0_ffn_sh_gate_w': _L0_ffn_in['sh_gate_w'], 'L0_ffn_sh_up_w': _L0_ffn_in['sh_up_w'], 'L0_ffn_sh_down_w': _L0_ffn_in['sh_down_w'], 'L0_ffn_sh_gate1_w': _L0_ffn_in['sh_gate1_w'], 'L0_c': _L0_c, 'L0_wmod': _L0_wmod, 'L1_attn_W_query': _L1_attn_in['W_query'], 'L1_attn_W_key': _L1_attn_in['W_key'], 'L1_attn_W_value': _L1_attn_in['W_value'], 'L1_attn_W_out': _L1_attn_in['W_out'], 'L1_attn_b_out': _L1_attn_in['b_out'], 'L1_ffn_W_q': _L1_ffn_in['W_q'], 'L1_ffn_keys': _L1_ffn_in['keys'], 'L1_ffn_down_embed': _L1_ffn_in['down_embed'], 'L1_ffn_up_embed': _L1_ffn_in['up_embed'], 'L1_ffn_gate_w': _L1_ffn_in['gate_w'], 'L1_ffn_up_w': _L1_ffn_in['up_w'], 'L1_ffn_down_w': _L1_ffn_in['down_w'], 'L1_c': _L1_c, 'L1_wmod': _L1_wmod}
    _x0 = _d['L0_attn_x']
    _d['L0_attn_x'] = jax.random.normal(jax.random.fold_in(jax.random.key(seed), 1), (2, 1024, 256), dtype=_x0.dtype)
    del _x0
    return _d

def reference(L0_attn_x, L0_attn_Wq, L0_attn_bq, L0_attn_Wk, L0_attn_bk, L0_attn_Wv, L0_attn_bv, L0_ffn_gate_w, L0_ffn_gu_w, L0_ffn_dp_w, L0_ffn_sh_gate_w, L0_ffn_sh_up_w, L0_ffn_sh_down_w, L0_ffn_sh_gate1_w, L0_c, L0_wmod, L1_attn_W_query, L1_attn_W_key, L1_attn_W_value, L1_attn_W_out, L1_attn_b_out, L1_ffn_W_q, L1_ffn_keys, L1_ffn_down_embed, L1_ffn_up_embed, L1_ffn_gate_w, L1_ffn_up_w, L1_ffn_down_w, L1_c, L1_wmod):

    def _L0_attn_ref(x, Wq, bq, Wk, bk, Wv, bv):
        import jax, jax.numpy as jnp
        import numpy as np
        B, T, C = (8, 256, 256)
        HEAD = 256
        q = jnp.einsum('btc,ch->bth', x, Wq) + bq
        k = jnp.einsum('btc,ch->bth', x, Wk) + bk
        v = jnp.einsum('btc,ch->bth', x, Wv) + bv
        scale = jnp.asarray(HEAD, x.dtype) ** (-0.5)
        w = jnp.einsum('bqh,bkh->bqk', q, k) * scale
        t = x.shape[1]
        causal = jnp.tril(jnp.ones((t, t), dtype=bool))
        w = jnp.where(causal, w, -jnp.inf)
        w = jax.nn.softmax(w, axis=-1)
        out = jnp.einsum('bqk,bkh->bqh', w, v)
        return out

    def _L0_ffn_ref(h, gate_w, gu_w, dp_w, sh_gate_w, sh_up_w, sh_down_w, sh_gate1_w):
        import jax, jax.numpy as jnp
        import numpy as np
        H = 256
        E = 64
        I = 64
        SI = 64
        TOP_K = 8
        B, T = (2, 64)
        Bb, Tt, Hh = h.shape
        x = h.reshape(Bb * Tt, Hh)
        N = x.shape[0]
        logits = x @ gate_w.T
        topv, topi = jax.lax.top_k(logits, TOP_K)
        rw = jax.nn.softmax(topv.astype(jnp.float32), axis=-1).astype(x.dtype)
        W = jnp.zeros((N, E), x.dtype).at[jnp.arange(N)[:, None], topi].set(rw)
        gu = jnp.einsum('nh,eih->nei', x, gu_w)
        gate, up = (gu[..., :I], gu[..., I:])
        inter = jax.nn.silu(gate) * up
        inter_w = inter * W[:, :, None]
        out = jnp.einsum('nei,ehi->nh', inter_w, dp_w)
        sh_inter = jax.nn.silu(x @ sh_gate_w.T) * (x @ sh_up_w.T)
        sh_out = sh_inter @ sh_down_w.T
        sh_g = jax.nn.sigmoid(x @ sh_gate1_w.T)
        out = out + sh_g * sh_out
        return out.reshape(Bb, Tt, Hh)

    def _L1_attn_ref(x, W_query, W_key, W_value, W_out, b_out):
        import jax, jax.numpy as jnp
        import numpy as np
        B, S, D_IN = (4, 256, 256)
        D_OUT, NUM_HEADS = (256, 16)
        HEAD_DIM = D_OUT // NUM_HEADS
        b, n, _ = x.shape
        q = (x @ W_query).reshape(b, n, NUM_HEADS, HEAD_DIM).transpose(0, 2, 1, 3)
        k = (x @ W_key).reshape(b, n, NUM_HEADS, HEAD_DIM).transpose(0, 2, 1, 3)
        v = (x @ W_value).reshape(b, n, NUM_HEADS, HEAD_DIM).transpose(0, 2, 1, 3)
        scores = jnp.einsum('bhqd,bhkd->bhqk', q, k)
        causal = jnp.triu(jnp.ones((n, n), dtype=bool), k=1)
        scores = jnp.where(causal, -jnp.inf, scores)
        attn = jax.nn.softmax(scores / jnp.sqrt(jnp.float32(HEAD_DIM)), axis=-1)
        ctx = jnp.einsum('bhqk,bhkd->bhqd', attn, v)
        ctx = ctx.transpose(0, 2, 1, 3).reshape(b, n, D_OUT)
        return ctx @ W_out + b_out

    def _L1_ffn_ref(hidden_states, W_q, keys, down_embed, up_embed, gate_w, up_w, down_w):
        import jax, jax.numpy as jnp
        import numpy as np
        HIDDEN = 256
        INTER = 1024
        RETRIEVAL = 128
        NUM_EXPERTS = 512
        NUM_KEYS = 64
        TOP_K = 8
        B, S = (4, 256)
        b, s, h = hidden_states.shape
        n = b * s
        queries = (hidden_states @ W_q).reshape(2, n, RETRIEVAL // 2)
        routing = jnp.einsum('tnd,tdk->tnk', queries, keys)
        scores2, idx2 = jax.lax.top_k(routing, TOP_K)
        sx, sy = (scores2[0], scores2[1])
        ix, iy = (idx2[0], idx2[1])
        all_scores = (sx[:, :, None] + sy[:, None, :]).reshape(n, TOP_K * TOP_K)
        all_idx = (ix[:, :, None] * NUM_KEYS + iy[:, None, :]).reshape(n, TOP_K * TOP_K)
        scores, pk = jax.lax.top_k(all_scores, TOP_K)
        indices = jnp.take_along_axis(all_idx, pk, axis=-1)
        de = down_embed[indices]
        ue = up_embed[indices]
        x = hidden_states.reshape(n, h)
        ew = jnp.einsum('nh,nkh->nk', x, de)
        ew = jax.nn.silu(ew) * jax.nn.softmax(scores, axis=-1)
        experts_states = jnp.einsum('nk,nkh->nh', ew, ue).reshape(b, s, h)
        mlp = jax.nn.silu(x @ gate_w) * (x @ up_w) @ down_w
        return mlp.reshape(b, s, h) + experts_states
    x = L0_attn_x
    mod = (_silu(L0_c) @ L0_wmod).reshape(L0_c.shape[0], 6, 1, -1)
    sa, ca, ga, sb, cb, gb = (mod[:, 0], mod[:, 1], mod[:, 2], mod[:, 3], mod[:, 4], mod[:, 5])
    ga = (2 * (ga >= 0) - 1) * jnp.maximum(jnp.abs(ga), 0.25)
    gb = (2 * (gb >= 0) - 1) * jnp.maximum(jnp.abs(gb), 0.25)
    h = _layernorm(x, axis=-1) * (1 + ca) + sa
    x = x + ga * _L0_attn_ref(h, L0_attn_Wq, L0_attn_bq, L0_attn_Wk, L0_attn_bk, L0_attn_Wv, L0_attn_bv)
    h = _layernorm(x, axis=-1) * (1 + cb) + sb
    x = x + gb * _L0_ffn_ref(h, L0_ffn_gate_w, L0_ffn_gu_w, L0_ffn_dp_w, L0_ffn_sh_gate_w, L0_ffn_sh_up_w, L0_ffn_sh_down_w, L0_ffn_sh_gate1_w)
    mod = (_silu(L1_c) @ L1_wmod).reshape(L1_c.shape[0], 6, 1, -1)
    sa, ca, ga, sb, cb, gb = (mod[:, 0], mod[:, 1], mod[:, 2], mod[:, 3], mod[:, 4], mod[:, 5])
    ga = (2 * (ga >= 0) - 1) * jnp.maximum(jnp.abs(ga), 0.25)
    gb = (2 * (gb >= 0) - 1) * jnp.maximum(jnp.abs(gb), 0.25)
    h = _layernorm(x, axis=-1) * (1 + ca) + sa
    x = x + ga * _L1_attn_ref(h, L1_attn_W_query, L1_attn_W_key, L1_attn_W_value, L1_attn_W_out, L1_attn_b_out)
    h = _layernorm(x, axis=-1) * (1 + cb) + sb
    x = x + gb * _L1_ffn_ref(h, L1_ffn_W_q, L1_ffn_keys, L1_ffn_down_embed, L1_ffn_up_embed, L1_ffn_gate_w, L1_ffn_up_w, L1_ffn_down_w)
    return x

_drawn_inputs = setup_inputs


def setup_inputs(seed=0):
    import zlib

    import numpy as np

    out = dict(_drawn_inputs(seed))
    spreads = {'L0_attn_bq': (0.0, 0.8), 'L0_attn_bk': (0.0, 2.0), 'L0_attn_bv': (0.0, 0.337)}
    factors = {'L0_ffn_gate_w': 8.0,
     'L0_ffn_gu_w': 8.0,
     'L0_ffn_dp_w': 8.0,
     'L0_ffn_sh_gate_w': 8.0,
     'L0_ffn_sh_up_w': 8.0,
     'L0_ffn_sh_down_w': 8.0,
     'L0_ffn_sh_gate1_w': 8.0,
     'L1_attn_W_query': 8.0,
     'L1_attn_W_key': 8.0,
     'L1_attn_W_value': 8.0,
     'L1_attn_W_out': 8.0,
     'L1_attn_b_out': 8.0,
     'L1_ffn_W_q': 64.0,
     'L1_ffn_keys': 64.0,
     'L1_ffn_down_embed': 30.288,
     'L1_ffn_up_embed': 27.44,
     'L1_ffn_gate_w': 6.764,
     'L1_ffn_up_w': 6.688,
     'L1_ffn_down_w': 6.679,
     'L1_c': 5.408,
     'L1_wmod': 5.619}
    for name, (base, spread) in spreads.items():
        noise = np.random.default_rng([zlib.crc32(name.encode()), seed]).standard_normal(out[name].shape)
        drawn = base * np.exp(spread * noise) if base else spread * noise
        out[name] = jnp.asarray(drawn.astype(out[name].dtype))
    for name, factor in factors.items():
        out[name] = (out[name] * factor).astype(out[name].dtype)
    return out
```

```python
from contextlib import ExitStack

import concourse.bass as bass
from concourse import mybir

F32 = mybir.dt.float32
BF16 = mybir.dt.bfloat16
U32 = mybir.dt.uint32
ALU = mybir.AluOpType
ACT = mybir.ActivationFunctionType
AX = mybir.AxisListType

P = 128
BATCH, SEQ, D = 2, 1024, 256
T = BATCH * SEQ
NT = T // P
TB = SEQ // P
KC = D // P
GW = 512
NG = T // GW
GB = SEQ // GW
EPS = 1e-5
E0, I0, TOPK = 64, 64, 8
PAIRS0 = E0 // 2 + 1
HEADS, HD = 16, 16
INTER = 1024
PAIRS1 = INTER // P
R1, NKEY, NEXP = 128, 64, 512
NA = NEXP // NKEY
SA, CA_, GA, SB_, CB, GB_ = range(6)
MASKED = -1.0e30
REPLACED = -3.0e38
C_ID, C_MS, C_MT, C_BLK, C_IOTA, C_RANK, C_SEL, C_SELR = 0, 128, 256, 384, 392, 456, 464, 976
C_N = 1104


def bc(ap, axis, n):
    v = ap.unsqueeze(axis)
    shape = list(v.shape)
    shape[axis] = n
    return v.to_broadcast(shape)


class Tick:

    def __init__(self, sem):
        self.sem, self.n = sem, 0

    def inc(self, ins):
        ins.then_inc(self.sem, 1)
        self.n += 1

    def dma(self, ins):
        ins.then_inc(self.sem, 16)
        self.n += 16


def build(nc, a):
    ctx = ExitStack()

    def sem(name):
        return ctx.enter_context(nc.semaphore(name))

    def sb(stack, name, shape, dt=F32):
        return stack.enter_context(nc.sbuf_tensor(name, shape, dt))

    with ctx:
        wt_dram = nc.dram_tensor("router_weights_t", (2 * PAIRS0, T), F32, kind="Internal").ap()
        qk_dram = nc.dram_tensor("qk_parts", (2, 3, BATCH * D, SEQ), BF16, kind="Internal").ap()
        ctx_dram = nc.dram_tensor("context_t", (BATCH * D, SEQ), F32, kind="Internal").ap()

        ps = ctx.enter_context(nc.psum_tensor("ps", [P, 8, GW], F32))
        consts = sb(ctx, "consts", [P, C_N])
        cbf = sb(ctx, "cbf", [P, 384], BF16)
        x_tok = sb(ctx, "x_tok", [P, NT, D])
        h_t = sb(ctx, "h_t", [P, KC, T])
        xn = sb(ctx, "xn", [P, NT, D])
        stats = sb(ctx, "stats", [P, NT, 6])
        mv = sb(ctx, "mv", [P, NT, 2])
        rstd = sb(ctx, "rstd", [P, NT])
        veps = sb(ctx, "veps", [P, NT])
        half = sb(ctx, "minus_half", [P, NT])
        cond = sb(ctx, "cond", [P, 2, KC, BATCH])
        csilu = sb(ctx, "csilu", [P, 2, KC, BATCH])
        modc = sb(ctx, "modc", [P, 2, 12, BATCH])
        gtmp = sb(ctx, "gtmp", [P, 2, 2, 2, KC, BATCH])
        ident = consts[:, C_ID:C_ID + P]
        ident_b = cbf[:, 0:P]
        mask_s = cbf[:, P:2 * P]
        mask_t = cbf[:, 2 * P:3 * P]
        phase = [0]

        def mod_col(layer, which, c, b):
            return modc[:, layer, which * KC + c, b:b + 1]

        s_var, s_rstd, s_half = sem("ln_var"), sem("ln_rstd"), sem("ln_half")

        def ln_pool(pool, ln):
            for g in range(NG):
                pool.wait_ge(s_var, ln * NG + g + 1)
                nc.gpsimd.tensor_tensor(rstd[:, 4 * g:4 * g + 4], veps[:, 4 * g:4 * g + 4], half[:, 4 * g:4 * g + 4],
                                        ALU.pow).then_inc(s_rstd, 1)

        def ln_dve(dve, g, link, ready, ln):
            for t in range(4 * g, 4 * g + 4):
                last = nc.vector.bn_stats(stats[:, t, :], x_tok[:, t, :])
            link(last)
            for t in range(4 * g, 4 * g + 4):
                last = nc.vector.bn_aggr(mv[:, t, :], stats[:, t, :])
            link(last)
            nc.vector.tensor_scalar(veps[:, 4 * g:4 * g + 4], mv[:, 4 * g:4 * g + 4, 1], EPS, None,
                                    ALU.add).then_inc(s_var, 1)
            dve.wait_ge(s_rstd, ln * NG + g + 1)
            for t in range(4 * g, 4 * g + 4):
                last = nc.vector.tensor_scalar(xn[:, t, :], x_tok[:, t, :], mv[:, t, 0:1], rstd[:, t:t + 1],
                                               ALU.subtract, ALU.mult)
            last.then_inc(ready, 1)

        def ln_transposes(g, bank):
            for c in range(KC):
                for j in range(4):
                    last = nc.tensor.transpose(ps[:, bank + c, j * P:(j + 1) * P],
                                               xn[:, 4 * g + j, c * P:(c + 1) * P], ident)
            return last

        def ln_modulate(layer, shift, scale, g, bank):
            for c in range(KC):
                last = nc.scalar.activation(h_t[:, c, g * GW:(g + 1) * GW], ps[:, bank + c, :], ACT.Identity,
                                            bias=mod_col(layer, shift, c, g // GB),
                                            scale=mod_col(layer, scale, c, g // GB))
            return last

        def chain(name, engine):
            tick = Tick(sem(name))

            def link(ins):
                tick.inc(ins)
                engine.wait_ge(tick.sem, tick.n)
            return link

        def mod_columns(layer, wmod):
            for j in range(12):
                for k in range(KC):
                    last = nc.tensor.matmul(ps[:, 0, 2 * j:2 * j + 2], wmod[:, k, j * P:(j + 1) * P],
                                            csilu[:, layer, k, :], start=k == 0, stop=k == KC - 1)
            return last

        def guard(g, tmp, link):
            link(nc.vector.tensor_scalar(tmp[0], g, 0.0, 2.0, ALU.is_ge, ALU.mult))
            link(nc.vector.scalar_tensor_tensor(tmp[1], g, -1.0, g, ALU.mult, ALU.max))
            link(nc.vector.tensor_scalar(tmp[1], tmp[1], 0.25, None, ALU.max))
            link(nc.vector.scalar_tensor_tensor(g, tmp[0], -1.0, tmp[1], ALU.add, ALU.mult))

        def mod_finish(layer, link):
            m = modc[:, layer, :, :]
            link(nc.vector.tensor_copy(m, ps[:, 0, 0:24].rearrange("p (j b) -> p j b", b=BATCH)))
            for n, which in enumerate((GA, GB_)):
                guard(m[:, which * KC:(which + 1) * KC, :],
                      (gtmp[:, layer, n, 0], gtmp[:, layer, n, 1]), link)
            for which in (CA_, CB):
                part = m[:, which * KC:(which + 1) * KC, :]
                last = nc.vector.tensor_scalar(part, part, 1.0, None, ALU.add)
            return last

        with ExitStack() as st:
            wqkv = sb(st, "wqkv", [P, 3, KC, D])
            bqk = sb(st, "bqk", [P, 2, KC])
            bv = sb(st, "bv", [P, D])
            wmod = sb(st, "wmod0", [P, KC, 6 * D])
            crep = sb(st, "crep", [P, BATCH, KC, P])
            ga = sb(st, "ga_rows", [P, BATCH, D])
            gat = sb(st, "ga_tmp", [P, 2, BATCH, D])
            qt = sb(st, "q_t", [P, KC, T])
            kt = sb(st, "k_t", [P, KC, T])
            vtok = sb(st, "v_tok", [P, NT, D])
            probs = sb(st, "probs", [P, 2, SEQ])
            probs_t = sb(st, "probs_t", [P, 2, SEQ])
            mx = sb(st, "mx", [P, NT])
            nmx = sb(st, "nmx", [P, NT])
            zs = sb(st, "zs", [P, NT])
            rz = sb(st, "rz", [P, NT])
            att = sb(st, "att", [P, 2, D])
            att2 = sb(st, "att2", [P, 2, D])
            s_const, s_cond, s_wmod, s_wqkv, s_bias = [sem(n) for n in
                ("a_const", "a_cond", "a_wmod", "a_wqkv", "a_bias")]
            s_x = [sem(f"a_x{g}") for g in range(NG)]
            s_csilu, s_crep, s_modp, s_modd, s_ln, s_lnt, s_h = [sem(n) for n in
                ("a_csilu", "a_crep", "a_modp", "a_modd", "a_ln", "a_lnt", "a_h")]
            s_proj, s_pev_a, s_pev_d, s_cb = [sem(n) for n in ("a_proj", "a_pev_act", "a_pev_dve", "a_cb")]
            with nc.Block() as block:
                @block.sync
                def _(sp):
                    sp.dma_start(cond[:, :, :, :], a["cond"]).then_inc(s_cond, 16)
                    sp.dma_start(wmod[:, :, :], a["wmod0"].rearrange("(k p) n -> p k n", p=P)).then_inc(s_wmod, 16)
                    for g in range(NG):
                        sp.dma_start(x_tok[:, 4 * g:4 * g + 4, :],
                                     a["x"].rearrange("b (t p) d -> p (b t) d", p=P)[:, 4 * g:4 * g + 4, :])\
                            .then_inc(s_x[g], 16)
                        if g == 0:
                            sp.dma_start(consts[:, :], a["consts"]).then_inc(s_const, 16)
                            for n, w in enumerate(("wq0", "wk0", "wv0")):
                                sp.dma_start(wqkv[:, n], a[w].rearrange("(k p) n -> p k n", p=P))\
                                    .then_inc(s_wqkv, 16)
                            sp.dma_start(bqk[:, 0, :], a["bq0"]).then_inc(s_bias, 16)
                            sp.dma_start(bqk[:, 1, :], a["bk0"]).then_inc(s_bias, 16)
                            sp.dma_start(bv[:, :], a["bv0"].unsqueeze(0).to_broadcast([P, D])).then_inc(s_bias, 16)

                @block.scalar
                def _(act):
                    act.wait_ge(s_cond, 16)
                    nc.scalar.activation(csilu[:, :, :, :], cond[:, :, :, :], ACT.Silu).then_inc(s_csilu, 1)
                    act.wait_ge(s_modd, 1)
                    act.wait_ge(s_bias, 48)
                    for g in range(NG):
                        act.wait_ge(s_lnt, g + 1)
                        ln_modulate(0, SA, CA_, g, 0).then_inc(s_h, 1)
                        for m in range(KC):
                            act.wait_ge(s_proj, 6 * g + m + 1)
                            nc.scalar.activation(qt[:, m, g * GW:(g + 1) * GW], ps[:, 2 + m, :], ACT.Identity,
                                                 bias=bqk[:, 0, m:m + 1]).then_inc(s_pev_a, 1)

                @block.vector
                def _(dve):
                    link = chain("a_dve", dve)
                    dve.wait_ge(s_csilu, 1)
                    for b in range(BATCH):
                        last = nc.vector.tensor_copy(crep[:, b], bc(csilu[:, 0, :, b], 2, P))
                    last.then_inc(s_crep, 1)
                    dve.wait_ge(s_const, 16)
                    nc.vector.tensor_copy(cbf[:, :], consts[:, 0:384]).then_inc(s_cb, 1)
                    dve.wait_ge(s_x[0], 16)
                    ln_dve(dve, 0, link, s_ln, 0)
                    dve.wait_ge(s_modp, 1)
                    link(nc.vector.tensor_copy(ga[:, :, :], ps[:, 1, :].rearrange("p (b d) -> p b d", b=BATCH)))
                    guard(ga[:, :, :], (gat[:, 0], gat[:, 1]), link)
                    mod_finish(0, link).then_inc(s_modd, 1)
                    dve.wait_ge(s_bias, 48)
                    for g in range(NG):
                        if g + 1 < NG:
                            dve.wait_ge(s_x[g + 1], 16)
                            ln_dve(dve, g + 1, link, s_ln, 0)
                        for m in range(KC):
                            dve.wait_ge(s_proj, 6 * g + 2 + m + 1)
                            nc.vector.tensor_scalar(kt[:, m, g * GW:(g + 1) * GW], ps[:, 4 + m, :],
                                                    bqk[:, 1, m:m + 1], None, ALU.add).then_inc(s_pev_d, 1)
                        for m in range(2):
                            dve.wait_ge(s_proj, 6 * g + 4 + m + 1)
                            nc.vector.tensor_copy(vtok[:, 4 * g + 2 * m:4 * g + 2 * m + 2, :],
                                                  ps[:, 6 + m, :].rearrange("p (t d) -> p t d", t=2))\
                                .then_inc(s_pev_d, 1)

                @block.gpsimd
                def _(pool):
                    nc.gpsimd.memset(half[:, :], -0.5).then_inc(s_half, 1)
                    pool.wait_ge(s_half, 1)
                    ln_pool(pool, 0)

                @block.tensor
                def _(pe):
                    pe.wait_ge(s_csilu, 1)
                    pe.wait_ge(s_wmod, 16)
                    mod_columns(0, wmod)
                    pe.wait_ge(s_crep, 1)
                    for b in range(BATCH):
                        for k in range(KC):
                            last = nc.tensor.matmul(ps[:, 1, b * D:(b + 1) * D], crep[:, b, k, :],
                                                    wmod[:, k, GA * D:(GA + 1) * D], start=k == 0, stop=k == KC - 1)
                    last.then_inc(s_modp, 1)
                    pe.wait_ge(s_modd, 1)
                    pe.wait_ge(s_const, 16)
                    pe.wait_ge(s_wqkv, 48)
                    for g in range(NG):
                        pe.wait_ge(s_ln, g + 1)
                        if g:
                            pe.wait_ge(s_h, g)
                        ln_transposes(g, 0).then_inc(s_lnt, 1)
                        pe.wait_ge(s_h, g + 1)
                        for w in range(2):
                            for m in range(KC):
                                if g:
                                    pe.wait_ge(s_pev_a if w == 0 else s_pev_d,
                                               2 * (g - 1) + m + 1 if w == 0 else 4 * (g - 1) + m + 1)
                                for k in range(KC):
                                    last = nc.tensor.matmul(ps[:, 2 + 2 * w + m, :],
                                                            wqkv[:, w, k, m * P:(m + 1) * P],
                                                            h_t[:, k, g * GW:(g + 1) * GW],
                                                            start=k == 0, stop=k == KC - 1)
                                last.then_inc(s_proj, 1)
                        for m in range(2):
                            if g:
                                pe.wait_ge(s_pev_d, 4 * (g - 1) + 2 + m + 1)
                            for i in range(2):
                                t = 4 * g + 2 * m + i
                                for k in range(KC):
                                    last = nc.tensor.matmul(ps[:, 6 + m, i * D:(i + 1) * D],
                                                            h_t[:, k, t * P:(t + 1) * P], wqkv[:, 2, k, :],
                                                            start=k == 0, stop=k == KC - 1)
                            last.then_inc(s_proj, 1)

            s_sc, s_mx, s_exp, s_pt, s_ptd, s_pta, s_av, s_out = [sem(n) for n in
                ("b_scores", "b_max", "b_exp", "b_pt", "b_pt_dve", "b_pt_act", "b_av", "b_out")]
            hi_blocks = [t for t in range(NT) if t % TB >= 4]
            with nc.Block() as block:
                @block.tensor
                def _(pe):
                    def scores(t):
                        b, i = divmod(t, TB)
                        n = (i + 1) * P
                        if t >= 2:
                            pe.wait_ge(s_exp, t - 1)
                        for lo in range(0, n, GW):
                            w = min(GW, n - lo)
                            out = ps[:, 2 * (t % 2) + lo // GW, 0:w]
                            diag = lo + w == n
                            for k in range(KC):
                                last = nc.tensor.matmul(out, qt[:, k, t * P:(t + 1) * P],
                                                        kt[:, k, b * SEQ + lo:b * SEQ + lo + w],
                                                        start=k == 0, stop=k == KC - 1 and not diag)
                            if diag:
                                last = nc.tensor.matmul(out[:, w - P:w], ident_b, mask_s, start=False, stop=True)
                        last.then_inc(s_sc, 1)

                    scores(0)
                    for t in range(NT):
                        b, i = divmod(t, TB)
                        if t + 1 < NT:
                            scores(t + 1)
                        pe.wait_ge(s_exp, t + 1)
                        for j in range(i + 1):
                            if j == 0 and t:
                                pe.wait_ge(s_ptd, t)
                            if j == 4:
                                last.then_inc(s_pt, 1)
                                done = len([u for u in hi_blocks if u < t])
                                if done:
                                    pe.wait_ge(s_pta, done)
                            last = nc.tensor.transpose(ps[:, 4 + j // 4, (j % 4) * P:(j % 4 + 1) * P],
                                                       probs[:, t % 2, j * P:(j + 1) * P], ident)
                        last.then_inc(s_pt, 1)
                        if t >= 2:
                            pe.wait_ge(s_out, t - 1)
                        for j in range(i + 1):
                            if j == 0:
                                pe.wait_ge(s_ptd, t + 1)
                            if j == 4:
                                pe.wait_ge(s_pta, len([u for u in hi_blocks if u <= t]))
                            last = nc.tensor.matmul(ps[:, 6 + t % 2, 0:D], probs_t[:, t % 2, j * P:(j + 1) * P],
                                                    vtok[:, b * TB + j, :], start=j == 0, stop=j == i)
                        last.then_inc(s_av, 1)

                def pt_count(t):
                    return t + len([u for u in hi_blocks if u < t]) + 1

                @block.scalar
                def _(act):
                    for t in range(NT + 1):
                        if t < NT:
                            n = (t % TB + 1) * P
                            act.wait_ge(s_mx, t + 1)
                            nc.scalar.activation(probs[:, t % 2, 0:n],
                                                 ps[:, 2 * (t % 2):2 * (t % 2) + 2, :].rearrange("p a n -> p (a n)")[:, 0:n],
                                                 ACT.Exp, bias=nmx[:, t:t + 1], scale=D ** -0.5,
                                                 accum_out=zs[:, t:t + 1]).then_inc(s_exp, 1)
                        u = t - 1
                        if u in hi_blocks:
                            act.wait_ge(s_pt, pt_count(u) + 1)
                            n = (u % TB + 1) * P
                            nc.scalar.copy(probs_t[:, u % 2, GW:n], ps[:, 5, 0:n - GW]).then_inc(s_pta, 1)

                @block.vector
                def _(dve):
                    link = chain("b_dve", dve)
                    for t in range(NT + 1):
                        if t < NT:
                            n = (t % TB + 1) * P
                            dve.wait_ge(s_sc, t + 1)
                            link(nc.vector.reduce_max(
                                mx[:, t:t + 1],
                                ps[:, 2 * (t % 2):2 * (t % 2) + 2, :].rearrange("p a n -> p (a n)")[:, 0:n], AX.X))
                            nc.vector.tensor_scalar(nmx[:, t:t + 1], mx[:, t:t + 1], -(D ** -0.5), None,
                                                    ALU.mult).then_inc(s_mx, 1)
                        if t >= 1:
                            u = t - 1
                            b = u // TB
                            n = min(u % TB + 1, 4) * P
                            dve.wait_ge(s_pt, pt_count(u))
                            nc.vector.tensor_copy(probs_t[:, u % 2, 0:n], ps[:, 4, 0:n]).then_inc(s_ptd, 1)
                            link(nc.vector.reciprocal(rz[:, u:u + 1], zs[:, u:u + 1]))
                            dve.wait_ge(s_av, u + 1)
                            ins = nc.vector.scalar_tensor_tensor(att[:, u % 2, :], ps[:, 6 + u % 2, 0:D],
                                                                 rz[:, u:u + 1], bv[:, :], ALU.mult, ALU.add)
                            link(ins)
                            link(nc.vector.tensor_tensor(att2[:, u % 2, :], att[:, u % 2, :], ga[:, b, :], ALU.mult))
                            nc.vector.tensor_tensor(x_tok[:, u, :], x_tok[:, u, :], att2[:, u % 2, :],
                                                    ALU.add).then_inc(s_out, 1)

        with ExitStack() as st:
            gw = sb(st, "gate_w_t", [P, KC, E0 + 2])
            lg = sb(st, "logits", [P, NT, E0 + 2])
            lrep = sb(st, "lrep", [P, NT, E0])
            top = sb(st, "top", [P, NT, TOPK])
            ntop = sb(st, "ntop", [P, NT])
            ex = sb(st, "ex", [P, NT, E0])
            sel = sb(st, "sel", [P, NT, E0])
            wts = sb(st, "wts", [P, NT, E0 + 2])
            zsum = sb(st, "zsum", [P, NT])
            esg = sb(st, "esg", [P, NT])
            wt = sb(st, "w_t", [E0 + 2, T])
            s_gw, s_ln, s_lnt, s_h, s_lg, s_lgc, s_lev, s_exd, s_w, s_wtp, s_wte, s_wst = [sem(n) for n in
                ("c_gw", "c_ln", "c_lnt", "c_h", "c_lg", "c_lgc", "c_lev", "c_exd", "c_w", "c_wtp", "c_wte", "c_wst")]
            with nc.Block() as block:
                @block.sync
                def _(sp):
                    sp.dma_start(gw[:, :, :], a["gate0"].rearrange("(k p) e -> p k e", p=P)).then_inc(s_gw, 16)
                    sp.wait_ge(s_wte, NG)
                    sp.dma_start(wt_dram, wt[:, :]).then_inc(s_wst, 16)
                    sp.wait_ge(s_wst, 16)

                @block.scalar
                def _(act):
                    for g in range(NG):
                        act.wait_ge(s_lnt, g + 1)
                        ln_modulate(0, SB_, CB, g, 2 * (g % 2)).then_inc(s_h, 1)
                        act.wait_ge(s_lg, g + 1)
                        nc.scalar.copy(lg[:, 4 * g:4 * g + 4, :],
                                       ps[:, 4 + g % 2, 0:4 * (E0 + 2)].rearrange("p (t e) -> p t e", t=4))\
                            .then_inc(s_lgc, 1)
                    for t in range(NT):
                        act.wait_ge(s_lev, 1)
                        last = nc.scalar.activation(ex[:, t, :], lg[:, t, 0:E0], ACT.Exp, bias=ntop[:, t:t + 1])
                    nc.scalar.activation(esg[:, :], lg[:, :, E0], ACT.Exp, scale=-1.0).then_inc(s_exd, 1)

                @block.vector
                def _(dve):
                    link = chain("c_dve", dve)
                    for g in range(NG):
                        ln_dve(dve, g, link, s_ln, 1)
                    for g in range(NG):
                        dve.wait_ge(s_lgc, g + 1)
                        for t in range(4 * g, 4 * g + 4):
                            last = nc.vector.max(top[:, t, :], lg[:, t, 0:E0])
                        link(last)
                        for t in range(4 * g, 4 * g + 4):
                            last = nc.vector.match_replace(lrep[:, t, :], top[:, t, :], lg[:, t, 0:E0], REPLACED)
                    link(last)
                    nc.vector.tensor_scalar(ntop[:, :], top[:, :, 0], -1.0, None, ALU.mult).then_inc(s_lev, 1)
                    link(nc.vector.tensor_tensor(sel[:, :, :], lrep[:, :, :], lg[:, :, 0:E0], ALU.not_equal))
                    dve.wait_ge(s_exd, 1)
                    link(nc.vector.tensor_tensor(ex[:, :, :], ex[:, :, :], sel[:, :, :], ALU.mult))
                    link(nc.vector.tensor_reduce(zsum[:, :], ex[:, :, :], AX.X, ALU.add))
                    link(nc.vector.reciprocal(zsum[:, :], zsum[:, :]))
                    nc.vector.memset(wts[:, :, E0 + 1:E0 + 2], 0.0)
                    link(nc.vector.tensor_scalar(esg[:, :], esg[:, :], 1.0, None, ALU.add))
                    nc.vector.reciprocal(wts[:, :, E0], esg[:, :])
                    nc.vector.tensor_tensor(wts[:, :, 0:E0], ex[:, :, :], bc(zsum[:, :], 2, E0),
                                            ALU.mult).then_inc(s_w, 1)
                    for g in range(NG):
                        dve.wait_ge(s_wtp, g + 1)
                        nc.vector.tensor_copy(wt[:, g * GW:(g + 1) * GW], ps[0:E0 + 2, 6 + g % 2, :]).then_inc(s_wte, 1)

                @block.gpsimd
                def _(pool):
                    ln_pool(pool, 1)

                @block.tensor
                def _(pe):
                    pe.wait_ge(s_gw, 16)
                    for g in range(NG):
                        pe.wait_ge(s_ln, g + 1)
                        if g >= 2:
                            pe.wait_ge(s_h, g - 1)
                        ln_transposes(g, 2 * (g % 2)).then_inc(s_lnt, 1)
                        pe.wait_ge(s_h, g + 1)
                        if g >= 2:
                            pe.wait_ge(s_lgc, g - 1)
                        for i in range(4):
                            t = 4 * g + i
                            for k in range(KC):
                                last = nc.tensor.matmul(ps[:, 4 + g % 2, i * (E0 + 2):(i + 1) * (E0 + 2)],
                                                        h_t[:, k, t * P:(t + 1) * P], gw[:, k, :],
                                                        start=k == 0, stop=k == KC - 1)
                        last.then_inc(s_lg, 1)
                    pe.wait_ge(s_w, 1)
                    for g in range(NG):
                        if g >= 2:
                            pe.wait_ge(s_wte, g - 1)
                        for i in range(4):
                            last = nc.tensor.transpose(ps[0:E0 + 2, 6 + g % 2, i * P:(i + 1) * P],
                                                       wts[:, 4 * g + i, :], ident)
                        last.then_inc(s_wtp, 1)

        def ffn(tag, layer, pairs, w_ap, weighted, extra, store):
            with ExitStack() as st:
                S = lambda n: sem(f"{tag}_{n}")
                units = 2 * pairs
                xtra = 2 * (NEXP // P) if extra else 0
                allu = units + xtra
                w_sb = sb(st, f"{tag}_w", [P, 2, 3 * D])
                wbc = sb(st, f"{tag}_wbc", [P, 2, SEQ]) if weighted else None
                sg = sb(st, f"{tag}_silu", [P, 4, GW])
                gu = sb(st, f"{tag}_gu", [P, 4, GW]) if weighted else None
                inter = sb(st, f"{tag}_inter", [P, 4, GW])
                out_t = sb(st, f"{tag}_out", [P, KC, SEQ])
                w_in = [S("w0"), S("w1")]
                wb_in = [S("wb0"), S("wb1")]
                s_gu, s_silu, s_t, s_int, s_dn, s_acc, s_tr, s_add, s_store = [S(n) for n in
                    ("gu", "silu", "t", "int", "dn", "acc", "tr", "add", "store")]
                if not weighted:
                    s_int = s_t
                n_slot = [(pairs + 1) // 2, pairs // 2]
                loops = (units - 4) // 4

                with nc.Block() as block:
                    @block.sync
                    def _(sp):
                        def load(b, q, slot, before):
                            first, rows_at = (q * P, q * 2) if isinstance(q, int) else (sp.snap(q * P), sp.snap(q * 2))
                            if before is not None:
                                sp.wait_ge(s_dn, before)
                            sp.dma_start(w_sb[:, slot, :], w_ap[bass.ds(first, P), :]).then_inc(w_in[slot], 16)
                            if weighted:
                                rows = wt_dram[bass.ds(rows_at, 2), b * SEQ:(b + 1) * SEQ]
                                sp.dma_start(wbc[:, slot, :], bc(rows, 1, P // 2)).then_inc(wb_in[slot], 16)

                        for b in range(BATCH):
                            for q in range(2):
                                load(b, q, q, b * allu if b else None)
                            with sp.Fori(0, (pairs - 2) // 2) as it:
                                for q in range(2):
                                    load(b, it * 2 + (2 + q), q, it * 4 + (b * allu + 2 * q + 2))
                            if pairs % 2:
                                load(b, pairs - 1, 0, b * allu + units - 4)
                            if store:
                                for t in range(TB):
                                    sp.wait_ge(s_add, b * TB + t + 1)
                                    sp.dma_start(a["out"][b, t * P:(t + 1) * P, :], x_tok[:, b * TB + t, :])\
                                        .then_inc(s_store, 16)
                        if store:
                            sp.wait_ge(s_store, 16 * NT)

                    def body(b, looped, straight, first):
                        for u in range(first):
                            straight(b, u)
                        looped(b)
                        for u in range(first + 4 * loops, units):
                            straight(b, u)

                    @block.tensor
                    def _(pe):
                        def gate_up(b, u, s, q2):
                            slot, g = (s // 2) % 2, s % 2
                            cols = slice(b * SEQ + g * GW, b * SEQ + (g + 1) * GW)
                            pe.wait_ge(w_in[slot], q2)
                            if not isinstance(u, int) or b or u >= 2:
                                pe.wait_ge(s_t, u + (b * allu - 1))
                            for m in range(2):
                                for k in range(KC):
                                    last = nc.tensor.matmul(ps[:, 2 * g + m, :],
                                                            w_sb[:, slot, k * D + m * P:k * D + (m + 1) * P],
                                                            h_t[:, k, cols], start=k == 0, stop=k == KC - 1)
                            last.then_inc(s_gu, 1)

                        def down(b, u, s, start, stop):
                            slot, g = (s // 2) % 2, s % 2
                            pe.wait_ge(s_int, u + (b * allu + 1))
                            for c in range(KC):
                                last = nc.tensor.matmul(ps[:, 4 + 2 * c + g, :],
                                                        w_sb[:, slot, 2 * D + c * P:2 * D + (c + 1) * P],
                                                        inter[:, s, :], start=start, stop=stop)
                            last.then_inc(s_dn, 1)

                        def step(b, u):
                            if u < units:
                                gate_up(b, u, u % 4, 16 * (b * n_slot[(u // 2) % 2] + u // 4 + 1))
                            elif u < allu:
                                expert_scores(b, u)
                            v = u - 2
                            if 0 <= v:
                                if v < 2 and b:
                                    pe.wait_ge(s_acc, b * 4)
                                if v < units:
                                    down(b, v, v % 4, v < 2, v >= allu - 2)
                                else:
                                    expert_out(b, v)

                        def expert_scores(b, u):
                            e, g = (u - units) // 2, u % 2
                            cols = slice(b * SEQ + g * GW, b * SEQ + (g + 1) * GW)
                            pe.wait_ge(s_t, b * allu + u - 1)
                            for k in range(KC):
                                last = nc.tensor.matmul(ps[:, 2 * g, :], extra[0][:, k, e * P:(e + 1) * P],
                                                        h_t[:, k, cols], start=k == 0, stop=k == KC - 1)
                            last.then_inc(s_gu, 1)

                        def expert_out(b, v):
                            e, g = (v - units) // 2, v % 2
                            pe.wait_ge(s_int, b * allu + v + 1)
                            for c in range(KC):
                                last = nc.tensor.matmul(ps[:, 4 + 2 * c + g, :], extra[1][:, e, c * P:(c + 1) * P],
                                                        inter[:, v % 4, :], start=False, stop=v >= allu - 2)
                            last.then_inc(s_dn, 1)

                        for b in range(BATCH):
                            for u in range(4):
                                step(b, u)
                            with pe.Fori(0, loops) as it:
                                for s in range(4):
                                    gate_up(b, it * 4 + (4 + s), s,
                                            it * 16 + 16 * (b * n_slot[(s // 2) % 2] + 2))
                                    down(b, it * 4 + (2 + s), (2 + s) % 4, False, False)
                            for u in range(4 + 4 * loops, allu + 2):
                                step(b, u)
                            for t in range(TB):
                                pe.wait_ge(s_acc, 4 * b + 4)
                                if t >= 4:
                                    pe.wait_ge(s_add, b * TB + t - 3)
                                for c in range(KC):
                                    last = nc.tensor.transpose(ps[:, t % 4, c * P:(c + 1) * P],
                                                               out_t[:, c, t * P:(t + 1) * P], ident)
                                last.then_inc(s_tr, 1)
                            if b + 1 < BATCH:
                                pe.wait_ge(s_add, (b + 1) * TB)

                    @block.scalar
                    def _(act):
                        def silu(b, u, s, free):
                            act.wait_ge(s_gu, u + (b * allu + 1))
                            if free is not None:
                                act.wait_ge(s_t, free)
                            nc.scalar.activation(sg[:, s, :], ps[:, 2 * (s % 2), :], ACT.Silu).then_inc(s_silu, 1)

                        for b in range(BATCH):
                            for u in range(4):
                                silu(b, u, u, b * allu + u - 3 if b else None)
                            with act.Fori(0, loops) as it:
                                for s in range(4):
                                    silu(b, it * 4 + (4 + s), s, it * 4 + (b * allu + s + 1))
                            for u in range(4 + 4 * loops, allu):
                                silu(b, u, u % 4, b * allu + u - 3)
                            act.wait_ge(s_dn, (b + 1) * allu)
                            for c in range(KC):
                                for g in range(GB):
                                    nc.scalar.activation(out_t[:, c, g * GW:(g + 1) * GW], ps[:, 4 + 2 * c + g, :],
                                                         ACT.Identity, scale=mod_col(layer, GB_, c, b))\
                                        .then_inc(s_acc, 1)

                    @block.vector
                    def _(dve):
                        def product(b, u, s):
                            dve.wait_ge(s_silu, u + (b * allu + 1))
                            if weighted:
                                if not isinstance(u, int) or b or u >= 4:
                                    dve.wait_ge(s_int, u + (b * allu - 3))
                                nc.vector.tensor_tensor(gu[:, s, :], sg[:, s, :], ps[:, 2 * (s % 2) + 1, :],
                                                        ALU.mult).then_inc(s_t, 1)
                            else:
                                if not isinstance(u, int) or b or u >= 4:
                                    dve.wait_ge(s_dn, u + (b * allu - 3))
                                nc.vector.tensor_tensor(inter[:, s, :], sg[:, s, :], ps[:, 2 * (s % 2) + 1, :],
                                                        ALU.mult).then_inc(s_t, 1)

                        for b in range(BATCH):
                            for u in range(4):
                                product(b, u, u)
                            with dve.Fori(0, loops) as it:
                                for s in range(4):
                                    product(b, it * 4 + (4 + s), s)
                            for u in range(4 + 4 * loops, units):
                                product(b, u, u % 4)
                            for u in range(units, allu):
                                e, g = (u - units) // 2, u % 2
                                dve.wait_ge(s_silu, b * allu + u + 1)
                                dve.wait_ge(s_dn, b * allu + u - 3)
                                nc.vector.tensor_tensor(inter[:, u % 4, :], sg[:, u % 4, :],
                                                        extra[2][:, e, b * SEQ + g * GW:b * SEQ + (g + 1) * GW],
                                                        ALU.mult).then_inc(s_t, 1)
                            for t in range(TB):
                                dve.wait_ge(s_tr, b * TB + t + 1)
                                nc.vector.tensor_tensor(x_tok[:, b * TB + t, :], ps[:, t % 4, 0:D],
                                                        x_tok[:, b * TB + t, :], ALU.add).then_inc(s_add, 1)

                    if weighted:
                        @block.gpsimd
                        def _(pool):
                            def weigh(b, u, s, q2):
                                slot, g = (s // 2) % 2, s % 2
                                pool.wait_ge(wb_in[slot], q2)
                                pool.wait_ge(s_t, u + (b * allu + 1))
                                if not isinstance(u, int) or b or u >= 4:
                                    pool.wait_ge(s_dn, u + (b * allu - 3))
                                nc.gpsimd.tensor_tensor(inter[:, s, :], gu[:, s, :],
                                                        wbc[:, slot, g * GW:(g + 1) * GW],
                                                        ALU.mult).then_inc(s_int, 1)

                            for b in range(BATCH):
                                for u in range(4):
                                    weigh(b, u, u, 16 * (b * n_slot[(u // 2) % 2] + u // 4 + 1))
                                with pool.Fori(0, loops) as it:
                                    for s in range(4):
                                        weigh(b, it * 4 + (4 + s), s,
                                              it * 16 + 16 * (b * n_slot[(s // 2) % 2] + 2))
                                for u in range(4 + 4 * loops, allu):
                                    weigh(b, u, u % 4, 16 * (b * n_slot[(u // 2) % 2] + u // 4 + 1))

        ffn("d", 0, PAIRS0, a["moe"], True, None, False)

        with ExitStack() as vst_:
          vu = sb(vst_, "v_heads", [P, BATCH * HEADS, TB, HD])
          with ExitStack() as st:
            wqkv = sb(st, "wqkv1", [P, 3, KC, D])
            wmod = sb(st, "wmod1", [P, KC, 6 * D])
            part1 = sb(st, "part1", [P, 4, GW], BF16)
            part2 = sb(st, "part2", [P, 4, GW], BF16)
            part3 = sb(st, "part3", [P, 4, GW], BF16)
            rest = sb(st, "rest", [P, 2, GW])
            s_wmod, s_w, s_modp, s_modd, s_ln, s_lnt, s_h, s_proj, s_p1, s_p3, s_v = [sem(n) for n in
                ("e_wmod", "e_w", "e_modp", "e_modd", "e_ln", "e_lnt", "e_h", "e_proj", "e_p1", "e_p3", "e_v")]
            s_sts = [sem(f"e_st{i}") for i in range(4)]
            NJ = 4 * NG
            with nc.Block() as block:
                @block.sync
                def _(sp):
                    sp.dma_start(wmod[:, :, :], a["wmod1"].rearrange("(k p) n -> p k n", p=P)).then_inc(s_wmod, 16)
                    for n, w in enumerate(("wq1", "wk1", "wv1")):
                        sp.dma_start(wqkv[:, n], a[w].rearrange("(k p) n -> p k n", p=P)).then_inc(s_w, 16)
                    for j in range(NJ):
                        g, w, m = j // 4, (j // 2) % 2, j % 2
                        b, col = g // GB, (g % GB) * GW
                        sp.wait_ge(s_p3, j + 1)
                        for n, part in enumerate((part1, part2, part3)):
                            sp.dma_start(qk_dram[w, n, b * D + m * P:b * D + (m + 1) * P, col:col + GW],
                                         part[:, j % 4, :]).then_inc(s_sts[j % 4], 16)
                    for i in range(4):
                        sp.wait_ge(s_sts[i], 48 * (NJ // 4))

                @block.scalar
                def _(act):
                    act.wait_ge(s_modd, 1)
                    for g in range(NG):
                        act.wait_ge(s_lnt, g + 1)
                        ln_modulate(1, SA, CA_, g, 0).then_inc(s_h, 1)
                        for j in range(4 * g, 4 * g + 4):
                            act.wait_ge(s_proj, 6 * g + j % 4 + 1)
                            if j >= 4:
                                act.wait_ge(s_sts[j % 4], 48 * (j // 4))
                            nc.scalar.copy(part1[:, j % 4, :], ps[:, 2 + j % 4, :]).then_inc(s_p1, 1)

                @block.vector
                def _(dve):
                    link = chain("e_dve", dve)
                    dve.wait_ge(s_modp, 1)
                    mod_finish(1, link).then_inc(s_modd, 1)
                    ln_dve(dve, 0, link, s_ln, 2)
                    for g in range(NG):
                        if g + 1 < NG:
                            ln_dve(dve, g + 1, link, s_ln, 2)
                        for j in range(4 * g, 4 * g + 4):
                            dve.wait_ge(s_p1, j + 1)
                            r = rest[:, j % 2, :]
                            link(nc.vector.tensor_tensor(r, ps[:, 2 + j % 4, :], part1[:, j % 4, :], ALU.subtract))
                            link(nc.vector.tensor_copy(part2[:, j % 4, :], r))
                            nc.vector.tensor_tensor(part3[:, j % 4, :], r, part2[:, j % 4, :],
                                                    ALU.subtract).then_inc(s_p3, 1)
                        for m in range(2):
                            dve.wait_ge(s_proj, 6 * g + 4 + m + 1)
                            for i in range(2):
                                t = 4 * g + 2 * m + i
                                b, tt = divmod(t, TB)
                                last = nc.vector.tensor_copy(vu[:, b * HEADS:(b + 1) * HEADS, tt, :],
                                                             ps[:, 6 + m, i * D:(i + 1) * D]
                                                             .rearrange("p (h d) -> p h d", h=HEADS))
                            last.then_inc(s_v, 1)

                @block.gpsimd
                def _(pool):
                    ln_pool(pool, 2)

                @block.tensor
                def _(pe):
                    pe.wait_ge(s_wmod, 16)
                    mod_columns(1, wmod).then_inc(s_modp, 1)
                    pe.wait_ge(s_modd, 1)
                    pe.wait_ge(s_w, 48)
                    for g in range(NG):
                        pe.wait_ge(s_ln, g + 1)
                        if g:
                            pe.wait_ge(s_h, g)
                        ln_transposes(g, 0).then_inc(s_lnt, 1)
                        pe.wait_ge(s_h, g + 1)
                        for j in range(4):
                            if g:
                                pe.wait_ge(s_p3, 4 * (g - 1) + j + 1)
                            for k in range(KC):
                                last = nc.tensor.matmul(ps[:, 2 + j, :], wqkv[:, j // 2, k, (j % 2) * P:(j % 2 + 1) * P],
                                                        h_t[:, k, g * GW:(g + 1) * GW], start=k == 0, stop=k == KC - 1)
                            last.then_inc(s_proj, 1)
                        for m in range(2):
                            if g:
                                pe.wait_ge(s_v, 2 * (g - 1) + m + 1)
                            for i in range(2):
                                t = 4 * g + 2 * m + i
                                for k in range(KC):
                                    last = nc.tensor.matmul(ps[:, 6 + m, i * D:(i + 1) * D],
                                                            h_t[:, k, t * P:(t + 1) * P], wqkv[:, 2, k, :],
                                                            start=k == 0, stop=k == KC - 1)
                            last.then_inc(s_proj, 1)

          with ExitStack() as st:
            NU = BATCH * HEADS
            NS = 4
            KR = 6 * HD
            KM = KR + 3 * TB
            qs = sb(st, "qs", [P, NS, SEQ], BF16)
            ks = sb(st, "ks", [P, NS, SEQ], BF16)
            vs = sb(st, "vs", [P, 2, TB, 64])
            ptile = sb(st, "p_tile", [P, 3, GW])
            hmax = sb(st, "hmax", [P, 2, TB])
            hrest = sb(st, "hrest", [P, TB])
            mparts = sb(st, "mparts", [P, P], BF16)
            blk = sb(st, "blk", [P, TB], BF16)
            rz = sb(st, "rz1", [HD, 2, GW])
            cx = sb(st, "cx", [HD, 2, GW])
            qk_in = [sem(f"f_qk{i}") for i in range(NS)]
            s_init, s_v, s_si, s_mx, s_mp, s_row, s_st, s_exp, s_av, s_cx = [sem(n) for n in
                ("f_init", "f_v", "f_s", "f_mx", "f_mp", "f_row", "f_st", "f_exp", "f_av", "f_cx")]
            s_cst = [sem("f_cst0"), sem("f_cst1")]
            s_seen = sem("f_seen")
            NTI = 4 + 8
            tiles = [(0, j) for j in range(4)] + [(1, j) for j in range(8)]
            s_dch = sem("f_dve")
            DCH = 7
            with nc.Block() as block:
                @block.sync
                def _(sp):
                    def load(u, slot, before):
                        row = u * HD if isinstance(u, int) else sp.snap(u * HD)
                        if before is not None:
                            sp.wait_ge(s_av, before)
                        for r, n in ((0, 3), (3 * HD, 2), (5 * HD, 1)):
                            for p in range(n):
                                sp.dma_start(qs[r + p * HD:r + (p + 1) * HD, slot, :],
                                             qk_dram[0, p, bass.ds(row, HD), :]).then_inc(qk_in[slot], 16)
                                sp.dma_start(ks[r + p * HD:r + (p + 1) * HD, slot, :],
                                             qk_dram[1, 3 - n, bass.ds(row, HD), :]).then_inc(qk_in[slot], 16)

                    def store(u, g, count):
                        row = u * HD if isinstance(u, int) else sp.snap(u * HD)
                        sp.wait_ge(s_cx, count)
                        sp.sem_inc(s_seen, 1)
                        sp.dma_start(ctx_dram[bass.ds(row, HD), g * GW:(g + 1) * GW],
                                     cx[:, g, :]).then_inc(s_cst[g], 16)

                    sp.wait_ge(s_init, 2)
                    for u in range(3):
                        load(u, u, None)
                    load(3, 3, None)
                    for g in range(2):
                        store(0, g, g + 1)
                    with sp.Fori(0, (NU - 4) // 4) as it:
                        for s in range(4):
                            load(it * 4 + (4 + s), s, it * (4 * NTI) + NTI * (1 + s))
                            for g in range(2):
                                store(it * 4 + (1 + s), g, it * 8 + (2 * (1 + s) + g + 1))
                    for u in range(NU - 3, NU):
                        for g in range(2):
                            store(u, g, 2 * u + g + 1)
                    for g in range(2):
                        sp.wait_ge(s_cst[g], 16 * NU)

                @block.gpsimd
                def _(pool):
                    nc.gpsimd.memset(vs[:, :, :, :], 0.0)
                    nc.gpsimd.memset(ks[:, :, :], 1.0).then_inc(s_init, 1)
                    nc.gpsimd.memset(qs[:, :, :], 0.0).then_inc(s_init, 1)
                    pool.wait_ge(s_init, 2)
                    nc.gpsimd.memset(vs[:, :, :, 32:48], 1.0).then_inc(s_init, 1)
                    nc.gpsimd.memset(mparts[:, :], 0.0).then_inc(s_init, 1)
                    pool.wait_ge(s_init, 4)

                    def values(u, slot, before):
                        at = u if isinstance(u, int) else pool.snap(u)
                        if before is not None:
                            pool.wait_ge(s_av, before)
                        nc.gpsimd.tensor_copy(vs[:, slot, :, 0:HD], vu[:, bass.ds(at, 1), :, :].rearrange(
                            "p a t d -> p (a t) d")).then_inc(s_v, 1)

                    for u in range(2):
                        values(u, u, None)
                    with pool.Fori(0, (NU - 2) // 2) as it:
                        for s in range(2):
                            values(it * 2 + (2 + s), s, it * (2 * NTI) + NTI * (1 + s))

                @block.tensor
                def _(pe):
                    def s_item(w, u, sl, i):
                        n = w * (TB + 1) + i
                        half = n % 2
                        cnt = u * TB + i
                        if i < TB:
                            if i == 0:
                                pe.wait_ge(qk_in[sl], pe_loads(u, sl))
                            if i == 0:
                                if not (isinstance(u, int) and u == 0):
                                    pe.wait_ge(s_mx, u * TB)
                            elif i == 1:
                                if not (isinstance(u, int) and u == 0):
                                    pe.wait_ge(s_row, u)
                            else:
                                pe.wait_ge(s_mx, cnt - 1)
                            k = (i + 1) * P
                            for lo in range(0, k, GW):
                                wd = min(GW, k - lo)
                                diag = lo + wd == k
                                out = ps[:, 2 * half + lo // GW, 0:wd]
                                last = nc.tensor.matmul(out, qs[0:KR, sl, i * P:(i + 1) * P],
                                                        ks[0:KR, sl, lo:lo + wd], start=True, stop=not diag)
                                if diag:
                                    last = nc.tensor.matmul(out[:, wd - P:wd], ident_b, mask_s, start=False, stop=True)
                            last.then_inc(s_si, 1)
                        else:
                            pe.wait_ge(s_mx, u * TB + TB)
                            pe.wait_ge(s_mp, u + 1)
                            nc.tensor.transpose(ps[:, 2 * half, 0:64].bitcast(BF16), mparts[:, :],
                                                ident_b).then_inc(s_si, 1)

                    def pe_loads(u, sl):
                        return (u - sl) * (192 // 4) + 192

                    def st_tile(u, sl, n):
                        g, j = tiles[n]
                        q0 = max(4 * g, j)
                        wd = (4 * g + 4 - q0) * P
                        if n == 0:
                            pe.wait_ge(s_row, u + 1)
                        if not (isinstance(u, int) and u == 0 and n < 2):
                            pe.wait_ge(s_exp, u * NTI + (n - 1))
                        diag = j >= 4 * g
                        out = ps[:, 4 + n % 2, 0:wd]
                        last = nc.tensor.matmul(out, ks[0:KM, sl, j * P:(j + 1) * P],
                                                qs[0:KM, sl, q0 * P:q0 * P + wd], start=True, stop=not diag)
                        if diag:
                            last = nc.tensor.matmul(out[:, 0:P], ident_b, mask_t, start=False, stop=True)
                        last.then_inc(s_st, 1)

                    def av_tile(u, par, n):
                        g, j = tiles[n]
                        q0 = max(4 * g, j)
                        off = (q0 - 4 * g) * P
                        if n == 0:
                            pe.wait_ge(s_v, u + 1)
                        if j == 0 and not (isinstance(u, int) and u == 0):
                            pe.wait_ge(s_cx, u * 2 + (g - 1))
                        pe.wait_ge(s_exp, u * NTI + (n + 1))
                        nc.tensor.matmul(ps[0:64, 6 + g, off:GW], vs[:, par, j, :], ptile[:, n % 3, 0:GW - off],
                                         start=j == 0, stop=j == 4 * g + 3).then_inc(s_av, 1)

                    def unit(u, s, ahead):
                        for n in range(NTI + 1):
                            if n < NTI:
                                st_tile(u, s % NS, n)
                            if ahead and n < TB:
                                s_item((s + 1) % 4, u + 1, (s + 1) % NS, n)
                            if ahead and n == TB + 1:
                                s_item((s + 1) % 4, u + 1, (s + 1) % NS, TB)
                            if n:
                                av_tile(u, s % 2, n - 1)

                    for i in range(TB + 1):
                        s_item(0, 0, 0, i)
                    unit(0, 0, True)
                    with pe.Fori(0, (NU - 4) // 4) as it:
                        for s in range(4):
                            unit(it * 4 + (1 + s), 1 + s, True)
                    for u in range(NU - 3, NU):
                        unit(u, u % 4, u < NU - 1)

                @block.scalar
                def _(act):
                    def exps(u):
                        for n in range(NTI):
                            g, j = tiles[n]
                            wd = (4 * g + 4 - max(4 * g, j)) * P
                            act.wait_ge(s_st, u * NTI + (n + 1))
                            if not (isinstance(u, int) and u == 0 and n < 3):
                                act.wait_ge(s_av, u * NTI + (n - 2))
                            nc.scalar.activation(ptile[:, n % 3, 0:wd], ps[:, 4 + n % 2, 0:wd], ACT.Exp,
                                                 scale=HD ** -0.5).then_inc(s_exp, 1)

                    exps(0)
                    with act.Fori(0, NU - 1) as it:
                        exps(it + 1)

                @block.vector
                def _(dve):
                    dve.wait_ge(s_init, 4)
                    nc.vector.tensor_copy(blk[:, :], consts[:, C_BLK:C_BLK + TB]).then_inc(s_dch, 1)
                    dve.wait_ge(s_dch, 1)

                    def maxima(w, u, i):
                        half = (w * (TB + 1) + i) % 2
                        k = (i + 1) * P
                        dve.wait_ge(s_si, u * (TB + 1) + (i + 1))
                        nc.vector.reduce_max(hmax[:, w % 2, i:i + 1],
                                             ps[:, 2 * half:2 * half + 2, :].rearrange("p a n -> p (a n)")[:, 0:k],
                                             AX.X).then_inc(s_mx, 1)

                    def minus_max(w, u):
                        m = hmax[:, w % 2, :]
                        parts = [mparts[:, KR + n * TB:KR + (n + 1) * TB] for n in range(3)]
                        dve.wait_ge(s_mx, u * TB + TB)
                        if not (isinstance(u, int) and u == 0):
                            dve.wait_ge(s_row, u)
                        link(nc.vector.tensor_scalar(parts[0], m, -1.0, None, ALU.mult), u, 0)
                        link(nc.vector.scalar_tensor_tensor(hrest[:, :], m, -1.0, parts[0], ALU.mult, ALU.subtract), u, 1)
                        link(nc.vector.tensor_copy(parts[1], hrest[:, :]), u, 2)
                        nc.vector.tensor_tensor(parts[2], hrest[:, :], parts[1], ALU.subtract).then_inc(s_mp, 1)

                    def max_rows(w, u):
                        half = (w * (TB + 1) + TB) % 2
                        dve.wait_ge(s_si, u * (TB + 1) + (TB + 1))
                        rows = slice(KR, KM)
                        nc.vector.tensor_tensor(qs[rows, w % NS, :].rearrange("p (i q) -> p i q", i=TB),
                                                bc(ps[rows, 2 * half, 0:64].bitcast(BF16), 1, TB),
                                                bc(blk[rows, :], 2, P), ALU.mult).then_inc(s_row, 1)

                    def context(u, g):
                        dve.wait_ge(s_av, u * NTI + (4 if g == 0 else 12))
                        if not (isinstance(u, int) and u == 0):
                            dve.wait_ge(s_cst[g], u * 16)
                        link(nc.vector.reciprocal(rz[:, g, :], ps[32:32 + HD, 6 + g, :]), u, 3 + g)
                        nc.vector.tensor_tensor(cx[:, g, :], ps[0:HD, 6 + g, :], rz[:, g, :],
                                                ALU.mult).then_inc(s_cx, 1)

                    def link(ins, u, k):
                        ins.then_inc(s_dch, 1)
                        dve.wait_ge(s_dch, seq(u, k))

                    def seq(u, k):
                        if k < 3:
                            if isinstance(u, int) and u == 0:
                                return 1 + k + 1
                            return u * 5 + (1 + 3 - 5 + 1 + k + 1)
                        return u * 5 + (1 + 3 + 1) if k == 3 else u * 5 + last_link[0]

                    last_link = [1 + 3 + 5]
                    for i in range(TB):
                        maxima(0, 0, i)
                    minus_max(0, 0)
                    max_rows(0, 0)

                    def unit(u, s, ahead):
                        if ahead:
                            for i in range(5):
                                maxima((s + 1) % 4, u + 1, i)
                        context(u, 0)
                        if ahead:
                            for i in range(5, TB):
                                maxima((s + 1) % 4, u + 1, i)
                            minus_max((s + 1) % 4, u + 1)
                            max_rows((s + 1) % 4, u + 1)
                        context(u, 1)

                    unit(0, 0, True)
                    with dve.Fori(0, (NU - 4) // 4) as it:
                        for s in range(4):
                            unit(it * 4 + (1 + s), 1 + s, True)
                    for u in range(NU - 3, NU - 1):
                        unit(u, u % 4, True)
                    last_link[0] = 1 + 3 + 2
                    unit(NU - 1, (NU - 1) % 4, False)

        with ExitStack() as st:
            wo = sb(st, "wo", [P, KC, D])
            bo = sb(st, "bo", [P, KC])
            cxt = sb(st, "cxt", [P, BATCH, KC, SEQ])
            out_t = sb(st, "att_out_t", [P, KC, T])
            s_w, s_c, s_o, s_oe, s_tr, s_add = [sem(n) for n in ("g_w", "g_c", "g_o", "g_oe", "g_tr", "g_add")]
            with nc.Block() as block:
                @block.sync
                def _(sp):
                    sp.dma_start(wo[:, :, :], a["wo1"].rearrange("(k p) n -> p k n", p=P)).then_inc(s_w, 16)
                    sp.dma_start(bo[:, :], a["bo1"]).then_inc(s_w, 16)
                    sp.dma_start(cxt[:, :, :, :], ctx_dram.rearrange("(b k p) n -> p b k n", b=BATCH, p=P))\
                        .then_inc(s_c, 16)

                @block.tensor
                def _(pe):
                    pe.wait_ge(s_w, 32)
                    pe.wait_ge(s_c, 16)
                    for g in range(NG):
                        for m in range(KC):
                            if g >= 2:
                                pe.wait_ge(s_oe, 2 * (g - 2) + m + 1)
                            for k in range(KC):
                                last = nc.tensor.matmul(ps[:, 2 * (g % 2) + m, :], wo[:, k, m * P:(m + 1) * P],
                                                        cxt[:, g // GB, k, (g % GB) * GW:(g % GB + 1) * GW],
                                                        start=k == 0, stop=k == KC - 1)
                            last.then_inc(s_o, 1)
                        pe.wait_ge(s_oe, 2 * g + 2)
                        for t in range(4 * g, 4 * g + 4):
                            if t >= 4:
                                pe.wait_ge(s_add, t - 3)
                            for c in range(KC):
                                last = nc.tensor.transpose(ps[:, 4 + t % 4, c * P:(c + 1) * P],
                                                           out_t[:, c, t * P:(t + 1) * P], ident)
                            last.then_inc(s_tr, 1)

                @block.vector
                def _(dve):
                    dve.wait_ge(s_w, 32)
                    for g in range(NG):
                        for m in range(KC):
                            dve.wait_ge(s_o, 2 * g + m + 1)
                            nc.vector.tensor_scalar(out_t[:, m, g * GW:(g + 1) * GW], ps[:, 2 * (g % 2) + m, :],
                                                    bo[:, m:m + 1], mod_col(1, GA, m, g // GB),
                                                    ALU.add, ALU.mult).then_inc(s_oe, 1)
                        for t in range(4 * g, 4 * g + 4):
                            dve.wait_ge(s_tr, t + 1)
                            nc.vector.tensor_tensor(x_tok[:, t, :], ps[:, 4 + t % 4, 0:D], x_tok[:, t, :],
                                                    ALU.add).then_inc(s_add, 1)

        with ExitStack() as keep:
            de = sb(keep, "de_t", [P, KC, NEXP])
            ue = sb(keep, "ue", [P, NEXP // P, D])
            pexp = sb(keep, "pexp", [P, NEXP // P, T])
            with ExitStack() as st:
                wq = sb(st, "wq_r", [P, KC, R1])
                keys = sb(st, "keys", [P, 2, NKEY])
                qr = sb(st, "qr", [P, T])
                rt = sb(st, "rt", [P, NT, 2, NKEY])
                srt = sb(st, "srt", [P, NT, 2, TOPK])
                ids = sb(st, "ids", [P, NT, 2, TOPK], U32)
                idf = sb(st, "idf", [P, NT, 2, TOPK])
                cand = sb(st, "cand", [P, NT, TOPK, TOPK])
                csel = sb(st, "csel", [P, NT, TOPK, TOPK])
                cprob = sb(st, "cprob", [P, NT, TOPK, TOPK])
                ctop = sb(st, "ctop", [P, NT, TOPK])
                cntj = sb(st, "cntj", [P, NT, TOPK])
                rowp = sb(st, "rowp", [P, NT, TOPK])
                far = sb(st, "far", [P, NT, TOPK])
                zc = sb(st, "zc", [P, NT])
                lnz = sb(st, "lnz", [P, NT])
                rzc = sb(st, "rzc", [P, NT])
                far_s = sb(st, "far_s", [P, NT])
                eq = sb(st, "eq", [P, 2, NKEY, TOPK])
                eqa = sb(st, "eqa", [P, NT, NA, TOPK])
                us = sb(st, "us", [P, NT, NA + NKEY + 1])
                ud = sb(st, "ud", [P, NT, NA + NKEY])
                ust = sb(st, "us_t", [NA + NKEY + 1, T])
                udt = sb(st, "ud_t", [NA + NKEY, T])
                pex = sb(st, "pex", [P, 2, GW])
                s_in, s_ln, s_lnt, s_h, s_q, s_qe, s_r, s_re, s_cd, s_ce, s_zd, s_lz, s_u, s_ut, s_ute, s_ex, s_pe, \
                    s_pm, s_l = [sem(f"h_{n}") for n in ("in", "ln", "lnt", "h", "q", "qe", "r", "re", "cd", "ce",
                                                         "zd", "lz", "u", "ut", "ute", "ex", "pe", "pm", "l")]
                iota = consts[:, C_IOTA:C_IOTA + NKEY]
                rank = consts[:, C_RANK:C_RANK + TOPK]
                NM = 4 * NG
                with nc.Block() as block:
                    @block.sync
                    def _(sp):
                        sp.dma_start(wq[:, :, :], a["wq_r"].rearrange("(k p) n -> p k n", p=P)).then_inc(s_in, 16)
                        for half in range(2):
                            sp.dma_start(keys[half * 64:(half + 1) * 64, :, :],
                                         a["keys"].rearrange("t d k -> d t k")).then_inc(s_in, 16)
                        sp.dma_start(de[:, :, :], a["de_t"].rearrange("(k p) e -> p k e", p=P)).then_inc(s_l, 16)
                        sp.dma_start(ue[:, :, :], a["ue"].rearrange("(e p) h -> p e h", p=P)).then_inc(s_l, 16)
                        sp.wait_ge(s_l, 32)

                    @block.scalar
                    def _(act):
                        for g in range(NG):
                            act.wait_ge(s_lnt, g + 1)
                            ln_modulate(1, SB_, CB, g, 0).then_inc(s_h, 1)
                            act.wait_ge(s_q, g + 1)
                            nc.scalar.copy(qr[:, g * GW:(g + 1) * GW], ps[:, 2 + g % 2, :]).then_inc(s_qe, 1)
                        for n in range(TB):
                            act.wait_ge(s_r, n + 1)
                            nc.scalar.copy(rt[:, 2 * n:2 * n + 2, :, :],
                                           ps[:, 4 - 2 * (n % 2):6 - 2 * (n % 2), 0:2 * NKEY]
                                           .rearrange("p h (t k) -> p h t k", t=2)).then_inc(s_re, 1)
                        act.wait_ge(s_cd, 1)
                        nc.scalar.activation(cprob[:, :, :, :], cand[:, :, :, :], ACT.Exp).then_inc(s_ce, 1)
                        act.wait_ge(s_zd, 1)
                        nc.scalar.activation(lnz[:, :], zc[:, :], ACT.Ln).then_inc(s_lz, 1)
                        for j in range(NM):
                            act.wait_ge(s_ex, 2 * j + 1)
                            if j >= 2:
                                act.wait_ge(s_pe, j - 1)
                            nc.scalar.activation(pex[:, j % 2, :], ps[:, 2 * (j % 2), :], ACT.Exp).then_inc(s_pm, 1)

                    @block.vector
                    def _(dve):
                        link = chain("h_dve", dve)
                        for g in range(NG):
                            ln_dve(dve, g, link, s_ln, 3)
                        for n in range(TB):
                            dve.wait_ge(s_re, n + 1)
                            for t in range(2 * n, 2 * n + 2):
                                for w in range(2):
                                    last = nc.vector.max(srt[:, t, w, :], rt[:, t, w, :])
                            link(last)
                            for t in range(2 * n, 2 * n + 2):
                                for w in range(2):
                                    last = nc.vector.max_index(ids[:, t, w, :], srt[:, t, w, :], rt[:, t, w, :])
                        link(last)
                        link(nc.vector.tensor_copy(idf[:, :, :, :], ids[:, :, :, :]))
                        for t in range(NT):
                            last = nc.vector.tensor_tensor(cand[:, t], bc(srt[:, t, 0, :], 2, TOPK),
                                                           bc(srt[:, t, 1, :], 1, TOPK), ALU.add)
                        link(last)
                        for t in range(NT):
                            last = nc.vector.max(ctop[:, t, :], cand[:, t].rearrange("p i j -> p (i j)"))
                        link(last)
                        for t in range(NT):
                            last = nc.vector.match_replace(csel[:, t].rearrange("p i j -> p (i j)"), ctop[:, t, :],
                                                           cand[:, t].rearrange("p i j -> p (i j)"), REPLACED)
                        link(last)
                        flat = lambda v: v[:, :, :, :].rearrange("p t i j -> p t (i j)")
                        link(nc.vector.tensor_tensor(flat(csel), flat(csel), flat(cand), ALU.not_equal))
                        nc.vector.tensor_tensor(flat(cand), flat(cand), bc(ctop[:, :, 0], 2, 64),
                                                ALU.subtract).then_inc(s_cd, 1)
                        link(nc.vector.tensor_reduce(cntj[:, :, :], csel[:, :, :, :], AX.X, ALU.add))
                        for t in range(NT):
                            last = nc.vector.tensor_tensor(eqa[:, t], bc(idf[:, t, 0, :], 1, NA),
                                                           bc(iota[:, 0:NA], 2, TOPK), ALU.is_equal)
                        link(last)
                        for t in range(NT):
                            last = nc.vector.tensor_tensor(eqa[:, t], eqa[:, t], bc(cntj[:, t, :], 1, NA), ALU.mult)
                        link(last)
                        link(nc.vector.tensor_reduce(ud[:, :, 0:NA], eqa[:, :, :, :], AX.X, ALU.add))
                        for t in range(NT):
                            e = eq[:, t % 2, :, :]
                            link(nc.vector.tensor_tensor(e, bc(idf[:, t, 1, :], 1, NKEY), bc(iota, 2, TOPK),
                                                         ALU.is_equal))
                            link(nc.vector.tensor_tensor(e, e, bc(rank, 1, NKEY), ALU.mult))
                            last = nc.vector.tensor_reduce(ud[:, t, NA:], e, AX.X, ALU.add)
                        link(last)
                        dve.wait_ge(s_ce, 1)
                        link(nc.vector.tensor_tensor(flat(cprob), flat(cprob), flat(csel), ALU.mult))
                        link(nc.vector.tensor_reduce(rowp[:, :, :], cprob[:, :, :, :], AX.X, ALU.add))
                        link(nc.vector.tensor_reduce(zc[:, :], rowp[:, :, :], AX.X, ALU.add))
                        link(nc.vector.reciprocal(rzc[:, :], zc[:, :]))
                        nc.vector.tensor_scalar(far[:, :, :], idf[:, :, 0, :], float(NA), None,
                                                ALU.is_ge).then_inc(s_zd, 1)
                        dve.wait_ge(s_zd, 1)
                        link(nc.vector.tensor_tensor(far[:, :, :], far[:, :, :], rowp[:, :, :], ALU.mult))
                        link(nc.vector.tensor_reduce(far_s[:, :], far[:, :, :], AX.X, ALU.add))
                        nc.vector.tensor_tensor(us[:, :, NA + NKEY], far_s[:, :], rzc[:, :], ALU.mult)
                        nc.vector.tensor_tensor(us[:, :, NA:NA + NKEY], rt[:, :, 1, :], bc(srt[:, :, 1, 0], 2, NKEY),
                                                ALU.subtract)
                        link(nc.vector.tensor_tensor(us[:, :, 0:NA], rt[:, :, 0, 0:NA], bc(srt[:, :, 0, 0], 2, NA),
                                                     ALU.subtract))
                        dve.wait_ge(s_lz, 1)
                        nc.vector.tensor_tensor(us[:, :, 0:NA], us[:, :, 0:NA], bc(lnz[:, :], 2, NA),
                                                ALU.subtract).then_inc(s_u, 1)
                        for n in range(NT // 2):
                            for v, dst, rows in ((0, ust, NA + NKEY + 1), (1, udt, NA + NKEY)):
                                dve.wait_ge(s_ut, 2 * n + v + 1)
                                nc.vector.tensor_copy(
                                    dst[:, n * 256:(n + 1) * 256].rearrange("p (s h) -> p h s", h=2),
                                    ps[0:rows, 6 + v, 0:256].rearrange("p (h s) -> p h s", h=2)).then_inc(s_ute, 1)
                        for j in range(NM):
                            g, e = divmod(j, 4)
                            cols = slice(g * GW, (g + 1) * GW)
                            dve.wait_ge(s_ex, 2 * j + 2)
                            dve.wait_ge(s_pm, j + 1)
                            ins = nc.vector.scalar_tensor_tensor(pexp[:, e, cols], ps[:, 2 * (j % 2) + 1, :],
                                                                 float(TOPK) + 0.5, pex[:, j % 2, :],
                                                                 ALU.is_gt, ALU.mult)
                            if e == 0:
                                link(ins)
                                ins = nc.vector.tensor_tensor(pexp[:, 0, cols], ps[:, 4 + g % 2, :],
                                                              pexp[:, 0, cols], ALU.add)
                            ins.then_inc(s_pe, 1)

                    @block.gpsimd
                    def _(pool):
                        ln_pool(pool, 3)

                    @block.tensor
                    def _(pe):
                        pe.wait_ge(s_in, 48)
                        for g in range(NG):
                            pe.wait_ge(s_ln, g + 1)
                            if g:
                                pe.wait_ge(s_h, g)
                            ln_transposes(g, 0).then_inc(s_lnt, 1)
                            pe.wait_ge(s_h, g + 1)
                            if g >= 2:
                                pe.wait_ge(s_qe, g - 1)
                            for k in range(KC):
                                last = nc.tensor.matmul(ps[:, 2 + g % 2, :], wq[:, k, :],
                                                        h_t[:, k, g * GW:(g + 1) * GW], start=k == 0, stop=k == KC - 1)
                            last.then_inc(s_q, 1)
                        pe.wait_ge(s_qe, NG)
                        for n in range(TB):
                            if n >= 2:
                                pe.wait_ge(s_re, n - 1)
                            for half in range(2):
                                for w in range(2):
                                    r = slice(half * 64, half * 64 + 64)
                                    last = nc.tensor.matmul(
                                        ps[:, 4 - 2 * (n % 2) + half, w * NKEY:(w + 1) * NKEY],
                                        qr[r, w * SEQ + n * P:w * SEQ + (n + 1) * P], keys[r, w, :],
                                        start=True, stop=True)
                            last.then_inc(s_r, 1)
                        pe.wait_ge(s_u, 1)
                        for n in range(NT // 2):
                            for v, (src, rows) in enumerate(((us, NA + NKEY + 1), (ud, NA + NKEY))):
                                if n:
                                    pe.wait_ge(s_ute, 2 * (n - 1) + v + 1)
                                for half in range(2):
                                    last = nc.tensor.transpose(ps[0:rows, 6 + v, half * P:(half + 1) * P],
                                                               src[:, 2 * n + half, :], ident)
                                last.then_inc(s_ut, 1)
                        pe.wait_ge(s_ute, NT)
                        for j in range(NM):
                            g, e = divmod(j, 4)
                            cols = slice(g * GW, (g + 1) * GW)
                            if j >= 2:
                                pe.wait_ge(s_pe, j - 1)
                            if e == 0:
                                nc.tensor.matmul(ps[:, 4 + g % 2, :], consts[0:NA + NKEY + 1, C_SELR:C_SELR + P],
                                                 ust[:, cols], start=True, stop=True)
                            sel = consts[0:NA + NKEY, C_SEL + e * P:C_SEL + (e + 1) * P]
                            nc.tensor.matmul(ps[:, 2 * (j % 2), :], sel, ust[0:NA + NKEY, cols],
                                             start=True, stop=True).then_inc(s_ex, 1)
                            nc.tensor.matmul(ps[:, 2 * (j % 2) + 1, :], sel, udt[:, cols],
                                             start=True, stop=True).then_inc(s_ex, 1)

            ffn("i", 1, PAIRS1, a["mlp"], False, (de, ue, pexp), True)


def constants():
    import numpy as np
    c = np.zeros((P, C_N), np.float32)
    p = np.arange(P)
    c[:, C_ID:C_ID + P] = np.eye(P)
    c[:, C_MS:C_MS + P] = np.where(p[None, :] > p[:, None], MASKED, 0.0)
    c[:, C_MT:C_MT + P] = np.where(p[:, None] > p[None, :], MASKED, 0.0)
    for r in range(3 * TB):
        c[6 * HD + r, C_BLK + r % TB] = 1.0
    c[:, C_IOTA:C_IOTA + NKEY] = np.arange(NKEY)
    c[:, C_RANK:C_RANK + TOPK] = TOPK - np.arange(TOPK)
    for e in range(NEXP):
        i = NEXP - 1 - e
        c[i // NKEY, C_SEL + e] = 1.0
        c[NA + i % NKEY, C_SEL + e] = 1.0
    c[NA + NKEY, C_SELR] = 1.0
    return c


def laid_out(inputs):
    import numpy as np
    x = {k: np.asarray(v) for k, v in inputs.items()}

    def pack(gates, ups, downs):
        n = gates.shape[0] // P
        g = gates.reshape(n, P, KC, P).transpose(0, 3, 2, 1)
        u = ups.reshape(n, P, KC, P).transpose(0, 3, 2, 1)
        gu = np.concatenate([g, u], axis=3).reshape(n, P, KC * 2 * P)
        return np.ascontiguousarray(np.concatenate([gu, downs.reshape(n, P, D)], axis=2).reshape(n * P, 3 * D))

    zero = np.zeros((I0, D), np.float32)
    gu = x["L0_ffn_gu_w"]
    moe = pack(np.concatenate([gu[:, :I0].reshape(-1, D), x["L0_ffn_sh_gate_w"], zero]),
               np.concatenate([gu[:, I0:].reshape(-1, D), x["L0_ffn_sh_up_w"], zero]),
               np.concatenate([x["L0_ffn_dp_w"].transpose(0, 2, 1).reshape(-1, D),
                               x["L0_ffn_sh_down_w"].T, zero]))
    mlp = pack(x["L1_ffn_gate_w"].T, x["L1_ffn_up_w"].T, x["L1_ffn_down_w"])
    gate0 = np.concatenate([x["L0_ffn_gate_w"], x["L0_ffn_sh_gate1_w"], np.zeros((1, D), np.float32)]).T

    def col(v):
        return v.reshape(KC, P).T

    cond = np.stack([x["L0_c"], x["L1_c"]]).transpose(0, 2, 1).reshape(2, KC, P, BATCH).transpose(2, 0, 1, 3)
    out = {
        "x": x["L0_attn_x"], "cond": cond, "consts": constants(), "wmod0": x["L0_wmod"], "wmod1": x["L1_wmod"],
        "wq0": x["L0_attn_Wq"], "wk0": x["L0_attn_Wk"], "wv0": x["L0_attn_Wv"],
        "bq0": col(x["L0_attn_bq"]), "bk0": col(x["L0_attn_bk"]), "bv0": x["L0_attn_bv"],
        "gate0": gate0, "moe": moe, "mlp": mlp,
        "wq1": x["L1_attn_W_query"], "wk1": x["L1_attn_W_key"], "wv1": x["L1_attn_W_value"],
        "wo1": x["L1_attn_W_out"], "bo1": col(x["L1_attn_b_out"]),
        "wq_r": x["L1_ffn_W_q"], "keys": x["L1_ffn_keys"],
        "de_t": x["L1_ffn_down_embed"][::-1].T, "ue": x["L1_ffn_up_embed"][::-1],
    }
    return {k: np.ascontiguousarray(v) for k, v in out.items()}


def kernel(**inputs):
    import concourse.bacc as bacc
    from concourse.bass_utils import run_bass_kernel_spmd

    nc = bacc.Bacc("TRN2", target_bir_lowering=False, num_devices=1)
    arrays = laid_out(inputs)
    aps = {k: nc.dram_tensor(f"in_{k}", v.shape, F32, kind="ExternalInput").ap() for k, v in arrays.items()}
    aps["out"] = nc.dram_tensor("out_x", (BATCH, SEQ, D), F32, kind="ExternalOutput").ap()
    build(nc, aps)
    r = run_bass_kernel_spmd(nc, [{f"in_{k}": v for k, v in arrays.items()}], core_ids=[0])
    return r.results[0]["out_x"]
```

```python
from contextlib import ExitStack

import concourse.bass as bass
from concourse import mybir

F32 = mybir.dt.float32
F32R = mybir.dt.float32r
BF16 = mybir.dt.bfloat16
U32 = mybir.dt.uint32
ALU = mybir.AluOpType
ACT = mybir.ActivationFunctionType
AX = mybir.AxisListType

P = 128
BATCH, SEQ, D = 2, 1024, 256
T = BATCH * SEQ
NT = T // P
TB = SEQ // P
KC = D // P
GW = 512
NG = T // GW
GB = SEQ // GW
EPS = 1e-5
E0, I0, TOPK = 64, 64, 8
PAIRS0 = E0 // 2 + 1
HEADS, HD = 16, 16
INTER = 1024
PAIRS1 = INTER // P
R1, NKEY, NEXP = 128, 64, 512
NA = NEXP // NKEY
SA, CA_, GA, SB_, CB, GB_ = range(6)
MASKED = -1.0e30
REPLACED = -3.0e38
C_ID, C_MS, C_MT, C_BLK, C_IOTA, C_RANK, C_SEL, C_SELR = 0, 128, 256, 384, 392, 456, 464, 976
C_N = 1104


def bc(ap, axis, n):
    v = ap.unsqueeze(axis)
    shape = list(v.shape)
    shape[axis] = n
    return v.to_broadcast(shape)


class Tick:

    def __init__(self, sem):
        self.sem, self.n = sem, 0

    def inc(self, ins):
        ins.then_inc(self.sem, 1)
        self.n += 1

    def dma(self, ins):
        ins.then_inc(self.sem, 16)
        self.n += 16


def build(nc, a):
    ctx = ExitStack()

    held = []

    def sem(name):
        held.append(nc.alloc_semaphore(name=name))
        return held[-1]

    def recycle(since):
        nc.clear_and_free_semaphores(held[since:])
        del held[since:]
        nc.all_engine_barrier()

    def sb(stack, name, shape, dt=F32):
        return stack.enter_context(nc.sbuf_tensor(name, shape, dt))

    with ctx:
        wt_dram = nc.dram_tensor("router_weights_t", (2 * PAIRS0, T), F32, kind="Internal").ap()
        qk_dram = nc.dram_tensor("qk_parts", (2, 3, BATCH * D, SEQ), BF16, kind="Internal").ap()
        ctx_dram = nc.dram_tensor("context_t", (BATCH * D, SEQ), F32, kind="Internal").ap()

        z_dram = nc.dram_tensor("prob_sums", (BATCH * HEADS, SEQ), F32, kind="Internal").ap()
        rz_dram = nc.dram_tensor("inverse_sums", (BATCH * HEADS, SEQ), F32, kind="Internal").ap()

        ps = ctx.enter_context(nc.psum_tensor("ps", [P, 8, GW], F32))
        consts = sb(ctx, "consts", [P, C_N])
        cbf = sb(ctx, "cbf", [P, 384], BF16)
        x_tok = sb(ctx, "x_tok", [P, NT, D])
        h_t = sb(ctx, "h_t", [P, KC, T])
        h_hi = sb(ctx, "h_hi", [P, KC, T], F32R)
        h_lo = sb(ctx, "h_lo", [P, KC, T], F32R)
        xn = sb(ctx, "xn", [P, NT, D])
        stats = sb(ctx, "stats", [P, NT, 6])
        mv = sb(ctx, "mv", [P, NT, 2])
        rstd = sb(ctx, "rstd", [P, NT])
        veps = sb(ctx, "veps", [P, NT])
        half = sb(ctx, "minus_half", [P, NT])
        cond = sb(ctx, "cond", [P, 2, KC, BATCH])
        csilu = sb(ctx, "csilu", [P, 2, KC, BATCH])
        modc = sb(ctx, "modc", [P, 2, 12, BATCH])
        gtmp = sb(ctx, "gtmp", [P, 2, 2, 2, KC, BATCH])
        ident = consts[:, C_ID:C_ID + P]
        ident_b = cbf[:, 0:P]
        mask_s = cbf[:, P:2 * P]
        mask_t = cbf[:, 2 * P:3 * P]
        phase = [0]

        def mod_col(layer, which, c, b):
            return modc[:, layer, which * KC + c, b:b + 1]

        s_var, s_rstd, s_half = sem("ln_var"), sem("ln_rstd"), sem("ln_half")

        def ln_pool(pool, ln, groups=range(NG)):
            for g in groups:
                pool.wait_ge(s_var, ln * NG + g + 1)
                nc.gpsimd.tensor_tensor(rstd[:, 4 * g:4 * g + 4], veps[:, 4 * g:4 * g + 4], half[:, 4 * g:4 * g + 4],
                                        ALU.pow).then_inc(s_rstd, 1)

        def ln_dve(dve, g, link, ready, ln):
            for t in range(4 * g, 4 * g + 4):
                last = nc.vector.bn_stats(stats[:, t, :], x_tok[:, t, :])
            link(last)
            for t in range(4 * g, 4 * g + 4):
                last = nc.vector.bn_aggr(mv[:, t, :], stats[:, t, :])
            link(last)
            nc.vector.tensor_scalar(veps[:, 4 * g:4 * g + 4], mv[:, 4 * g:4 * g + 4, 1], EPS, None,
                                    ALU.add).then_inc(s_var, 1)
            dve.wait_ge(s_rstd, ln * NG + g + 1)
            for t in range(4 * g, 4 * g + 4):
                last = nc.vector.tensor_scalar(xn[:, t, :], x_tok[:, t, :], mv[:, t, 0:1], rstd[:, t:t + 1],
                                               ALU.subtract, ALU.mult)
            last.then_inc(ready, 1)

        def ln_transposes(g, bank):
            for c in range(KC):
                for j in range(4):
                    last = nc.tensor.transpose(ps[:, bank + c, j * P:(j + 1) * P],
                                               xn[:, 4 * g + j, c * P:(c + 1) * P], ident)
            return last

        def ln_modulate(layer, shift, scale, g, bank):
            for c in range(KC):
                last = nc.scalar.activation(h_t[:, c, g * GW:(g + 1) * GW], ps[:, bank + c, :], ACT.Identity,
                                            bias=mod_col(layer, shift, c, g // GB),
                                            scale=mod_col(layer, scale, c, g // GB))
            return last

        s_hhi, s_hlo = sem("split_h_hi"), sem("split_h_lo")

        def split_h(pool, g, s_h, nth):
            cols = slice(g * GW, (g + 1) * GW)
            pool.wait_ge(s_h, g + 1)
            nc.gpsimd.tensor_copy(h_hi[:, :, cols], h_t[:, :, cols]).then_inc(s_hhi, 1)
            pool.wait_ge(s_hhi, nth * NG + g + 1)
            nc.gpsimd.tensor_tensor(h_lo[:, :, cols], h_t[:, :, cols], h_hi[:, :, cols].bitcast(F32),
                                    ALU.subtract).then_inc(s_hlo, 1)

        def chain(name, engine):
            tick = Tick(sem(name))

            def link(ins):
                tick.inc(ins)
                engine.wait_ge(tick.sem, tick.n)
            return link

        def mod_columns(layer, wmod):
            for j in range(12):
                for k in range(KC):
                    last = nc.tensor.matmul(ps[:, 0, 2 * j:2 * j + 2], wmod[:, k, j * P:(j + 1) * P],
                                            csilu[:, layer, k, :], start=k == 0, stop=k == KC - 1)
            return last

        def guard(g, tmp, link):
            link(nc.vector.tensor_scalar(tmp[0], g, 0.0, 2.0, ALU.is_ge, ALU.mult))
            link(nc.vector.scalar_tensor_tensor(tmp[1], g, -1.0, g, ALU.mult, ALU.max))
            link(nc.vector.tensor_scalar(tmp[1], tmp[1], 0.25, None, ALU.max))
            link(nc.vector.scalar_tensor_tensor(g, tmp[0], -1.0, tmp[1], ALU.add, ALU.mult))

        def mod_finish(layer, link):
            m = modc[:, layer, :, :]
            link(nc.vector.tensor_copy(m, ps[:, 0, 0:24].rearrange("p (j b) -> p j b", b=BATCH)))
            for n, which in enumerate((GA, GB_)):
                guard(m[:, which * KC:(which + 1) * KC, :],
                      (gtmp[:, layer, n, 0], gtmp[:, layer, n, 1]), link)
            for which in (CA_, CB):
                part = m[:, which * KC:(which + 1) * KC, :]
                last = nc.vector.tensor_scalar(part, part, 1.0, None, ALU.add)
            return last

        kept = len(held)

        with ExitStack() as st:
            wqkv = sb(st, "wqkv", [P, 3, KC, D])
            bqk = sb(st, "bqk", [P, 2, KC])
            bv = sb(st, "bv", [P, D])
            wmod = sb(st, "wmod0", [P, KC, 6 * D])
            crep = sb(st, "crep", [P, BATCH, KC, P])
            ga = sb(st, "ga_rows", [P, BATCH, D])
            gat = sb(st, "ga_tmp", [P, 2, BATCH, D])
            qt = sb(st, "q_t", [P, KC, T])
            kt = sb(st, "k_t", [P, KC, T])
            vtok = sb(st, "v_tok", [P, NT, D])
            probs = sb(st, "probs", [P, 2, SEQ])
            probs_t = sb(st, "probs_t", [P, 2, SEQ])
            mx = sb(st, "mx", [P, NT])
            nmx = sb(st, "nmx", [P, NT])
            zs = sb(st, "zs", [P, NT])
            rz = sb(st, "rz", [P, NT])
            att = sb(st, "att", [P, 2, D])
            att2 = sb(st, "att2", [P, 2, D])
            s_const, s_cond, s_wmod, s_wqkv, s_bias = [sem(n) for n in
                ("a_const", "a_cond", "a_wmod", "a_wqkv", "a_bias")]
            s_x = [sem(f"a_x{g}") for g in range(NG)]
            s_csilu, s_crep, s_modp, s_modd, s_ln, s_lnt, s_h = [sem(n) for n in
                ("a_csilu", "a_crep", "a_modp", "a_modd", "a_ln", "a_lnt", "a_h")]
            s_proj, s_pev_a, s_pev_d, s_cb = [sem(n) for n in ("a_proj", "a_pev_act", "a_pev_dve", "a_cb")]
            with nc.Block() as block:
                @block.sync
                def _(sp):
                    sp.dma_start(cond[:, :, :, :], a["cond"]).then_inc(s_cond, 16)
                    sp.dma_start(wmod[:, :, :], a["wmod0"].rearrange("(k p) n -> p k n", p=P)).then_inc(s_wmod, 16)
                    for g in range(NG):
                        sp.dma_start(x_tok[:, 4 * g:4 * g + 4, :],
                                     a["x"].rearrange("b (t p) d -> p (b t) d", p=P)[:, 4 * g:4 * g + 4, :])\
                            .then_inc(s_x[g], 16)
                        if g == 0:
                            sp.dma_start(consts[:, :], a["consts"]).then_inc(s_const, 16)
                            for n, w in enumerate(("wq0", "wk0", "wv0")):
                                sp.dma_start(wqkv[:, n], a[w].rearrange("(k p) n -> p k n", p=P))\
                                    .then_inc(s_wqkv, 16)
                            sp.dma_start(bqk[:, 0, :], a["bq0"]).then_inc(s_bias, 16)
                            sp.dma_start(bqk[:, 1, :], a["bk0"]).then_inc(s_bias, 16)
                            sp.dma_start(bv[:, :], a["bv0"].unsqueeze(0).to_broadcast([P, D])).then_inc(s_bias, 16)

                @block.scalar
                def _(act):
                    act.wait_ge(s_cond, 16)
                    nc.scalar.activation(csilu[:, :, :, :], cond[:, :, :, :], ACT.Silu).then_inc(s_csilu, 1)
                    act.wait_ge(s_modd, 1)
                    act.wait_ge(s_bias, 48)
                    for g in range(NG):
                        act.wait_ge(s_lnt, g + 1)
                        ln_modulate(0, SA, CA_, g, 0).then_inc(s_h, 1)
                        for m in range(KC):
                            act.wait_ge(s_proj, 6 * g + m + 1)
                            nc.scalar.activation(qt[:, m, g * GW:(g + 1) * GW], ps[:, 2 + m, :], ACT.Identity,
                                                 bias=bqk[:, 0, m:m + 1]).then_inc(s_pev_a, 1)

                @block.vector
                def _(dve):
                    link = chain("a_dve", dve)
                    dve.wait_ge(s_csilu, 1)
                    for b in range(BATCH):
                        last = nc.vector.tensor_copy(crep[:, b], bc(csilu[:, 0, :, b], 2, P))
                    last.then_inc(s_crep, 1)
                    dve.wait_ge(s_const, 16)
                    nc.vector.tensor_copy(cbf[:, :], consts[:, 0:384]).then_inc(s_cb, 1)
                    dve.wait_ge(s_x[0], 16)
                    ln_dve(dve, 0, link, s_ln, 0)
                    dve.wait_ge(s_modp, 1)
                    link(nc.vector.tensor_copy(ga[:, :, :], ps[:, 1, :].rearrange("p (b d) -> p b d", b=BATCH)))
                    guard(ga[:, :, :], (gat[:, 0], gat[:, 1]), link)
                    mod_finish(0, link).then_inc(s_modd, 1)
                    dve.wait_ge(s_bias, 48)
                    for g in range(NG):
                        if g + 1 < NG:
                            dve.wait_ge(s_x[g + 1], 16)
                            ln_dve(dve, g + 1, link, s_ln, 0)
                        for m in range(KC):
                            dve.wait_ge(s_proj, 6 * g + 2 + m + 1)
                            nc.vector.tensor_scalar(kt[:, m, g * GW:(g + 1) * GW], ps[:, 4 + m, :],
                                                    bqk[:, 1, m:m + 1], None, ALU.add).then_inc(s_pev_d, 1)
                        for m in range(2):
                            dve.wait_ge(s_proj, 6 * g + 4 + m + 1)
                            nc.vector.tensor_copy(vtok[:, 4 * g + 2 * m:4 * g + 2 * m + 2, :],
                                                  ps[:, 6 + m, :].rearrange("p (t d) -> p t d", t=2))\
                                .then_inc(s_pev_d, 1)

                @block.gpsimd
                def _(pool):
                    nc.gpsimd.memset(half[:, :], -0.5).then_inc(s_half, 1)
                    pool.wait_ge(s_half, 1)
                    ln_pool(pool, 0)

                @block.tensor
                def _(pe):
                    pe.wait_ge(s_csilu, 1)
                    pe.wait_ge(s_wmod, 16)
                    mod_columns(0, wmod)
                    pe.wait_ge(s_crep, 1)
                    for b in range(BATCH):
                        for k in range(KC):
                            last = nc.tensor.matmul(ps[:, 1, b * D:(b + 1) * D], crep[:, b, k, :],
                                                    wmod[:, k, GA * D:(GA + 1) * D], start=k == 0, stop=k == KC - 1)
                    last.then_inc(s_modp, 1)
                    pe.wait_ge(s_modd, 1)
                    pe.wait_ge(s_const, 16)
                    pe.wait_ge(s_wqkv, 48)
                    for g in range(NG):
                        pe.wait_ge(s_ln, g + 1)
                        if g:
                            pe.wait_ge(s_h, g)
                        ln_transposes(g, 0).then_inc(s_lnt, 1)
                        pe.wait_ge(s_h, g + 1)
                        for w in range(2):
                            for m in range(KC):
                                if g:
                                    pe.wait_ge(s_pev_a if w == 0 else s_pev_d,
                                               2 * (g - 1) + m + 1 if w == 0 else 4 * (g - 1) + m + 1)
                                for k in range(KC):
                                    last = nc.tensor.matmul(ps[:, 2 + 2 * w + m, :],
                                                            wqkv[:, w, k, m * P:(m + 1) * P],
                                                            h_t[:, k, g * GW:(g + 1) * GW],
                                                            start=k == 0, stop=k == KC - 1)
                                last.then_inc(s_proj, 1)
                        for m in range(2):
                            if g:
                                pe.wait_ge(s_pev_d, 4 * (g - 1) + 2 + m + 1)
                            for i in range(2):
                                t = 4 * g + 2 * m + i
                                for k in range(KC):
                                    last = nc.tensor.matmul(ps[:, 6 + m, i * D:(i + 1) * D],
                                                            h_t[:, k, t * P:(t + 1) * P], wqkv[:, 2, k, :],
                                                            start=k == 0, stop=k == KC - 1)
                            last.then_inc(s_proj, 1)

            s_sc, s_mx, s_exp, s_pt, s_ptd, s_pta, s_av, s_out = [sem(n) for n in
                ("b_scores", "b_max", "b_exp", "b_pt", "b_pt_dve", "b_pt_act", "b_av", "b_out")]
            hi_blocks = [t for t in range(NT) if t % TB >= 4]
            with nc.Block() as block:
                @block.tensor
                def _(pe):
                    def scores(t):
                        b, i = divmod(t, TB)
                        n = (i + 1) * P
                        if t >= 2:
                            pe.wait_ge(s_exp, t - 1)
                        for lo in range(0, n, GW):
                            w = min(GW, n - lo)
                            out = ps[:, 2 * (t % 2) + lo // GW, 0:w]
                            diag = lo + w == n
                            for k in range(KC):
                                last = nc.tensor.matmul(out, qt[:, k, t * P:(t + 1) * P],
                                                        kt[:, k, b * SEQ + lo:b * SEQ + lo + w],
                                                        start=k == 0, stop=k == KC - 1 and not diag)
                            if diag:
                                last = nc.tensor.matmul(out[:, w - P:w], ident_b, mask_s, start=False, stop=True)
                        last.then_inc(s_sc, 1)

                    scores(0)
                    for t in range(NT):
                        b, i = divmod(t, TB)
                        if t + 1 < NT:
                            scores(t + 1)
                        pe.wait_ge(s_exp, t + 1)
                        for j in range(i + 1):
                            if j == 0 and t:
                                pe.wait_ge(s_ptd, t)
                            if j == 4:
                                last.then_inc(s_pt, 1)
                                done = len([u for u in hi_blocks if u < t])
                                if done:
                                    pe.wait_ge(s_pta, done)
                            last = nc.tensor.transpose(ps[:, 4 + j // 4, (j % 4) * P:(j % 4 + 1) * P],
                                                       probs[:, t % 2, j * P:(j + 1) * P], ident)
                        last.then_inc(s_pt, 1)
                        if t >= 2:
                            pe.wait_ge(s_out, t - 1)
                        for j in range(i + 1):
                            if j == 0:
                                pe.wait_ge(s_ptd, t + 1)
                            if j == 4:
                                pe.wait_ge(s_pta, len([u for u in hi_blocks if u <= t]))
                            last = nc.tensor.matmul(ps[:, 6 + t % 2, 0:D], probs_t[:, t % 2, j * P:(j + 1) * P],
                                                    vtok[:, b * TB + j, :], start=j == 0, stop=j == i)
                        last.then_inc(s_av, 1)

                def pt_count(t):
                    return t + len([u for u in hi_blocks if u < t]) + 1

                @block.scalar
                def _(act):
                    for t in range(NT + 1):
                        if t < NT:
                            n = (t % TB + 1) * P
                            act.wait_ge(s_mx, t + 1)
                            nc.scalar.activation(probs[:, t % 2, 0:n],
                                                 ps[:, 2 * (t % 2):2 * (t % 2) + 2, :].rearrange("p a n -> p (a n)")[:, 0:n],
                                                 ACT.Exp, bias=nmx[:, t:t + 1], scale=D ** -0.5,
                                                 accum_out=zs[:, t:t + 1]).then_inc(s_exp, 1)
                        u = t - 1
                        if u in hi_blocks:
                            act.wait_ge(s_pt, pt_count(u) + 1)
                            n = (u % TB + 1) * P
                            nc.scalar.copy(probs_t[:, u % 2, GW:n], ps[:, 5, 0:n - GW]).then_inc(s_pta, 1)

                @block.vector
                def _(dve):
                    link = chain("b_dve", dve)
                    for t in range(NT + 1):
                        if t < NT:
                            n = (t % TB + 1) * P
                            dve.wait_ge(s_sc, t + 1)
                            link(nc.vector.reduce_max(
                                mx[:, t:t + 1],
                                ps[:, 2 * (t % 2):2 * (t % 2) + 2, :].rearrange("p a n -> p (a n)")[:, 0:n], AX.X))
                            nc.vector.tensor_scalar(nmx[:, t:t + 1], mx[:, t:t + 1], -(D ** -0.5), None,
                                                    ALU.mult).then_inc(s_mx, 1)
                        if t >= 1:
                            u = t - 1
                            b = u // TB
                            n = min(u % TB + 1, 4) * P
                            dve.wait_ge(s_pt, pt_count(u))
                            nc.vector.tensor_copy(probs_t[:, u % 2, 0:n], ps[:, 4, 0:n]).then_inc(s_ptd, 1)
                            link(nc.vector.reciprocal(rz[:, u:u + 1], zs[:, u:u + 1]))
                            dve.wait_ge(s_av, u + 1)
                            ins = nc.vector.scalar_tensor_tensor(att[:, u % 2, :], ps[:, 6 + u % 2, 0:D],
                                                                 rz[:, u:u + 1], bv[:, :], ALU.mult, ALU.add)
                            link(ins)
                            link(nc.vector.tensor_tensor(att2[:, u % 2, :], att[:, u % 2, :], ga[:, b, :], ALU.mult))
                            nc.vector.tensor_tensor(x_tok[:, u, :], x_tok[:, u, :], att2[:, u % 2, :],
                                                    ALU.add).then_inc(s_out, 1)

        with ExitStack() as st:
            gw = sb(st, "gate_w_t", [P, KC, E0 + 2])
            lg = sb(st, "logits", [P, NT, E0 + 2])
            lrep = sb(st, "lrep", [P, NT, E0])
            top = sb(st, "top", [P, NT, TOPK])
            ntop = sb(st, "ntop", [P, NT])
            ex = sb(st, "ex", [P, NT, E0])
            sel = sb(st, "sel", [P, NT, E0])
            wts = sb(st, "wts", [P, NT, E0 + 2])
            zsum = sb(st, "zsum", [P, NT])
            esg = sb(st, "esg", [P, NT])
            wt = sb(st, "w_t", [E0 + 2, T])
            s_gw, s_ln, s_lnt, s_h, s_lg, s_lgc, s_lev, s_exd, s_w, s_wtp, s_wte, s_wst = [sem(n) for n in
                ("c_gw", "c_ln", "c_lnt", "c_h", "c_lg", "c_lgc", "c_lev", "c_exd", "c_w", "c_wtp", "c_wte", "c_wst")]
            with nc.Block() as block:
                @block.sync
                def _(sp):
                    sp.dma_start(gw[:, :, :], a["gate0"].rearrange("(k p) e -> p k e", p=P)).then_inc(s_gw, 16)
                    sp.wait_ge(s_wte, NG)
                    sp.dma_start(wt_dram, wt[:, :]).then_inc(s_wst, 16)
                    sp.wait_ge(s_wst, 16)

                @block.scalar
                def _(act):
                    for g in range(NG):
                        act.wait_ge(s_lnt, g + 1)
                        ln_modulate(0, SB_, CB, g, 2 * (g % 2)).then_inc(s_h, 1)
                        act.wait_ge(s_lg, g + 1)
                        nc.scalar.copy(lg[:, 4 * g:4 * g + 4, :],
                                       ps[:, 4 + g % 2, 0:4 * (E0 + 2)].rearrange("p (t e) -> p t e", t=4))\
                            .then_inc(s_lgc, 1)
                    for t in range(NT):
                        act.wait_ge(s_lev, 1)
                        last = nc.scalar.activation(ex[:, t, :], lg[:, t, 0:E0], ACT.Exp, bias=ntop[:, t:t + 1])
                    nc.scalar.activation(esg[:, :], lg[:, :, E0], ACT.Exp, scale=-1.0).then_inc(s_exd, 1)

                @block.vector
                def _(dve):
                    link = chain("c_dve", dve)
                    for g in range(NG):
                        ln_dve(dve, g, link, s_ln, 1)
                    for g in range(NG):
                        dve.wait_ge(s_lgc, g + 1)
                        for t in range(4 * g, 4 * g + 4):
                            last = nc.vector.max(top[:, t, :], lg[:, t, 0:E0])
                        link(last)
                        for t in range(4 * g, 4 * g + 4):
                            last = nc.vector.match_replace(lrep[:, t, :], top[:, t, :], lg[:, t, 0:E0], REPLACED)
                    link(last)
                    nc.vector.tensor_scalar(ntop[:, :], top[:, :, 0], -1.0, None, ALU.mult).then_inc(s_lev, 1)
                    link(nc.vector.tensor_tensor(sel[:, :, :], lrep[:, :, :], lg[:, :, 0:E0], ALU.not_equal))
                    dve.wait_ge(s_exd, 1)
                    link(nc.vector.tensor_tensor(ex[:, :, :], ex[:, :, :], sel[:, :, :], ALU.mult))
                    link(nc.vector.tensor_reduce(zsum[:, :], ex[:, :, :], AX.X, ALU.add))
                    link(nc.vector.reciprocal(zsum[:, :], zsum[:, :]))
                    nc.vector.memset(wts[:, :, E0 + 1:E0 + 2], 0.0)
                    link(nc.vector.tensor_scalar(esg[:, :], esg[:, :], 1.0, None, ALU.add))
                    nc.vector.reciprocal(wts[:, :, E0], esg[:, :])
                    nc.vector.tensor_tensor(wts[:, :, 0:E0], ex[:, :, :], bc(zsum[:, :], 2, E0),
                                            ALU.mult).then_inc(s_w, 1)
                    for g in range(NG):
                        dve.wait_ge(s_wtp, g + 1)
                        nc.vector.tensor_copy(wt[:, g * GW:(g + 1) * GW], ps[0:E0 + 2, 6 + g % 2, :]).then_inc(s_wte, 1)

                @block.gpsimd
                def _(pool):
                    ln_pool(pool, 1, range(2))
                    for g in range(NG):
                        if g + 2 < NG:
                            ln_pool(pool, 1, (g + 2,))
                        split_h(pool, g, s_h, 0)

                @block.tensor
                def _(pe):
                    pe.wait_ge(s_gw, 16)
                    for g in range(NG):
                        pe.wait_ge(s_ln, g + 1)
                        if g >= 2:
                            pe.wait_ge(s_h, g - 1)
                        ln_transposes(g, 2 * (g % 2)).then_inc(s_lnt, 1)
                        pe.wait_ge(s_h, g + 1)
                        if g >= 2:
                            pe.wait_ge(s_lgc, g - 1)
                        for i in range(4):
                            t = 4 * g + i
                            for k in range(KC):
                                last = nc.tensor.matmul(ps[:, 4 + g % 2, i * (E0 + 2):(i + 1) * (E0 + 2)],
                                                        h_t[:, k, t * P:(t + 1) * P], gw[:, k, :],
                                                        start=k == 0, stop=k == KC - 1)
                        last.then_inc(s_lg, 1)
                    pe.wait_ge(s_w, 1)
                    for g in range(NG):
                        if g >= 2:
                            pe.wait_ge(s_wte, g - 1)
                        for i in range(4):
                            last = nc.tensor.transpose(ps[0:E0 + 2, 6 + g % 2, i * P:(i + 1) * P],
                                                       wts[:, 4 * g + i, :], ident)
                        last.then_inc(s_wtp, 1)

        def ffn(tag, layer, pairs, w_ap, weighted, side=None):
            with ExitStack() as st:
                S = lambda n: sem(f"{tag}_{n}")
                units = 2 * pairs
                W = 3 * D
                raw = sb(st, f"{tag}_raw", [P, 3, W])
                w_hi = sb(st, f"{tag}_w_hi", [P, 3, W], F32R)
                w_lo = sb(st, f"{tag}_w_lo", [P, 3, W], F32R)
                wbc = sb(st, f"{tag}_wbc", [P, 3, SEQ]) if weighted else None
                sg = sb(st, f"{tag}_silu", [P, 3, GW])
                prod = sb(st, f"{tag}_prod", [P, 3, GW])
                inter = sb(st, f"{tag}_inter", [P, 3, GW]) if weighted else prod
                i_hi = sb(st, f"{tag}_i_hi", [P, 3, GW], F32R)
                i_lo = sb(st, f"{tag}_i_lo", [P, 3, GW], F32R)
                out_t = sb(st, f"{tag}_out", [P, KC, SEQ])
                raw_in = [S(f"raw{i}") for i in range(3)]
                wb_in = [S(f"wb{i}") for i in range(3)]
                s_whi, s_wlo, s_gu, s_silu, s_t, s_int, s_ihi, s_ilo, s_dn, s_acc, s_tr, s_add = [S(n) for n in
                    ("whi", "wlo", "gu", "silu", "t", "int", "ihi", "ilo", "dn", "acc", "tr", "add")]
                if not weighted:
                    s_int = s_t
                n_slot = [(pairs + 2 - i) // 3 for i in range(3)]
                HEAD = 4
                loops = (units - HEAD - 2) // 6

                def later(b, u, n):
                    return not isinstance(u, int) or b > 0 or u >= n

                def freed(b, u):
                    return b * units if isinstance(u, int) and u < 3 else u + (b * units - 2)

                def pairs_before(b, q):
                    return (b - 1) * pairs + 3 * (n_slot[q] - 1) + q + 1

                with nc.Block() as block:
                    @block.sync
                    def _(sp):
                        def load(b, q, slot):
                            fixed = isinstance(q, int)
                            first, rows_at = (q * P, q * 2) if fixed else (sp.snap(q * P), sp.snap(q * 2))
                            if not fixed or b or q >= 3:
                                sp.wait_ge(s_wlo, pairs_before(b, q) if fixed and q < 3 else
                                           q + (b * pairs - 2))
                            sp.dma_start(raw[:, slot, :], w_ap[bass.ds(first, P), :]).then_inc(raw_in[slot], 16)
                            if weighted:
                                if not fixed or b or q >= 3:
                                    used = q * 2 + (b * units - 4)
                                    if fixed and b and q < 3:
                                        used = b * units
                                    sp.wait_ge(s_int, used)
                                rows = wt_dram[bass.ds(rows_at, 2), b * SEQ:(b + 1) * SEQ]
                                sp.dma_start(wbc[:, slot, :], bc(rows, 1, P // 2)).then_inc(wb_in[slot], 16)

                        for b in range(BATCH):
                            for q in range(3):
                                load(b, q, q)
                            with sp.Fori(0, (pairs - 3) // 3) as it:
                                for q in range(3):
                                    load(b, it * 3 + (3 + q), q)
                            for q in range(3 + 3 * ((pairs - 3) // 3), pairs):
                                load(b, q, q % 3)

                    @block.tensor
                    def _(pe):
                        def gate_up(b, u, s):
                            slot, g = s // 2, s % 2
                            cols = slice(b * SEQ + g * GW, b * SEQ + (g + 1) * GW)
                            if g == 0:
                                pe.wait_ge(s_wlo, b * pairs + u // 2 + 1 if isinstance(u, int) else pair_of(u, b))
                            if later(b, u, 2):
                                pe.wait_ge(s_t, u + (b * units - 1))
                            for m in range(2):
                                for n, (w, h) in enumerate(((w_hi, h_hi), (w_hi, h_lo), (w_lo, h_hi))):
                                    for k in range(KC):
                                        last = nc.tensor.matmul(ps[:, 2 * g + m, :],
                                                                w[:, slot, k * D + m * P:k * D + (m + 1) * P],
                                                                h[:, k, cols], start=n == 0 and k == 0,
                                                                stop=n == 2 and k == KC - 1)
                            last.then_inc(s_gu, 1)

                        def down(b, u, s):
                            slot, g = s // 2, s % 2
                            fixed = isinstance(u, int)
                            pe.wait_ge(s_ilo, u + (b * units + 1))
                            for c in range(KC):
                                for n, (w, i) in enumerate(((w_hi, i_hi), (w_hi, i_lo), (w_lo, i_hi))):
                                    last = nc.tensor.matmul(ps[:, 4 + 2 * c + g, :],
                                                            w[:, slot, 2 * D + c * P:2 * D + (c + 1) * P],
                                                            i[:, s % 3, :], start=fixed and u < 2 and n == 0,
                                                            stop=fixed and u >= units - 2 and n == 2)
                            last.then_inc(s_dn, 1)

                        pair = {}

                        def pair_of(u, b):
                            return pair["it"] * 3 + (b * pairs + pair["s"] // 2 + 1)

                        def flush(b):
                            pe.wait_ge(s_acc, 4 * b + 4)
                            for t in range(TB):
                                if t >= 4:
                                    pe.wait_ge(s_add, b * TB + t - 3)
                                for c in range(KC):
                                    last = nc.tensor.transpose(ps[:, 4 + t % 4, c * P:(c + 1) * P],
                                                               out_t[:, c, t * P:(t + 1) * P], ident)
                                last.then_inc(s_tr, 1)

                        for b in range(BATCH):
                            gate_up(b, 0, 0)
                            gate_up(b, 1, 1)
                            if b:
                                flush(b - 1)
                                pe.wait_ge(s_add, b * TB)
                            for u in range(2, HEAD):
                                gate_up(b, u, u)
                                down(b, u - 2, u - 2)
                            with pe.Fori(0, loops) as it:
                                pair["it"] = it
                                for s in range(HEAD, HEAD + 6):
                                    pair["s"] = s
                                    gate_up(b, it * 6 + s, s % 6)
                                    down(b, it * 6 + (s - 2), (s - 2) % 6)
                            for u in range(HEAD + 6 * loops, units):
                                gate_up(b, u, u % 6)
                                down(b, u - 2, (u - 2) % 6)
                            for u in range(units - 2, units):
                                down(b, u, u % 6)
                        flush(BATCH - 1)

                    @block.scalar
                    def _(act):
                        def weights_hi(b, q, slot, loads, before):
                            act.wait_ge(raw_in[slot], loads)
                            if before is not None:
                                act.wait_ge(s_dn, before)
                            nc.scalar.copy(w_hi[:, slot, :], raw[:, slot, :]).then_inc(s_whi, 1)

                        def inter_hi(b, u, s):
                            act.wait_ge(s_int, u + (b * units + 1))
                            if later(b, u, 3):
                                act.wait_ge(s_dn, freed(b, u))
                            nc.scalar.copy(i_hi[:, s % 3, :], inter[:, s % 3, :]).then_inc(s_ihi, 1)

                        def step(b, u, s):
                            if s % 2 == 0:
                                slot = (s // 2 + 1) % 3
                                if isinstance(u, int):
                                    q = u // 2 + 1
                                    if q < pairs:
                                        weights_hi(b, q, slot, 16 * (b * n_slot[slot] + q // 3 + 1),
                                                   b * units + u - 2 if q >= 3 else
                                                   2 * pairs_before(b, q) if b else None)
                                else:
                                    first = loop_s[0] // 2 + 1
                                    weights_hi(b, None, slot, loop_it[0] * 16 + 16 * (b * n_slot[slot] + first // 3 + 1),
                                               u + (b * units - 2))
                            act.wait_ge(s_gu, u + (b * units + 1))
                            if later(b, u, 3):
                                act.wait_ge(s_t, freed(b, u))
                            nc.scalar.activation(sg[:, s % 3, :], ps[:, 2 * (s % 2), :], ACT.Silu).then_inc(s_silu, 1)
                            if not isinstance(u, int) or u >= 1:
                                inter_hi(b, u + (-1), (s - 1) % 6)

                        loop_it, loop_s = [None], [None]

                        def evacuate(b):
                            act.wait_ge(s_dn, (b + 1) * units)
                            for c in range(KC):
                                for g in range(GB):
                                    nc.scalar.activation(out_t[:, c, g * GW:(g + 1) * GW], ps[:, 4 + 2 * c + g, :],
                                                         ACT.Identity, scale=mod_col(layer, GB_, c, b))\
                                        .then_inc(s_acc, 1)

                        for b in range(BATCH):
                            weights_hi(b, 0, 0, 16 * (b * n_slot[0] + 1), 2 * pairs_before(b, 0) if b else None)
                            if b:
                                evacuate(b - 1)
                            for u in range(HEAD):
                                step(b, u, u)
                            with act.Fori(0, loops) as it:
                                loop_it[0] = it
                                for s in range(HEAD, HEAD + 6):
                                    loop_s[0] = s
                                    step(b, it * 6 + s, s % 6)
                            for u in range(HEAD + 6 * loops, units):
                                step(b, u, u % 6)
                            inter_hi(b, units - 1, (units - 1) % 6)
                        evacuate(BATCH - 1)

                    @block.vector
                    def _(dve):
                        def inter_lo(b, u, s):
                            dve.wait_ge(s_ihi, u + (b * units + 1))
                            nc.vector.tensor_tensor(i_lo[:, s % 3, :], inter[:, s % 3, :],
                                                    i_hi[:, s % 3, :].bitcast(F32), ALU.subtract).then_inc(s_ilo, 1)

                        def step(b, u, s):
                            dve.wait_ge(s_silu, u + (b * units + 1))
                            if later(b, u, 3):
                                dve.wait_ge(s_int if weighted else s_ilo, freed(b, u))
                            nc.vector.tensor_tensor(prod[:, s % 3, :], sg[:, s % 3, :], ps[:, 2 * (s % 2) + 1, :],
                                                    ALU.mult).then_inc(s_t, 1)
                            if not isinstance(u, int) or u >= 1:
                                inter_lo(b, u + (-1), (s - 1) % 6)

                        def add_back(b):
                            for t in range(TB):
                                dve.wait_ge(s_tr, b * TB + t + 1)
                                nc.vector.tensor_tensor(x_tok[:, b * TB + t, :], ps[:, 4 + t % 4, 0:D],
                                                        x_tok[:, b * TB + t, :], ALU.add).then_inc(s_add, 1)

                        for b in range(BATCH):
                            for u in range(HEAD):
                                step(b, u, u)
                                if b and u == 1:
                                    add_back(b - 1)
                            with dve.Fori(0, loops) as it:
                                for s in range(HEAD, HEAD + 6):
                                    step(b, it * 6 + s, s % 6)
                            for u in range(HEAD + 6 * loops, units):
                                step(b, u, u % 6)
                            inter_lo(b, units - 1, (units - 1) % 6)
                        add_back(BATCH - 1)

                    @block.gpsimd
                    def _(pool):
                        def weights_lo(count, slot):
                            pool.wait_ge(s_whi, count)
                            nc.gpsimd.tensor_tensor(w_lo[:, slot, :], raw[:, slot, :], w_hi[:, slot, :].bitcast(F32),
                                                    ALU.subtract).then_inc(s_wlo, 1)

                        def weigh(b, u, s, loads):
                            if s % 2 == 0:
                                pool.wait_ge(wb_in[s // 2], loads)
                            pool.wait_ge(s_t, u + (b * units + 1))
                            if later(b, u, 3):
                                pool.wait_ge(s_ilo, freed(b, u))
                            nc.gpsimd.tensor_tensor(inter[:, s % 3, :], prod[:, s % 3, :],
                                                    wbc[:, s // 2, (s % 2) * GW:(s % 2 + 1) * GW],
                                                    ALU.mult).then_inc(s_int, 1)

                        def straight(b, u):
                            if u % 2 == 0 and u // 2 + 1 < pairs:
                                weights_lo(b * pairs + u // 2 + 2, (u // 2 + 1) % 3)
                            if weighted:
                                weigh(b, u, u % 6, 16 * (b * n_slot[(u // 2) % 3] + u // 6 + 1))

                        for b in range(BATCH):
                            weights_lo(b * pairs + 1, 0)
                            for u in range(HEAD):
                                straight(b, u)
                            with pool.Fori(0, loops) as it:
                                for s in range(HEAD, HEAD + 6):
                                    if s % 2 == 0:
                                        weights_lo(it * 3 + (b * pairs + s // 2 + 2), (s // 2 + 1) % 3)
                                    if weighted:
                                        weigh(b, it * 6 + s, s % 6, it * 16 + 16 * (b * n_slot[(s // 2) % 3] + s // 6 + 1))
                            for u in range(HEAD + 6 * loops, units):
                                straight(b, u)

        ffn("d", 0, PAIRS0, a["moe"], True)

        recycle(kept)

        with ExitStack() as vst_:
          vu = sb(vst_, "v_heads", [P, BATCH * HEADS, TB, HD])
          with ExitStack() as st:
            wqkv = sb(st, "wqkv1", [P, 3, KC, D])
            wmod = sb(st, "wmod1", [P, KC, 6 * D])
            part1 = sb(st, "part1", [P, 4, GW], BF16)
            part2 = sb(st, "part2", [P, 4, GW], BF16)
            part3 = sb(st, "part3", [P, 4, GW], BF16)
            rest = sb(st, "rest", [P, 2, GW])
            s_wmod, s_w, s_modp, s_modd, s_ln, s_lnt, s_h, s_proj, s_p1, s_p3, s_v = [sem(n) for n in
                ("e_wmod", "e_w", "e_modp", "e_modd", "e_ln", "e_lnt", "e_h", "e_proj", "e_p1", "e_p3", "e_v")]
            s_sts = [sem(f"e_st{i}") for i in range(4)]
            NJ = 4 * NG
            with nc.Block() as block:
                @block.sync
                def _(sp):
                    sp.dma_start(wmod[:, :, :], a["wmod1"].rearrange("(k p) n -> p k n", p=P)).then_inc(s_wmod, 16)
                    for n, w in enumerate(("wq1", "wk1", "wv1")):
                        sp.dma_start(wqkv[:, n], a[w].rearrange("(k p) n -> p k n", p=P)).then_inc(s_w, 16)
                    for j in range(NJ):
                        g, w, m = j // 4, (j // 2) % 2, j % 2
                        b, col = g // GB, (g % GB) * GW
                        sp.wait_ge(s_p3, j + 1)
                        for n, part in enumerate((part1, part2, part3)):
                            sp.dma_start(qk_dram[w, n, b * D + m * P:b * D + (m + 1) * P, col:col + GW],
                                         part[:, j % 4, :]).then_inc(s_sts[j % 4], 16)
                    for i in range(4):
                        sp.wait_ge(s_sts[i], 48 * (NJ // 4))

                @block.scalar
                def _(act):
                    act.wait_ge(s_modd, 1)
                    for g in range(NG):
                        act.wait_ge(s_lnt, g + 1)
                        ln_modulate(1, SA, CA_, g, 0).then_inc(s_h, 1)
                        for j in range(4 * g, 4 * g + 4):
                            act.wait_ge(s_proj, 6 * g + j % 4 + 1)
                            if j >= 4:
                                act.wait_ge(s_sts[j % 4], 48 * (j // 4))
                            nc.scalar.copy(part1[:, j % 4, :], ps[:, 2 + j % 4, :]).then_inc(s_p1, 1)

                @block.vector
                def _(dve):
                    link = chain("e_dve", dve)
                    dve.wait_ge(s_modp, 1)
                    mod_finish(1, link).then_inc(s_modd, 1)
                    ln_dve(dve, 0, link, s_ln, 2)
                    for g in range(NG):
                        if g + 1 < NG:
                            ln_dve(dve, g + 1, link, s_ln, 2)
                        for j in range(4 * g, 4 * g + 4):
                            dve.wait_ge(s_p1, j + 1)
                            r = rest[:, j % 2, :]
                            link(nc.vector.tensor_tensor(r, ps[:, 2 + j % 4, :], part1[:, j % 4, :], ALU.subtract))
                            link(nc.vector.tensor_copy(part2[:, j % 4, :], r))
                            nc.vector.tensor_tensor(part3[:, j % 4, :], r, part2[:, j % 4, :],
                                                    ALU.subtract).then_inc(s_p3, 1)
                        for m in range(2):
                            dve.wait_ge(s_proj, 6 * g + 4 + m + 1)
                            for i in range(2):
                                t = 4 * g + 2 * m + i
                                b, tt = divmod(t, TB)
                                last = nc.vector.tensor_copy(vu[:, b * HEADS:(b + 1) * HEADS, tt, :],
                                                             ps[:, 6 + m, i * D:(i + 1) * D]
                                                             .rearrange("p (h d) -> p h d", h=HEADS))
                            last.then_inc(s_v, 1)

                @block.gpsimd
                def _(pool):
                    ln_pool(pool, 2)

                @block.tensor
                def _(pe):
                    pe.wait_ge(s_wmod, 16)
                    mod_columns(1, wmod).then_inc(s_modp, 1)
                    pe.wait_ge(s_modd, 1)
                    pe.wait_ge(s_w, 48)
                    for g in range(NG):
                        pe.wait_ge(s_ln, g + 1)
                        if g:
                            pe.wait_ge(s_h, g)
                        ln_transposes(g, 0).then_inc(s_lnt, 1)
                        pe.wait_ge(s_h, g + 1)
                        for j in range(4):
                            if g:
                                pe.wait_ge(s_p3, 4 * (g - 1) + j + 1)
                            for k in range(KC):
                                last = nc.tensor.matmul(ps[:, 2 + j, :], wqkv[:, j // 2, k, (j % 2) * P:(j % 2 + 1) * P],
                                                        h_t[:, k, g * GW:(g + 1) * GW], start=k == 0, stop=k == KC - 1)
                            last.then_inc(s_proj, 1)
                        for m in range(2):
                            if g:
                                pe.wait_ge(s_v, 2 * (g - 1) + m + 1)
                            for i in range(2):
                                t = 4 * g + 2 * m + i
                                for k in range(KC):
                                    last = nc.tensor.matmul(ps[:, 6 + m, i * D:(i + 1) * D],
                                                            h_t[:, k, t * P:(t + 1) * P], wqkv[:, 2, k, :],
                                                            start=k == 0, stop=k == KC - 1)
                            last.then_inc(s_proj, 1)

          with ExitStack() as st:
            NU = BATCH * HEADS
            NS = 4
            KR = 6 * HD
            KM = KR + 3 * TB
            qs = sb(st, "qs", [P, NS, SEQ], BF16)
            ks = sb(st, "ks", [P, NS, SEQ], BF16)
            vs = sb(st, "vs", [P, 2, TB, 32])
            ptile = sb(st, "p_tile", [P, 3, GW])
            hmax = sb(st, "hmax", [P, 2, TB])
            hrest = sb(st, "hrest", [P, TB])
            mparts = sb(st, "mparts", [P, P], BF16)
            blk = sb(st, "blk", [P, TB], BF16)
            cx = sb(st, "cx", [32, 2, GW])
            qk_in = [sem(f"f_qk{i}") for i in range(NS)]
            s_init, s_v, s_si, s_mx, s_mp, s_row, s_st, s_exp, s_av, s_cx = [sem(n) for n in
                ("f_init", "f_v", "f_s", "f_mx", "f_mp", "f_row", "f_st", "f_exp", "f_av", "f_cx")]
            s_cst = [sem("f_cst0"), sem("f_cst1")]
            s_seen = sem("f_seen")
            NTI = 4 + 8
            tiles = [(0, j) for j in range(4)] + [(1, j) for j in range(8)]
            s_dch = sem("f_dve")
            with nc.Block() as block:
                @block.sync
                def _(sp):
                    def load(u, slot, before):
                        row = u * HD if isinstance(u, int) else sp.snap(u * HD)
                        if before is not None:
                            sp.wait_ge(s_av, before)
                        for r, n in ((0, 3), (3 * HD, 2), (5 * HD, 1)):
                            for p in range(n):
                                sp.dma_start(qs[r + p * HD:r + (p + 1) * HD, slot, :],
                                             qk_dram[0, p, bass.ds(row, HD), :]).then_inc(qk_in[slot], 16)
                                sp.dma_start(ks[r + p * HD:r + (p + 1) * HD, slot, :],
                                             qk_dram[1, 3 - n, bass.ds(row, HD), :]).then_inc(qk_in[slot], 16)

                    def store(u, g, count):
                        row, one = (u * HD, u) if isinstance(u, int) else (sp.snap(u * HD), sp.snap(u))
                        sp.wait_ge(s_cx, count)
                        sp.sem_inc(s_seen, 1)
                        sp.dma_start(ctx_dram[bass.ds(row, HD), g * GW:(g + 1) * GW],
                                     cx[0:HD, g, :]).then_inc(s_cst[g], 16)
                        sp.dma_start(z_dram[bass.ds(one, 1), g * GW:(g + 1) * GW],
                                     cx[HD:HD + 1, g, :]).then_inc(s_cst[g], 16)

                    sp.wait_ge(s_init, 2)
                    for u in range(3):
                        load(u, u, None)
                    load(3, 3, None)
                    for g in range(2):
                        store(0, g, g + 1)
                    with sp.Fori(0, (NU - 4) // 4) as it:
                        for s in range(4):
                            load(it * 4 + (4 + s), s, it * (4 * NTI) + NTI * (1 + s))
                            for g in range(2):
                                store(it * 4 + (1 + s), g, it * 8 + (2 * (1 + s) + g + 1))
                    for u in range(NU - 3, NU):
                        for g in range(2):
                            store(u, g, 2 * u + g + 1)
                    for g in range(2):
                        sp.wait_ge(s_cst[g], 32 * NU)

                @block.gpsimd
                def _(pool):
                    nc.gpsimd.memset(vs[:, :, :, :], 0.0)
                    nc.gpsimd.memset(ks[:, :, :], 1.0).then_inc(s_init, 1)
                    nc.gpsimd.memset(qs[:, :, :], 0.0).then_inc(s_init, 1)
                    pool.wait_ge(s_init, 2)
                    nc.gpsimd.memset(vs[:, :, :, HD:HD + 1], 1.0).then_inc(s_init, 1)
                    nc.gpsimd.memset(mparts[:, :], 0.0).then_inc(s_init, 1)
                    pool.wait_ge(s_init, 4)

                    def values(u, slot, before):
                        at = u if isinstance(u, int) else pool.snap(u)
                        if before is not None:
                            pool.wait_ge(s_av, before)
                        nc.gpsimd.tensor_copy(vs[:, slot, :, 0:HD], vu[:, bass.ds(at, 1), :, :].rearrange(
                            "p a t d -> p (a t) d")).then_inc(s_v, 1)

                    for u in range(2):
                        values(u, u, None)
                    with pool.Fori(0, (NU - 2) // 2) as it:
                        for s in range(2):
                            values(it * 2 + (2 + s), s, it * (2 * NTI) + NTI * (1 + s))

                @block.tensor
                def _(pe):
                    def s_item(w, u, sl, i):
                        n = w * (TB + 1) + i
                        half = n % 2
                        cnt = u * TB + i
                        if i < TB:
                            if i == 0:
                                pe.wait_ge(qk_in[sl], pe_loads(u, sl))
                            if i == 0:
                                if not (isinstance(u, int) and u == 0):
                                    pe.wait_ge(s_mx, u * TB)
                            elif i == 1:
                                if not (isinstance(u, int) and u == 0):
                                    pe.wait_ge(s_row, u)
                            else:
                                pe.wait_ge(s_mx, cnt - 1)
                            k = (i + 1) * P
                            for lo in range(0, k, GW):
                                wd = min(GW, k - lo)
                                diag = lo + wd == k
                                out = ps[:, 2 * half + lo // GW, 0:wd]
                                last = nc.tensor.matmul(out, qs[0:KR, sl, i * P:(i + 1) * P],
                                                        ks[0:KR, sl, lo:lo + wd], start=True, stop=not diag)
                                if diag:
                                    last = nc.tensor.matmul(out[:, wd - P:wd], ident_b, mask_s, start=False, stop=True)
                            last.then_inc(s_si, 1)
                        else:
                            pe.wait_ge(s_mx, u * TB + TB)
                            pe.wait_ge(s_mp, u + 1)
                            nc.tensor.transpose(ps[:, 2 * half, 0:64].bitcast(BF16), mparts[:, :],
                                                ident_b).then_inc(s_si, 1)

                    def pe_loads(u, sl):
                        return (u - sl) * (192 // 4) + 192

                    def st_tile(u, sl, n):
                        g, j = tiles[n]
                        q0 = max(4 * g, j)
                        wd = (4 * g + 4 - q0) * P
                        if n == 0:
                            pe.wait_ge(s_row, u + 1)
                        if not (isinstance(u, int) and u == 0 and n < 2):
                            pe.wait_ge(s_exp, u * NTI + (n - 1))
                        diag = j >= 4 * g
                        out = ps[:, 4 + n % 2, 0:wd]
                        last = nc.tensor.matmul(out, ks[0:KM, sl, j * P:(j + 1) * P],
                                                qs[0:KM, sl, q0 * P:q0 * P + wd], start=True, stop=not diag)
                        if diag:
                            last = nc.tensor.matmul(out[:, 0:P], ident_b, mask_t, start=False, stop=True)
                        last.then_inc(s_st, 1)

                    def av_tile(u, par, n):
                        g, j = tiles[n]
                        q0 = max(4 * g, j)
                        off = (q0 - 4 * g) * P
                        if n == 0:
                            pe.wait_ge(s_v, u + 1)
                        if j == 0 and not (isinstance(u, int) and u == 0):
                            pe.wait_ge(s_cx, u * 2 + (g - 1))
                        pe.wait_ge(s_exp, u * NTI + (n + 1))
                        nc.tensor.matmul(ps[0:32, 6 + g, off:GW], vs[:, par, j, :], ptile[:, n % 3, 0:GW - off],
                                         start=j == 0, stop=j == 4 * g + 3).then_inc(s_av, 1)

                    def unit(u, s, ahead):
                        for n in range(NTI + 1):
                            if n < NTI:
                                st_tile(u, s % NS, n)
                            if ahead and n < TB:
                                s_item((s + 1) % 4, u + 1, (s + 1) % NS, n)
                            if ahead and n == TB + 1:
                                s_item((s + 1) % 4, u + 1, (s + 1) % NS, TB)
                            if n:
                                av_tile(u, s % 2, n - 1)

                    for i in range(TB + 1):
                        s_item(0, 0, 0, i)
                    unit(0, 0, True)
                    with pe.Fori(0, (NU - 4) // 4) as it:
                        for s in range(4):
                            unit(it * 4 + (1 + s), 1 + s, True)
                    for u in range(NU - 3, NU):
                        unit(u, u % 4, u < NU - 1)

                @block.scalar
                def _(act):
                    def exps(u):
                        for n in range(NTI):
                            g, j = tiles[n]
                            wd = (4 * g + 4 - max(4 * g, j)) * P
                            act.wait_ge(s_st, u * NTI + (n + 1))
                            if not (isinstance(u, int) and u == 0 and n < 3):
                                act.wait_ge(s_av, u * NTI + (n - 2))
                            nc.scalar.activation(ptile[:, n % 3, 0:wd], ps[:, 4 + n % 2, 0:wd], ACT.Exp,
                                                 scale=HD ** -0.5).then_inc(s_exp, 1)

                    exps(0)
                    with act.Fori(0, NU - 1) as it:
                        exps(it + 1)

                @block.vector
                def _(dve):
                    dve.wait_ge(s_init, 4)
                    nc.vector.tensor_copy(blk[:, :], consts[:, C_BLK:C_BLK + TB]).then_inc(s_dch, 1)
                    dve.wait_ge(s_dch, 1)

                    def maxima(w, u, i):
                        half = (w * (TB + 1) + i) % 2
                        k = (i + 1) * P
                        dve.wait_ge(s_si, u * (TB + 1) + (i + 1))
                        nc.vector.reduce_max(hmax[:, w % 2, i:i + 1],
                                             ps[:, 2 * half:2 * half + 2, :].rearrange("p a n -> p (a n)")[:, 0:k],
                                             AX.X).then_inc(s_mx, 1)

                    def minus_max(w, u):
                        m = hmax[:, w % 2, :]
                        parts = [mparts[:, KR + n * TB:KR + (n + 1) * TB] for n in range(3)]
                        dve.wait_ge(s_mx, u * TB + TB)
                        if not (isinstance(u, int) and u == 0):
                            dve.wait_ge(s_row, u)
                        link(nc.vector.tensor_scalar(parts[0], m, -1.0, None, ALU.mult), u, 0)
                        link(nc.vector.scalar_tensor_tensor(hrest[:, :], m, -1.0, parts[0], ALU.mult, ALU.subtract), u, 1)
                        link(nc.vector.tensor_copy(parts[1], hrest[:, :]), u, 2)
                        nc.vector.tensor_tensor(parts[2], hrest[:, :], parts[1], ALU.subtract).then_inc(s_mp, 1)

                    def max_rows(w, u):
                        half = (w * (TB + 1) + TB) % 2
                        dve.wait_ge(s_si, u * (TB + 1) + (TB + 1))
                        rows = slice(KR, KM)
                        nc.vector.tensor_tensor(qs[rows, w % NS, :].rearrange("p (i q) -> p i q", i=TB),
                                                bc(ps[rows, 2 * half, 0:64].bitcast(BF16), 1, TB),
                                                bc(blk[rows, :], 2, P), ALU.mult).then_inc(s_row, 1)

                    def context(u, g):
                        dve.wait_ge(s_av, u * NTI + (4 if g == 0 else 12))
                        if not (isinstance(u, int) and u == 0):
                            dve.wait_ge(s_cst[g], u * 32)
                        nc.vector.tensor_copy(cx[:, g, :], ps[0:32, 6 + g, :]).then_inc(s_cx, 1)

                    def link(ins, u, k):
                        ins.then_inc(s_dch, 1)
                        dve.wait_ge(s_dch, u * 3 + (1 + k + 1))

                    for i in range(TB):
                        maxima(0, 0, i)
                    minus_max(0, 0)
                    max_rows(0, 0)

                    def unit(u, s, ahead):
                        if ahead:
                            for i in range(5):
                                maxima((s + 1) % 4, u + 1, i)
                        context(u, 0)
                        if ahead:
                            for i in range(5, TB):
                                maxima((s + 1) % 4, u + 1, i)
                            minus_max((s + 1) % 4, u + 1)
                            max_rows((s + 1) % 4, u + 1)
                        context(u, 1)

                    unit(0, 0, True)
                    with dve.Fori(0, (NU - 4) // 4) as it:
                        for s in range(4):
                            unit(it * 4 + (1 + s), 1 + s, True)
                    for u in range(NU - 3, NU - 1):
                        unit(u, u % 4, True)
                    unit(NU - 1, (NU - 1) % 4, False)

        with ExitStack() as st:
            wo = sb(st, "wo", [P, KC, D])
            bo = sb(st, "bo", [P, KC])
            cxt = sb(st, "cxt", [P, BATCH, KC, SEQ])
            out_t = sb(st, "att_out_t", [P, KC, T])
            z128 = sb(st, "z128", [P, BATCH * HEADS * SEQ // P])
            rz128 = sb(st, "rz128", [P, BATCH * HEADS * SEQ // P])
            rzb = sb(st, "rzb", [P, BATCH, KC, SEQ])
            s_w, s_c, s_o, s_oe, s_tr, s_add, s_z, s_rz, s_rst, s_cn = [sem(f"g_{n}") for n in
                ("w", "c", "o", "oe", "tr", "add", "z", "rz", "rst", "cn")]
            s_rzb = [sem(f"g_rzb{i}") for i in range(4)]
            with nc.Block() as block:
                @block.sync
                def _(sp):
                    sp.dma_start(z128[:, :], z_dram.rearrange("u (a n) -> (u a) n", a=P // (BATCH * HEADS)))\
                        .then_inc(s_z, 16)
                    sp.dma_start(wo[:, :, :], a["wo1"].rearrange("(k p) n -> p k n", p=P)).then_inc(s_w, 16)
                    sp.dma_start(bo[:, :], a["bo1"]).then_inc(s_w, 16)
                    sp.dma_start(cxt[:, :, :, :], ctx_dram.rearrange("(b k p) n -> p b k n", b=BATCH, p=P))\
                        .then_inc(s_c, 16)
                    sp.wait_ge(s_rz, 1)
                    sp.dma_start(rz_dram.rearrange("u (a n) -> (u a) n", a=P // (BATCH * HEADS)),
                                 rz128[:, :]).then_inc(s_rst, 16)
                    sp.wait_ge(s_rst, 16)
                    for i in range(4):
                        b, k = divmod(i, KC)
                        rows = rz_dram[b * HEADS + k * 8:b * HEADS + k * 8 + 8, :]
                        sp.dma_start(rzb[:, b, k, :], bc(rows, 1, HD)).then_inc(s_rzb[i], 16)

                @block.tensor
                def _(pe):
                    pe.wait_ge(s_w, 32)
                    for g in range(NG):
                        pe.wait_ge(s_cn, KC * (g // GB + 1))
                        for m in range(KC):
                            if g >= 2:
                                pe.wait_ge(s_oe, 2 * (g - 2) + m + 1)
                            for k in range(KC):
                                last = nc.tensor.matmul(ps[:, 2 * (g % 2) + m, :], wo[:, k, m * P:(m + 1) * P],
                                                        cxt[:, g // GB, k, (g % GB) * GW:(g % GB + 1) * GW],
                                                        start=k == 0, stop=k == KC - 1)
                            last.then_inc(s_o, 1)
                        pe.wait_ge(s_oe, 2 * g + 2)
                        for t in range(4 * g, 4 * g + 4):
                            if t >= 4:
                                pe.wait_ge(s_add, t - 3)
                            for c in range(KC):
                                last = nc.tensor.transpose(ps[:, 4 + t % 4, c * P:(c + 1) * P],
                                                           out_t[:, c, t * P:(t + 1) * P], ident)
                            last.then_inc(s_tr, 1)

                @block.vector
                def _(dve):
                    dve.wait_ge(s_z, 16)
                    nc.vector.reciprocal(rz128[:, :], z128[:, :]).then_inc(s_rz, 1)
                    dve.wait_ge(s_c, 16)
                    for i in range(4):
                        b, k = divmod(i, KC)
                        dve.wait_ge(s_rzb[i], 16)
                        nc.vector.tensor_tensor(cxt[:, b, k, :], cxt[:, b, k, :], rzb[:, b, k, :],
                                                ALU.mult).then_inc(s_cn, 1)
                    dve.wait_ge(s_w, 32)
                    for g in range(NG):
                        for m in range(KC):
                            dve.wait_ge(s_o, 2 * g + m + 1)
                            nc.vector.tensor_scalar(out_t[:, m, g * GW:(g + 1) * GW], ps[:, 2 * (g % 2) + m, :],
                                                    bo[:, m:m + 1], mod_col(1, GA, m, g // GB),
                                                    ALU.add, ALU.mult).then_inc(s_oe, 1)
                        for t in range(4 * g, 4 * g + 4):
                            dve.wait_ge(s_tr, t + 1)
                            nc.vector.tensor_tensor(x_tok[:, t, :], ps[:, 4 + t % 4, 0:D], x_tok[:, t, :],
                                                    ALU.add).then_inc(s_add, 1)

        recycle(kept)

        with ExitStack() as keep:
            de = sb(keep, "de_t", [P, KC, NEXP])
            ue = sb(keep, "ue", [P, NEXP // P, D])
            pexp = sb(keep, "pexp", [P, NEXP // P, T])
            with ExitStack() as st:
                wq = sb(st, "wq_r", [P, KC, R1])
                keys = sb(st, "keys", [P, 2, NKEY])
                qr = sb(st, "qr", [P, T])
                rt = sb(st, "rt", [P, NT, 2, NKEY])
                srt = sb(st, "srt", [P, NT, 2, TOPK])
                ids = sb(st, "ids", [P, NT, 2, TOPK], U32)
                idf = sb(st, "idf", [P, NT, 2, TOPK])
                cand = sb(st, "cand", [P, NT, TOPK, TOPK])
                csel = sb(st, "csel", [P, NT, TOPK, TOPK])
                cprob = sb(st, "cprob", [P, NT, TOPK, TOPK])
                ctop = sb(st, "ctop", [P, NT, TOPK])
                cntj = sb(st, "cntj", [P, NT, TOPK])
                rowp = sb(st, "rowp", [P, NT, TOPK])
                far = sb(st, "far", [P, NT, TOPK])
                zc = sb(st, "zc", [P, NT])
                lnz = sb(st, "lnz", [P, NT])
                rzc = sb(st, "rzc", [P, NT])
                far_s = sb(st, "far_s", [P, NT])
                eq = sb(st, "eq", [P, 2, NKEY, TOPK])
                eqa = sb(st, "eqa", [P, NT, NA, TOPK])
                us = sb(st, "us", [P, NT, NA + NKEY + 1])
                ud = sb(st, "ud", [P, NT, NA + NKEY])
                ust = sb(st, "us_t", [NA + NKEY + 1, T])
                udt = sb(st, "ud_t", [NA + NKEY, T])
                pex = sb(st, "pex", [P, 2, GW])
                s_in, s_ln, s_lnt, s_h, s_q, s_qe, s_r, s_re, s_cd, s_ce, s_zd, s_lz, s_u, s_ut, s_ute, s_ex, s_pe, \
                    s_pm, s_l = [sem(f"h_{n}") for n in ("in", "ln", "lnt", "h", "q", "qe", "r", "re", "cd", "ce",
                                                         "zd", "lz", "u", "ut", "ute", "ex", "pe", "pm", "l")]
                iota = consts[:, C_IOTA:C_IOTA + NKEY]
                rank = consts[:, C_RANK:C_RANK + TOPK]
                NM = 4 * NG
                with nc.Block() as block:
                    @block.sync
                    def _(sp):
                        sp.dma_start(wq[:, :, :], a["wq_r"].rearrange("(k p) n -> p k n", p=P)).then_inc(s_in, 16)
                        for half in range(2):
                            sp.dma_start(keys[half * 64:(half + 1) * 64, :, :],
                                         a["keys"].rearrange("t d k -> d t k")).then_inc(s_in, 16)
                        sp.dma_start(de[:, :, :], a["de_t"].rearrange("(k p) e -> p k e", p=P)).then_inc(s_l, 16)
                        sp.dma_start(ue[:, :, :], a["ue"].rearrange("(e p) h -> p e h", p=P)).then_inc(s_l, 16)
                        sp.wait_ge(s_l, 32)

                    @block.scalar
                    def _(act):
                        for g in range(NG):
                            act.wait_ge(s_lnt, g + 1)
                            ln_modulate(1, SB_, CB, g, 0).then_inc(s_h, 1)
                            act.wait_ge(s_q, g + 1)
                            nc.scalar.copy(qr[:, g * GW:(g + 1) * GW], ps[:, 2 + g % 2, :]).then_inc(s_qe, 1)
                        for n in range(TB):
                            act.wait_ge(s_r, n + 1)
                            nc.scalar.copy(rt[:, 2 * n:2 * n + 2, :, :],
                                           ps[:, 4 - 2 * (n % 2):6 - 2 * (n % 2), 0:2 * NKEY]
                                           .rearrange("p h (t k) -> p h t k", t=2)).then_inc(s_re, 1)
                        act.wait_ge(s_cd, 1)
                        nc.scalar.activation(cprob[:, :, :, :], cand[:, :, :, :], ACT.Exp).then_inc(s_ce, 1)
                        act.wait_ge(s_zd, 1)
                        nc.scalar.activation(lnz[:, :], zc[:, :], ACT.Ln).then_inc(s_lz, 1)
                        for j in range(NM):
                            act.wait_ge(s_ex, 2 * j + 1)
                            if j >= 2:
                                act.wait_ge(s_pe, j - 1)
                            nc.scalar.activation(pex[:, j % 2, :], ps[:, 2 * (j % 2), :], ACT.Exp).then_inc(s_pm, 1)

                    @block.vector
                    def _(dve):
                        link = chain("h_dve", dve)
                        for g in range(NG):
                            ln_dve(dve, g, link, s_ln, 3)
                        for n in range(TB):
                            dve.wait_ge(s_re, n + 1)
                            for t in range(2 * n, 2 * n + 2):
                                for w in range(2):
                                    last = nc.vector.max(srt[:, t, w, :], rt[:, t, w, :])
                            link(last)
                            for t in range(2 * n, 2 * n + 2):
                                for w in range(2):
                                    last = nc.vector.max_index(ids[:, t, w, :], srt[:, t, w, :], rt[:, t, w, :])
                        link(last)
                        link(nc.vector.tensor_copy(idf[:, :, :, :], ids[:, :, :, :]))
                        for t in range(NT):
                            last = nc.vector.tensor_tensor(cand[:, t], bc(srt[:, t, 0, :], 2, TOPK),
                                                           bc(srt[:, t, 1, :], 1, TOPK), ALU.add)
                        link(last)
                        for t in range(NT):
                            last = nc.vector.max(ctop[:, t, :], cand[:, t].rearrange("p i j -> p (i j)"))
                        link(last)
                        for t in range(NT):
                            last = nc.vector.match_replace(csel[:, t].rearrange("p i j -> p (i j)"), ctop[:, t, :],
                                                           cand[:, t].rearrange("p i j -> p (i j)"), REPLACED)
                        link(last)
                        flat = lambda v: v[:, :, :, :].rearrange("p t i j -> p t (i j)")
                        link(nc.vector.tensor_tensor(flat(csel), flat(csel), flat(cand), ALU.not_equal))
                        nc.vector.tensor_tensor(flat(cand), flat(cand), bc(ctop[:, :, 0], 2, 64),
                                                ALU.subtract).then_inc(s_cd, 1)
                        link(nc.vector.tensor_reduce(cntj[:, :, :], csel[:, :, :, :], AX.X, ALU.add))
                        for t in range(NT):
                            last = nc.vector.tensor_tensor(eqa[:, t], bc(idf[:, t, 0, :], 1, NA),
                                                           bc(iota[:, 0:NA], 2, TOPK), ALU.is_equal)
                        link(last)
                        for t in range(NT):
                            last = nc.vector.tensor_tensor(eqa[:, t], eqa[:, t], bc(cntj[:, t, :], 1, NA), ALU.mult)
                        link(last)
                        link(nc.vector.tensor_reduce(ud[:, :, 0:NA], eqa[:, :, :, :], AX.X, ALU.add))
                        for t in range(NT):
                            e = eq[:, t % 2, :, :]
                            link(nc.vector.tensor_tensor(e, bc(idf[:, t, 1, :], 1, NKEY), bc(iota, 2, TOPK),
                                                         ALU.is_equal))
                            link(nc.vector.tensor_tensor(e, e, bc(rank, 1, NKEY), ALU.mult))
                            last = nc.vector.tensor_reduce(ud[:, t, NA:], e, AX.X, ALU.add)
                        link(last)
                        dve.wait_ge(s_ce, 1)
                        link(nc.vector.tensor_tensor(flat(cprob), flat(cprob), flat(csel), ALU.mult))
                        link(nc.vector.tensor_reduce(rowp[:, :, :], cprob[:, :, :, :], AX.X, ALU.add))
                        link(nc.vector.tensor_reduce(zc[:, :], rowp[:, :, :], AX.X, ALU.add))
                        link(nc.vector.reciprocal(rzc[:, :], zc[:, :]))
                        nc.vector.tensor_scalar(far[:, :, :], idf[:, :, 0, :], float(NA), None,
                                                ALU.is_ge).then_inc(s_zd, 1)
                        dve.wait_ge(s_zd, 1)
                        link(nc.vector.tensor_tensor(far[:, :, :], far[:, :, :], rowp[:, :, :], ALU.mult))
                        link(nc.vector.tensor_reduce(far_s[:, :], far[:, :, :], AX.X, ALU.add))
                        nc.vector.tensor_tensor(us[:, :, NA + NKEY], far_s[:, :], rzc[:, :], ALU.mult)
                        nc.vector.tensor_tensor(us[:, :, NA:NA + NKEY], rt[:, :, 1, :], bc(srt[:, :, 1, 0], 2, NKEY),
                                                ALU.subtract)
                        link(nc.vector.tensor_tensor(us[:, :, 0:NA], rt[:, :, 0, 0:NA], bc(srt[:, :, 0, 0], 2, NA),
                                                     ALU.subtract))
                        dve.wait_ge(s_lz, 1)
                        nc.vector.tensor_tensor(us[:, :, 0:NA], us[:, :, 0:NA], bc(lnz[:, :], 2, NA),
                                                ALU.subtract).then_inc(s_u, 1)
                        for n in range(NT // 2):
                            for v, dst, rows in ((0, ust, NA + NKEY + 1), (1, udt, NA + NKEY)):
                                dve.wait_ge(s_ut, 2 * n + v + 1)
                                nc.vector.tensor_copy(
                                    dst[:, n * 256:(n + 1) * 256].rearrange("p (s h) -> p h s", h=2),
                                    ps[0:rows, 6 + v, 0:256].rearrange("p (h s) -> p h s", h=2)).then_inc(s_ute, 1)
                        for j in range(NM):
                            g, e = divmod(j, 4)
                            cols = slice(g * GW, (g + 1) * GW)
                            dve.wait_ge(s_ex, 2 * j + 2)
                            dve.wait_ge(s_pm, j + 1)
                            ins = nc.vector.scalar_tensor_tensor(pexp[:, e, cols], ps[:, 2 * (j % 2) + 1, :],
                                                                 float(TOPK) + 0.5, pex[:, j % 2, :],
                                                                 ALU.is_gt, ALU.mult)
                            if e == 0:
                                link(ins)
                                ins = nc.vector.tensor_tensor(pexp[:, 0, cols], ps[:, 4 + g % 2, :],
                                                              pexp[:, 0, cols], ALU.add)
                            ins.then_inc(s_pe, 1)

                    @block.gpsimd
                    def _(pool):
                        ln_pool(pool, 3, range(2))
                        for g in range(NG):
                            if g + 2 < NG:
                                ln_pool(pool, 3, (g + 2,))
                            split_h(pool, g, s_h, 1)

                    @block.tensor
                    def _(pe):
                        pe.wait_ge(s_in, 48)
                        for g in range(NG):
                            pe.wait_ge(s_ln, g + 1)
                            if g:
                                pe.wait_ge(s_h, g)
                            ln_transposes(g, 0).then_inc(s_lnt, 1)
                            pe.wait_ge(s_h, g + 1)
                            if g >= 2:
                                pe.wait_ge(s_qe, g - 1)
                            for k in range(KC):
                                last = nc.tensor.matmul(ps[:, 2 + g % 2, :], wq[:, k, :],
                                                        h_t[:, k, g * GW:(g + 1) * GW], start=k == 0, stop=k == KC - 1)
                            last.then_inc(s_q, 1)
                        pe.wait_ge(s_qe, NG)
                        for n in range(TB):
                            if n >= 2:
                                pe.wait_ge(s_re, n - 1)
                            for half in range(2):
                                for w in range(2):
                                    r = slice(half * 64, half * 64 + 64)
                                    last = nc.tensor.matmul(
                                        ps[:, 4 - 2 * (n % 2) + half, w * NKEY:(w + 1) * NKEY],
                                        qr[r, w * SEQ + n * P:w * SEQ + (n + 1) * P], keys[r, w, :],
                                        start=True, stop=True)
                            last.then_inc(s_r, 1)
                        pe.wait_ge(s_u, 1)
                        for n in range(NT // 2):
                            for v, (src, rows) in enumerate(((us, NA + NKEY + 1), (ud, NA + NKEY))):
                                if n:
                                    pe.wait_ge(s_ute, 2 * (n - 1) + v + 1)
                                for half in range(2):
                                    last = nc.tensor.transpose(ps[0:rows, 6 + v, half * P:(half + 1) * P],
                                                               src[:, 2 * n + half, :], ident)
                                last.then_inc(s_ut, 1)
                        pe.wait_ge(s_ute, NT)
                        for j in range(NM):
                            g, e = divmod(j, 4)
                            cols = slice(g * GW, (g + 1) * GW)
                            if j >= 2:
                                pe.wait_ge(s_pe, j - 1)
                            if e == 0:
                                nc.tensor.matmul(ps[:, 4 + g % 2, :], consts[0:NA + NKEY + 1, C_SELR:C_SELR + P],
                                                 ust[:, cols], start=True, stop=True)
                            sel = consts[0:NA + NKEY, C_SEL + e * P:C_SEL + (e + 1) * P]
                            nc.tensor.matmul(ps[:, 2 * (j % 2), :], sel, ust[0:NA + NKEY, cols],
                                             start=True, stop=True).then_inc(s_ex, 1)
                            nc.tensor.matmul(ps[:, 2 * (j % 2) + 1, :], sel, udt[:, cols],
                                             start=True, stop=True).then_inc(s_ex, 1)

            ffn("i", 1, PAIRS1, a["mlp"], False)

            with ExitStack() as st:
                score = sb(st, "score", [P, 2, GW])
                coef = sb(st, "coef", [P, 3, GW])
                out_t = sb(st, "pk_out_t", [P, KC, T])
                s_sc, s_silu, s_cf, s_up, s_oe, s_tr, s_add, s_store = [sem(f"j_{n}") for n in
                    ("sc", "silu", "cf", "up", "oe", "tr", "add", "store")]
                NE = NEXP // P
                units = NE * NG
                with nc.Block() as block:
                    @block.sync
                    def _(sp):
                        for t in range(NT):
                            sp.wait_ge(s_add, t + 1)
                            sp.dma_start(a["out"][t // TB, (t % TB) * P:(t % TB + 1) * P, :], x_tok[:, t, :])\
                                .then_inc(s_store, 16)
                        sp.wait_ge(s_store, 16 * NT)

                    @block.scalar
                    def _(act):
                        for u in range(units):
                            act.wait_ge(s_sc, u + 1)
                            if u >= 2:
                                act.wait_ge(s_cf, u - 1)
                            nc.scalar.activation(score[:, u % 2, :], ps[:, u % 2, :], ACT.Silu).then_inc(s_silu, 1)

                    @block.vector
                    def _(dve):
                        def finish(g):
                            b = g // GB
                            dve.wait_ge(s_up, NE * (g + 1))
                            for c in range(KC):
                                nc.vector.tensor_scalar(out_t[:, c, g * GW:(g + 1) * GW], ps[:, 2 + 2 * (g % 2) + c, :],
                                                        mod_col(1, GB_, c, b), None, ALU.mult).then_inc(s_oe, 1)

                        def add(g):
                            for t in range(4 * g, 4 * g + 4):
                                dve.wait_ge(s_tr, t + 1)
                                nc.vector.tensor_tensor(x_tok[:, t, :], ps[:, 6 + t % 2, 0:D], x_tok[:, t, :],
                                                        ALU.add).then_inc(s_add, 1)

                        for u in range(units):
                            g, e = divmod(u, NE)
                            dve.wait_ge(s_silu, u + 1)
                            if u >= 3:
                                dve.wait_ge(s_up, u - 2)
                            nc.vector.tensor_tensor(coef[:, u % 3, :], score[:, u % 2, :],
                                                    pexp[:, e, g * GW:(g + 1) * GW], ALU.mult).then_inc(s_cf, 1)
                            if e == 1 and g:
                                finish(g - 1)
                            if e == 2 and g:
                                add(g - 1)
                        finish(NG - 1)
                        add(NG - 1)

                    @block.tensor
                    def _(pe):
                        def up(u):
                            g, e = divmod(u, NE)
                            pe.wait_ge(s_cf, u + 1)
                            if e == 0 and g >= 2:
                                pe.wait_ge(s_oe, 2 * (g - 1))
                            for c in range(KC):
                                last = nc.tensor.matmul(ps[:, 2 + 2 * (g % 2) + c, :], ue[:, e, c * P:(c + 1) * P],
                                                        coef[:, u % 3, :], start=e == 0, stop=e == NE - 1)
                            last.then_inc(s_up, 1)

                        def back(g):
                            pe.wait_ge(s_oe, 2 * g + 2)
                            for t in range(4 * g, 4 * g + 4):
                                if t >= 2:
                                    pe.wait_ge(s_add, t - 1)
                                for c in range(KC):
                                    last = nc.tensor.transpose(ps[:, 6 + t % 2, c * P:(c + 1) * P],
                                                               out_t[:, c, t * P:(t + 1) * P], ident)
                                last.then_inc(s_tr, 1)

                        for u in range(units + 1):
                            if u < units:
                                g, e = divmod(u, NE)
                                if u >= 2:
                                    pe.wait_ge(s_silu, u - 1)
                                for k in range(KC):
                                    last = nc.tensor.matmul(ps[:, u % 2, :], de[:, k, e * P:(e + 1) * P],
                                                            h_t[:, k, g * GW:(g + 1) * GW],
                                                            start=k == 0, stop=k == KC - 1)
                                last.then_inc(s_sc, 1)
                            if u:
                                up(u - 1)
                            if u % NE == 3 and u > NE:
                                back(u // NE - 1)
                        back(NG - 1)


def constants():
    import numpy as np
    c = np.zeros((P, C_N), np.float32)
    p = np.arange(P)
    c[:, C_ID:C_ID + P] = np.eye(P)
    c[:, C_MS:C_MS + P] = np.where(p[None, :] > p[:, None], MASKED, 0.0)
    c[:, C_MT:C_MT + P] = np.where(p[:, None] > p[None, :], MASKED, 0.0)
    for r in range(3 * TB):
        c[6 * HD + r, C_BLK + r % TB] = 1.0
    c[:, C_IOTA:C_IOTA + NKEY] = np.arange(NKEY)
    c[:, C_RANK:C_RANK + TOPK] = TOPK - np.arange(TOPK)
    for e in range(NEXP):
        i = NEXP - 1 - e
        c[i // NKEY, C_SEL + e] = 1.0
        c[NA + i % NKEY, C_SEL + e] = 1.0
    c[NA + NKEY, C_SELR] = 1.0
    return c


def laid_out(inputs):
    import numpy as np
    x = {k: np.asarray(v) for k, v in inputs.items()}

    def pack(gates, ups, downs):
        n = gates.shape[0] // P
        g = gates.reshape(n, P, KC, P).transpose(0, 3, 2, 1)
        u = ups.reshape(n, P, KC, P).transpose(0, 3, 2, 1)
        gu = np.concatenate([g, u], axis=3).reshape(n, P, KC * 2 * P)
        return np.ascontiguousarray(np.concatenate([gu, downs.reshape(n, P, D)], axis=2).reshape(n * P, 3 * D))

    zero = np.zeros((I0, D), np.float32)
    gu = x["L0_ffn_gu_w"]
    moe = pack(np.concatenate([gu[:, :I0].reshape(-1, D), x["L0_ffn_sh_gate_w"], zero]),
               np.concatenate([gu[:, I0:].reshape(-1, D), x["L0_ffn_sh_up_w"], zero]),
               np.concatenate([x["L0_ffn_dp_w"].transpose(0, 2, 1).reshape(-1, D),
                               x["L0_ffn_sh_down_w"].T, zero]))
    mlp = pack(x["L1_ffn_gate_w"].T, x["L1_ffn_up_w"].T, x["L1_ffn_down_w"])
    gate0 = np.concatenate([x["L0_ffn_gate_w"], x["L0_ffn_sh_gate1_w"], np.zeros((1, D), np.float32)]).T

    def col(v):
        return v.reshape(KC, P).T

    cond = np.stack([x["L0_c"], x["L1_c"]]).transpose(0, 2, 1).reshape(2, KC, P, BATCH).transpose(2, 0, 1, 3)
    out = {
        "x": x["L0_attn_x"], "cond": cond, "consts": constants(), "wmod0": x["L0_wmod"], "wmod1": x["L1_wmod"],
        "wq0": x["L0_attn_Wq"], "wk0": x["L0_attn_Wk"], "wv0": x["L0_attn_Wv"],
        "bq0": col(x["L0_attn_bq"]), "bk0": col(x["L0_attn_bk"]), "bv0": x["L0_attn_bv"],
        "gate0": gate0, "moe": moe, "mlp": mlp,
        "wq1": x["L1_attn_W_query"], "wk1": x["L1_attn_W_key"], "wv1": x["L1_attn_W_value"],
        "wo1": x["L1_attn_W_out"], "bo1": col(x["L1_attn_b_out"]),
        "wq_r": x["L1_ffn_W_q"], "keys": x["L1_ffn_keys"],
        "de_t": x["L1_ffn_down_embed"][::-1].T, "ue": x["L1_ffn_up_embed"][::-1],
    }
    return {k: np.ascontiguousarray(v) for k, v in out.items()}


def kernel(**inputs):
    import concourse.bacc as bacc
    from concourse.bass_utils import run_bass_kernel_spmd

    nc = bacc.Bacc("TRN2", target_bir_lowering=False, num_devices=1)
    arrays = laid_out(inputs)
    aps = {k: nc.dram_tensor(f"in_{k}", v.shape, F32, kind="ExternalInput").ap() for k, v in arrays.items()}
    aps["out"] = nc.dram_tensor("out_x", (BATCH, SEQ, D), F32, kind="ExternalOutput").ap()
    build(nc, aps)
    r = run_bass_kernel_spmd(nc, [{f"in_{k}": v for k, v in arrays.items()}], core_ids=[0])
    return r.results[0]["out_x"]
```

```python
from contextlib import ExitStack

import concourse.bass as bass
from concourse import mybir

F32 = mybir.dt.float32
F32R = mybir.dt.float32r
BF16 = mybir.dt.bfloat16
U32 = mybir.dt.uint32
ALU = mybir.AluOpType
ACT = mybir.ActivationFunctionType
AX = mybir.AxisListType

P = 128
BATCH, SEQ, D = 2, 1024, 256
T = BATCH * SEQ
NT = T // P
TB = SEQ // P
KC = D // P
GW = 512
NG = T // GW
GB = SEQ // GW
EPS = 1e-5
E0, I0, TOPK = 64, 64, 8
PAIRS0 = E0 // 2 + 1
HEADS, HD = 16, 16
INTER = 1024
PAIRS1 = INTER // P
R1, NKEY, NEXP = 128, 64, 512
NA = NEXP // NKEY
SHIFT_A, SCALE_A, GATE_A, SHIFT_B, SCALE_B, GATE_B = range(6)
CXR = 32 + HD
MASKED = -1.0e30
REPLACED = -3.0e38
C_ID, C_MS, C_MT, C_BLK, C_IOTA, C_RANK, C_SEL, C_SELR = 0, 128, 256, 384, 392, 456, 464, 976
C_N = 1104


def bc(ap, axis, n):
    v = ap.unsqueeze(axis)
    shape = list(v.shape)
    shape[axis] = n
    return v.to_broadcast(shape)


class Tick:

    def __init__(self, sem):
        self.sem, self.n = sem, 0

    def inc(self, ins):
        ins.then_inc(self.sem, 1)
        self.n += 1


def build(nc, a):
    ctx = ExitStack()
    held = []

    def sem(name):
        held.append(nc.alloc_semaphore(name=name))
        return held[-1]

    def recycle(since):
        nc.clear_and_free_semaphores(held[since:])
        del held[since:]
        nc.all_engine_barrier()

    def sb(stack, name, shape, dt=F32):
        return stack.enter_context(nc.sbuf_tensor(name, shape, dt))

    with ctx:
        wt_dram = nc.dram_tensor("router_weights_t", (2 * PAIRS0, T), F32, kind="Internal").ap()
        qk_dram = nc.dram_tensor("qk_parts", (2, 3, BATCH * D, SEQ), BF16, kind="Internal").ap()
        ctx_dram = nc.dram_tensor("context_t", (BATCH * HEADS * CXR, SEQ), F32, kind="Internal").ap()
        rz_dram = nc.dram_tensor("inverse_sums", (BATCH * HEADS, SEQ), F32, kind="Internal").ap()

        ps = ctx.enter_context(nc.psum_tensor("ps", [P, 8, GW], F32))
        consts = sb(ctx, "consts", [P, C_N])
        cbf = sb(ctx, "cbf", [P, 384], BF16)
        x_tok = sb(ctx, "x_tok", [P, NT, D])
        h_t = sb(ctx, "h_t", [P, KC, T])
        h_hi = sb(ctx, "h_hi", [P, KC, T], F32R)
        h_lo = sb(ctx, "h_lo", [P, KC, T], F32R)
        xn = sb(ctx, "xn", [P, NT, D])
        stats = sb(ctx, "stats", [P, NT, 6])
        mv = sb(ctx, "mv", [P, NT, 2])
        rstd = sb(ctx, "rstd", [P, NT])
        veps = sb(ctx, "veps", [P, NT])
        half = sb(ctx, "minus_half", [P, NT])
        cond = sb(ctx, "cond", [P, 2, KC, BATCH])
        csilu = sb(ctx, "csilu", [P, 2, KC, BATCH])
        modc = sb(ctx, "modc", [P, 2, 12, BATCH])
        gtmp = sb(ctx, "gtmp", [P, 2, 2, 2, KC, BATCH])
        ident = consts[:, C_ID:C_ID + P]
        ident_b = cbf[:, 0:P]
        mask_s = cbf[:, P:2 * P]
        mask_t = cbf[:, 2 * P:3 * P]

        def mod_col(layer, which, c, b):
            return modc[:, layer, which * KC + c, b:b + 1]

        s_var, s_rstd, s_half = sem("ln_var"), sem("ln_rstd"), sem("ln_half")

        def ln_pool(pool, ln, groups=range(NG)):
            for g in groups:
                pool.wait_ge(s_var, ln * NG + g + 1)
                nc.gpsimd.tensor_tensor(rstd[:, 4 * g:4 * g + 4], veps[:, 4 * g:4 * g + 4], half[:, 4 * g:4 * g + 4],
                                        ALU.pow).then_inc(s_rstd, 1)

        def ln_stats(g, link):
            for t in range(4 * g, 4 * g + 4):
                last = nc.vector.bn_stats(stats[:, t, :], x_tok[:, t, :])
            link(last)
            for t in range(4 * g, 4 * g + 4):
                last = nc.vector.bn_aggr(mv[:, t, :], stats[:, t, :])
            link(last)
            nc.vector.tensor_scalar(veps[:, 4 * g:4 * g + 4], mv[:, 4 * g:4 * g + 4, 1], EPS, None,
                                    ALU.add).then_inc(s_var, 1)

        def ln_rows(dve, g, ready, ln):
            dve.wait_ge(s_rstd, ln * NG + g + 1)
            for t in range(4 * g, 4 * g + 4):
                last = nc.vector.tensor_scalar(xn[:, t, :], x_tok[:, t, :], mv[:, t, 0:1], rstd[:, t:t + 1],
                                               ALU.subtract, ALU.mult)
            last.then_inc(ready, 1)

        def ln_transposes(g, bank):
            for c in range(KC):
                for j in range(4):
                    last = nc.tensor.transpose(ps[:, bank + c, j * P:(j + 1) * P],
                                               xn[:, 4 * g + j, c * P:(c + 1) * P], ident)
            return last

        def ln_modulate(layer, shift, scale, g, bank):
            for c in range(KC):
                last = nc.scalar.activation(h_t[:, c, g * GW:(g + 1) * GW], ps[:, bank + c, :], ACT.Identity,
                                            bias=mod_col(layer, shift, c, g // GB),
                                            scale=mod_col(layer, scale, c, g // GB))
            return last

        def high_h(layer, shift, scale, g, bank):
            for c in range(KC):
                last = nc.scalar.activation(h_hi[:, c, g * GW:(g + 1) * GW], ps[:, bank + c, :], ACT.Identity,
                                            bias=mod_col(layer, shift, c, g // GB),
                                            scale=mod_col(layer, scale, c, g // GB))
            return last

        def low_h(pool, g, s_split):
            cols = slice(g * GW, (g + 1) * GW)
            pool.wait_ge(s_split, g + 1)
            return nc.gpsimd.tensor_tensor(h_lo[:, :, cols], h_t[:, :, cols], h_hi[:, :, cols].bitcast(F32),
                                           ALU.subtract)

        def chain(name, engine):
            tick = Tick(sem(name))

            def link(ins):
                tick.inc(ins)
                engine.wait_ge(tick.sem, tick.n)
            return link

        def mod_columns(layer, wmod, out, chunks):
            for j in chunks:
                for k in range(KC):
                    last = nc.tensor.matmul(out[:, 2 * j:2 * j + 2], wmod[:, k, j * P:(j + 1) * P],
                                            csilu[:, layer, k, :], start=k == 0, stop=k == KC - 1)
            return last

        def guard(g, tmp, link):
            link(nc.vector.tensor_scalar(tmp[0], g, 0.0, 2.0, ALU.is_ge, ALU.mult))
            link(nc.vector.scalar_tensor_tensor(tmp[1], g, -1.0, g, ALU.mult, ALU.max))
            link(nc.vector.tensor_scalar(tmp[1], tmp[1], 0.25, None, ALU.max))
            link(nc.vector.scalar_tensor_tensor(g, tmp[0], -1.0, tmp[1], ALU.add, ALU.mult))

        def mod_finish(layer, link, src, parts):
            for part in parts:
                m = modc[:, layer, 6 * part:6 * part + 6, :]
                link(nc.vector.tensor_copy(m, src[:, 12 * part:12 * part + 12].rearrange("p (j b) -> p j b", b=BATCH)))
                guard(m[:, 4:6, :], (gtmp[:, layer, part, 0], gtmp[:, layer, part, 1]), link)
                last = nc.vector.tensor_scalar(m[:, 2:4, :], m[:, 2:4, :], 1.0, None, ALU.add)
            return last

        kept = len(held)

        with ExitStack() as st:
            wqkv = sb(st, "wqkv", [P, 3, KC, D])
            wq_hi = sb(st, "wqkv_hi", [P, 3, KC, D], F32R)
            wq_lo = sb(st, "wqkv_lo", [P, 3, KC, D], F32R)
            bqk = sb(st, "bqk", [P, 2, KC])
            bv = sb(st, "bv", [P, D])
            wmod = sb(st, "wmod", [P, KC, 6 * D])
            crep = sb(st, "crep", [P, BATCH, KC, P])
            ga = sb(st, "ga_rows", [P, BATCH, D])
            gat = sb(st, "ga_tmp", [P, 2, BATCH, D])
            qt = sb(st, "q_t", [P, KC, T])
            kt = sb(st, "k_t", [P, KC, T])
            vtok = sb(st, "v_tok", [P, NT, D])
            probs = sb(st, "probs", [P, 3, SEQ])
            probs_t = sb(st, "probs_t", [P, 2, SEQ])
            mx = sb(st, "mx", [P, NT])
            nmx = sb(st, "nmx", [P, NT])
            zs = sb(st, "zs", [P, NT])
            rz = sb(st, "rz", [P, NT])
            att = sb(st, "att", [P, 2, D])
            att2 = sb(st, "att2", [P, 2, D])
            s_const, s_cond, s_wqkv, s_bias, s_consts = [sem(n) for n in
                ("a_const", "a_cond", "a_wqkv", "a_bias", "a_consts")]
            s_wmods = [sem("a_wmod_att"), sem("a_wmod_ffn")]
            s_x = [sem(f"a_x{g}") for g in range(NG)]
            s_csilu, s_crep, s_modp, s_modd, s_ln, s_lnt, s_h, s_hlo, s_whi, s_wlo, s_wmod1 = [sem(n) for n in
                ("a_csilu", "a_crep", "a_modp", "a_modd", "a_ln", "a_lnt", "a_h", "a_h_lo", "a_whi", "a_wlo",
                 "a_wmod1")]
            s_proj, s_pev_a, s_pev_d, s_cb = [sem(n) for n in ("a_proj", "a_pev_act", "a_pev_dve", "a_cb")]
            with nc.Block() as block:
                @block.sync
                def _(sp):
                    def load_mod(n):
                        cols = slice(n * 3 * D, (n + 1) * 3 * D)
                        sp.dma_start(wmod[:, :, cols], a["wmod0"].rearrange("(k p) n -> p k n", p=P)[:, :, cols])\
                            .then_inc(s_wmods[n], 16)

                    sp.dma_start(cond[:, :, :, :], a["cond"]).then_inc(s_cond, 16)
                    for g in range(NG):
                        sp.dma_start(x_tok[:, 4 * g:4 * g + 4, :],
                                     a["x"].rearrange("b (t p) d -> p (b t) d", p=P)[:, 4 * g:4 * g + 4, :])\
                            .then_inc(s_x[g], 16)
                        if g == 0:
                            load_mod(0)
                            sp.dma_start(consts[:, 0:C_BLK], a["consts"][:, 0:C_BLK]).then_inc(s_const, 16)
                            for n, w in enumerate(("wq0", "wk0", "wv0")):
                                sp.dma_start(wqkv[:, n], a[w].rearrange("(k p) n -> p k n", p=P))\
                                    .then_inc(s_wqkv, 16)
                            sp.dma_start(bqk[:, 0, :], a["bq0"]).then_inc(s_bias, 16)
                            sp.dma_start(bqk[:, 1, :], a["bk0"]).then_inc(s_bias, 16)
                            sp.dma_start(bv[:, :], a["bv0"].unsqueeze(0).to_broadcast([P, D])).then_inc(s_bias, 16)
                    load_mod(1)
                    sp.dma_start(consts[:, C_BLK:], a["consts"][:, C_BLK:]).then_inc(s_consts, 16)
                    sp.wait_ge(s_consts, 16)

                @block.scalar
                def _(act):
                    act.wait_ge(s_cond, 16)
                    nc.scalar.activation(csilu[:, :, :, :], cond[:, :, :, :], ACT.Silu).then_inc(s_csilu, 1)
                    act.wait_ge(s_wqkv, 48)
                    nc.scalar.copy(wq_hi[:, :, :, :], wqkv[:, :, :, :]).then_inc(s_whi, 1)
                    act.wait_ge(s_modd, 1)
                    act.wait_ge(s_bias, 48)

                    def modulate(g):
                        act.wait_ge(s_lnt, g + 1)
                        ln_modulate(0, SHIFT_A, SCALE_A, g, 0)
                        high_h(0, SHIFT_A, SCALE_A, g, 0).then_inc(s_h, 1)

                    modulate(0)
                    for g in range(NG):
                        if g + 1 < NG:
                            modulate(g + 1)
                        for m in range(KC):
                            act.wait_ge(s_proj, 6 * g + m + 1)
                            nc.scalar.activation(qt[:, m, g * GW:(g + 1) * GW], ps[:, 2 + m, :], ACT.Identity,
                                                 bias=bqk[:, 0, m:m + 1]).then_inc(s_pev_a, 1)

                @block.vector
                def _(dve):
                    link = chain("a_dve", dve)
                    dve.wait_ge(s_csilu, 1)
                    for b in range(BATCH):
                        last = nc.vector.tensor_copy(crep[:, b], bc(csilu[:, 0, :, b], 2, P))
                    last.then_inc(s_crep, 1)
                    dve.wait_ge(s_const, 16)
                    nc.vector.tensor_copy(cbf[:, :], consts[:, 0:384]).then_inc(s_cb, 1)
                    dve.wait_ge(s_x[0], 16)
                    ln_stats(0, link)
                    dve.wait_ge(s_x[1], 16)
                    ln_stats(1, link)
                    ln_rows(dve, 0, s_ln, 0)
                    dve.wait_ge(s_modp, 1)
                    link(nc.vector.tensor_copy(ga[:, :, :], ps[:, 1, :].rearrange("p (b d) -> p b d", b=BATCH)))
                    guard(ga[:, :, :], (gat[:, 0], gat[:, 1]), link)
                    mod_finish(0, link, ps[:, 0, 0:24], (0,)).then_inc(s_modd, 1)
                    dve.wait_ge(s_bias, 48)
                    for g in range(NG):
                        if g + 2 < NG:
                            dve.wait_ge(s_x[g + 2], 16)
                            ln_stats(g + 2, link)
                        if g + 1 < NG:
                            ln_rows(dve, g + 1, s_ln, 0)
                        for m in range(KC):
                            dve.wait_ge(s_proj, 6 * g + 2 + m + 1)
                            nc.vector.tensor_scalar(kt[:, m, g * GW:(g + 1) * GW], ps[:, 4 + m, :],
                                                    bqk[:, 1, m:m + 1], None, ALU.add).then_inc(s_pev_d, 1)
                        for m in range(2):
                            dve.wait_ge(s_proj, 6 * g + 4 + m + 1)
                            nc.vector.tensor_copy(vtok[:, 4 * g + 2 * m:4 * g + 2 * m + 2, :],
                                                  ps[:, 6 + m, :].rearrange("p (t d) -> p t d", t=2))\
                                .then_inc(s_pev_d, 1)
                    dve.wait_ge(s_modp, 2)
                    mod_finish(0, link, ps[:, 0, 0:24], (1,))

                @block.gpsimd
                def _(pool):
                    nc.gpsimd.memset(half[:, :], -0.5).then_inc(s_half, 1)
                    pool.wait_ge(s_half, 1)
                    ln_pool(pool, 0, range(2))
                    pool.wait_ge(s_whi, 1)
                    nc.gpsimd.tensor_tensor(wq_lo[:, :, :, :], wqkv[:, :, :, :], wq_hi[:, :, :, :].bitcast(F32),
                                            ALU.subtract).then_inc(s_wlo, 1)
                    for g in range(NG):
                        if g + 2 < NG:
                            ln_pool(pool, 0, (g + 2,))
                        low_h(pool, g, s_h).then_inc(s_hlo, 1)

                @block.tensor
                def _(pe):
                    pe.wait_ge(s_csilu, 1)
                    pe.wait_ge(s_wmods[0], 16)
                    mod_columns(0, wmod, ps[:, 0, 0:24], range(6))
                    pe.wait_ge(s_crep, 1)
                    for b in range(BATCH):
                        for k in range(KC):
                            last = nc.tensor.matmul(ps[:, 1, b * D:(b + 1) * D], crep[:, b, k, :],
                                                    wmod[:, k, GATE_A * D:(GATE_A + 1) * D],
                                                    start=k == 0, stop=k == KC - 1)
                    last.then_inc(s_modp, 1)
                    pe.wait_ge(s_modd, 1)
                    pe.wait_ge(s_const, 16)
                    pe.wait_ge(s_wqkv, 48)
                    pe.wait_ge(s_wlo, 1)
                    pe.wait_ge(s_ln, 1)
                    ln_transposes(0, 0).then_inc(s_lnt, 1)
                    for g in range(NG):
                        pe.wait_ge(s_h, g + 1)
                        for w in range(2):
                            for m in range(KC):
                                if g:
                                    pe.wait_ge(s_pev_a if w == 0 else s_pev_d,
                                               2 * (g - 1) + m + 1 if w == 0 else 4 * (g - 1) + m + 1)
                                for n, wt in enumerate((wq_hi, wq_lo)):
                                    for k in range(KC):
                                        nc.tensor.matmul(ps[:, 2 + 2 * w + m, :], wt[:, w, k, m * P:(m + 1) * P],
                                                         h_hi[:, k, g * GW:(g + 1) * GW],
                                                         start=n == 0 and k == 0, stop=False)
                        if g + 1 < NG:
                            pe.wait_ge(s_ln, g + 2)
                            ln_transposes(g + 1, 0).then_inc(s_lnt, 1)
                        pe.wait_ge(s_hlo, g + 1)
                        for w in range(2):
                            for m in range(KC):
                                for k in range(KC):
                                    last = nc.tensor.matmul(ps[:, 2 + 2 * w + m, :], wq_hi[:, w, k, m * P:(m + 1) * P],
                                                            h_lo[:, k, g * GW:(g + 1) * GW],
                                                            start=False, stop=k == KC - 1)
                                last.then_inc(s_proj, 1)
                        for m in range(2):
                            if g:
                                pe.wait_ge(s_pev_d, 4 * (g - 1) + 2 + m + 1)
                            for i in range(2):
                                t = 4 * g + 2 * m + i
                                for n, (h, wt) in enumerate(((h_hi, wq_hi), (h_hi, wq_lo), (h_lo, wq_hi))):
                                    for k in range(KC):
                                        last = nc.tensor.matmul(ps[:, 6 + m, i * D:(i + 1) * D],
                                                                h[:, k, t * P:(t + 1) * P], wt[:, 2, k, :],
                                                                start=n == 0 and k == 0, stop=n == 2 and k == KC - 1)
                            last.then_inc(s_proj, 1)
                    pe.wait_ge(s_wmods[1], 16)
                    mod_columns(0, wmod, ps[:, 0, 0:24], range(6, 12)).then_inc(s_modp, 1)

            s_sc, s_mx, s_exp, s_pt, s_ptd, s_pta, s_av, s_out = [sem(n) for n in
                ("b_scores", "b_max", "b_exp", "b_pt", "b_pt_dve", "b_pt_act", "b_av", "b_out")]
            hi_blocks = [t for t in range(NT) if t % TB >= 4]
            s_mod1 = sem("b_mod1")
            with nc.Block() as block:
                @block.sync
                def _(sp):
                    sp.dma_start(wmod[:, :, :], a["wmod1"].rearrange("(k p) n -> p k n", p=P)).then_inc(s_wmod1, 16)

                @block.tensor
                def _(pe):
                    def scores(t):
                        b, i = divmod(t, TB)
                        n = (i + 1) * P
                        if t >= 2:
                            pe.wait_ge(s_exp, t - 1)
                        for lo in range(0, n, GW):
                            w = min(GW, n - lo)
                            out = ps[:, 2 * (t % 2) + lo // GW, 0:w]
                            diag = lo + w == n
                            for k in range(KC):
                                last = nc.tensor.matmul(out, qt[:, k, t * P:(t + 1) * P],
                                                        kt[:, k, b * SEQ + lo:b * SEQ + lo + w],
                                                        start=k == 0, stop=k == KC - 1 and not diag)
                            if diag:
                                last = nc.tensor.matmul(out[:, w - P:w], ident_b, mask_s, start=False, stop=True)
                        last.then_inc(s_sc, 1)

                    def transposes(t):
                        pe.wait_ge(s_exp, t + 1)
                        for j in range(t % TB + 1):
                            if j == 0 and t:
                                pe.wait_ge(s_ptd, t)
                            if j == 4:
                                last.then_inc(s_pt, 1)
                                done = len([u for u in hi_blocks if u < t])
                                if done:
                                    pe.wait_ge(s_pta, done)
                            last = nc.tensor.transpose(ps[:, 4 + j // 4, (j % 4) * P:(j % 4 + 1) * P],
                                                       probs[:, t % 3, j * P:(j + 1) * P], ident)
                        last.then_inc(s_pt, 1)

                    def values(t):
                        b, i = divmod(t, TB)
                        if t >= 2:
                            pe.wait_ge(s_out, t - 1)
                        pe.wait_ge(s_ptd, t + 1)
                        if t in hi_blocks:
                            pe.wait_ge(s_pta, len([u for u in hi_blocks if u <= t]))
                        for j in range(i + 1):
                            last = nc.tensor.matmul(ps[:, 6 + t % 2, 0:D], probs_t[:, t % 2, j * P:(j + 1) * P],
                                                    vtok[:, b * TB + j, :], start=j == 0, stop=j == i)
                        last.then_inc(s_av, 1)

                    scores(0)
                    for t in range(NT):
                        if t + 1 < NT:
                            scores(t + 1)
                        if t:
                            values(t - 1)
                        transposes(t)
                    pe.wait_ge(s_wmod1, 16)
                    mod_columns(1, wmod, ps[:, 0, 0:24], range(12)).then_inc(s_mod1, 1)
                    values(NT - 1)

                def pt_count(t):
                    return t + len([u for u in hi_blocks if u < t]) + 1

                @block.scalar
                def _(act):
                    for t in range(NT + 1):
                        if t < NT:
                            n = (t % TB + 1) * P
                            act.wait_ge(s_mx, t + 1)
                            if t >= 3:
                                act.wait_ge(s_pt, pt_count(t - 2) - 1)
                            nc.scalar.activation(probs[:, t % 3, 0:n],
                                                 ps[:, 2 * (t % 2):2 * (t % 2) + 2, :].rearrange("p a n -> p (a n)")[:, 0:n],
                                                 ACT.Exp, bias=nmx[:, t:t + 1], scale=D ** -0.5,
                                                 accum_out=zs[:, t:t + 1]).then_inc(s_exp, 1)
                        u = t - 1
                        if u in hi_blocks:
                            act.wait_ge(s_pt, pt_count(u) + 1)
                            if u >= 2:
                                act.wait_ge(s_av, u - 1)
                            n = (u % TB + 1) * P
                            nc.scalar.copy(probs_t[:, u % 2, GW:n], ps[:, 5, 0:n - GW]).then_inc(s_pta, 1)

                @block.vector
                def _(dve):
                    link = chain("b_dve", dve)

                    def output(u):
                        dve.wait_ge(s_av, u + 1)
                        link(nc.vector.scalar_tensor_tensor(att[:, u % 2, :], ps[:, 6 + u % 2, 0:D],
                                                            rz[:, u:u + 1], bv[:, :], ALU.mult, ALU.add))
                        link(nc.vector.tensor_tensor(att2[:, u % 2, :], att[:, u % 2, :], ga[:, u // TB, :], ALU.mult))
                        nc.vector.tensor_tensor(x_tok[:, u, :], x_tok[:, u, :], att2[:, u % 2, :],
                                                ALU.add).then_inc(s_out, 1)

                    for t in range(NT + 1):
                        if t < NT:
                            n = (t % TB + 1) * P
                            dve.wait_ge(s_sc, t + 1)
                            link(nc.vector.reduce_max(
                                mx[:, t:t + 1],
                                ps[:, 2 * (t % 2):2 * (t % 2) + 2, :].rearrange("p a n -> p (a n)")[:, 0:n], AX.X))
                            nc.vector.tensor_scalar(nmx[:, t:t + 1], mx[:, t:t + 1], -(D ** -0.5), None,
                                                    ALU.mult).then_inc(s_mx, 1)
                        if t >= 2:
                            output(t - 2)
                        if t >= 1:
                            u = t - 1
                            n = min(u % TB + 1, 4) * P
                            dve.wait_ge(s_pt, pt_count(u))
                            if u >= 2:
                                dve.wait_ge(s_av, u - 1)
                            nc.vector.tensor_copy(probs_t[:, u % 2, 0:n], ps[:, 4, 0:n]).then_inc(s_ptd, 1)
                            link(nc.vector.reciprocal(rz[:, u:u + 1], zs[:, u:u + 1]))
                    dve.wait_ge(s_mod1, 1)
                    mod_finish(1, link, ps[:, 0, 0:24], (0, 1))
                    output(NT - 1)

        raw = sb(ctx, "raw", [P, 3, 3 * D])
        raw_in_moe = [sem(f"d_raw{i}") for i in range(3)]
        wqkv1 = sb(ctx, "wqkv1", [P, 3, KC, D])
        rzb0 = sb(ctx, "rzb0", [P, KC, SEQ])
        wt = rzb0[:, :, :].rearrange("p k n -> p (k n)")[0:E0 + 2, :]
        wq1_hi = sb(ctx, "wqkv1_hi", [P, 3, KC, D], F32R)
        wq1_lo = sb(ctx, "wqkv1_lo", [P, 3, KC, D], F32R)

        with ExitStack() as st:
            E2 = E0 + 2
            gw = sb(st, "gate_w_t", [P, KC, E2])
            lg = sb(st, "logits", [P, NT, E2])
            lrep = sb(st, "lrep", [P, NT, E0])
            top = sb(st, "top", [P, NT, TOPK])
            ex = sb(st, "ex", [P, NT, E0])
            sel = sb(st, "sel", [P, NT, E0])
            wts = sb(st, "wts", [P, NT, E2])
            zsum = sb(st, "zsum", [P, NT])
            esg = sb(st, "esg", [P, NT])
            s_gw, s_ln, s_lnt, s_hhi, s_lg, s_lgc, s_exi, s_exd, s_w, s_wtp, s_wte, s_wst, s_w1, s_w1hi, s_h = \
                [sem(f"c_{n}") for n in ("gw", "ln", "lnt", "h_hi", "lg", "lgc", "exin", "exd", "w", "wtp", "wte",
                                         "wst", "w1", "w1hi", "h")]
            with nc.Block() as block:
                @block.sync
                def _(sp):
                    sp.dma_start(gw[:, :, :], a["gate0"].rearrange("(k p) e -> p k e", p=P)).then_inc(s_gw, 16)
                    for q in range(3):
                        sp.dma_start(raw[:, q, :], a["moe"][q * P:(q + 1) * P, :]).then_inc(raw_in_moe[q], 16)
                    for n, w in enumerate(("wq1", "wk1", "wv1")):
                        sp.dma_start(wqkv1[:, n], a[w].rearrange("(k p) n -> p k n", p=P)).then_inc(s_w1, 16)
                    for g in range(NG):
                        sp.wait_ge(s_wte, g + 1)
                        sp.dma_start(wt_dram[:, g * GW:(g + 1) * GW], wt[:, g * GW:(g + 1) * GW]).then_inc(s_wst, 16)

                @block.scalar
                def _(act):
                    def weights_out(g):
                        act.wait_ge(s_wtp, g + 1)
                        nc.scalar.copy(wt[:, g * GW:(g + 1) * GW], ps[0:E2, 6 + g % 2, :]).then_inc(s_wte, 1)

                    def exponentials(g):
                        act.wait_ge(s_exi, g + 1)
                        nc.scalar.activation(ex[:, 4 * g:4 * g + 4, :], ex[:, 4 * g:4 * g + 4, :], ACT.Exp)
                        nc.scalar.activation(esg[:, 4 * g:4 * g + 4], lg[:, 4 * g:4 * g + 4, E0], ACT.Exp,
                                             scale=-1.0).then_inc(s_exd, 1)

                    def modulate(g):
                        act.wait_ge(s_lnt, g + 1)
                        ln_modulate(0, SHIFT_B, SCALE_B, g, 2 * (g % 2)).then_inc(s_h, 1)
                        high_h(0, SHIFT_B, SCALE_B, g, 2 * (g % 2)).then_inc(s_hhi, 1)

                    modulate(0)
                    for g in range(NG):
                        if g + 1 < NG:
                            modulate(g + 1)
                        act.wait_ge(s_lg, g + 1)
                        nc.scalar.copy(lg[:, 4 * g:4 * g + 4, :],
                                       ps[:, 4 + g % 2, 0:4 * E2].rearrange("p (t e) -> p t e", t=4))\
                            .then_inc(s_lgc, 1)
                        if g == 0:
                            act.wait_ge(s_w1, 48)
                            nc.scalar.copy(wq1_hi[:, :, :, :], wqkv1[:, :, :, :]).then_inc(s_w1hi, 1)
                        if g:
                            exponentials(g - 1)
                        if g >= 2:
                            weights_out(g - 2)
                    exponentials(NG - 1)
                    for g in range(NG - 2, NG):
                        weights_out(g)

                @block.vector
                def _(dve):
                    link = chain("c_dve", dve)

                    def choose(g):
                        ts = slice(4 * g, 4 * g + 4)
                        dve.wait_ge(s_lgc, g + 1)
                        for t in range(4 * g, 4 * g + 4):
                            last = nc.vector.max(top[:, t, :], lg[:, t, 0:E0])
                        link(last)
                        nc.vector.tensor_tensor(ex[:, ts, :], lg[:, ts, 0:E0], bc(top[:, ts, 0], 2, E0),
                                                ALU.subtract).then_inc(s_exi, 1)
                        for t in range(4 * g, 4 * g + 4):
                            last = nc.vector.match_replace(lrep[:, t, :], top[:, t, :], lg[:, t, 0:E0], REPLACED)
                        link(last)
                        link(nc.vector.tensor_tensor(sel[:, ts, :], lrep[:, ts, :], lg[:, ts, 0:E0], ALU.not_equal))

                    def weigh(g):
                        ts = slice(4 * g, 4 * g + 4)
                        dve.wait_ge(s_exd, g + 1)
                        nc.vector.tensor_scalar(esg[:, ts], esg[:, ts], 1.0, None, ALU.add)
                        link(nc.vector.tensor_tensor(ex[:, ts, :], ex[:, ts, :], sel[:, ts, :], ALU.mult))
                        link(nc.vector.tensor_reduce(zsum[:, ts], ex[:, ts, :], AX.X, ALU.add))
                        nc.vector.reciprocal(wts[:, ts, E0], esg[:, ts])
                        link(nc.vector.reciprocal(zsum[:, ts], zsum[:, ts]))
                        nc.vector.tensor_tensor(wts[:, ts, 0:E0], ex[:, ts, :], bc(zsum[:, ts], 2, E0),
                                                ALU.mult).then_inc(s_w, 1)

                    link(nc.vector.memset(wts[:, :, E0 + 1:E0 + 2], 0.0))
                    ln_stats(0, link)
                    ln_stats(1, link)
                    ln_rows(dve, 0, s_ln, 1)
                    ln_stats(2, link)
                    ln_rows(dve, 1, s_ln, 1)
                    for g in range(NG):
                        if g + 3 < NG:
                            ln_stats(g + 3, link)
                        if g + 2 < NG:
                            ln_rows(dve, g + 2, s_ln, 1)
                        if g:
                            weigh(g - 1)
                        choose(g)
                    weigh(NG - 1)

                @block.gpsimd
                def _(pool):
                    ln_pool(pool, 1, range(3))
                    for g in range(NG):
                        if g + 3 < NG:
                            ln_pool(pool, 1, (g + 3,))
                        low_h(pool, g, s_hhi)
                    pool.wait_ge(s_w1hi, 1)
                    nc.gpsimd.tensor_tensor(wq1_lo[:, :, :, :], wqkv1[:, :, :, :], wq1_hi[:, :, :, :].bitcast(F32),
                                            ALU.subtract)

                @block.tensor
                def _(pe):
                    def back(g):
                        pe.wait_ge(s_w, g + 1)
                        if g >= 2:
                            pe.wait_ge(s_wte, g - 1)
                        for i in range(4):
                            last = nc.tensor.transpose(ps[0:E2, 6 + g % 2, i * P:(i + 1) * P],
                                                       wts[:, 4 * g + i, :], ident)
                        last.then_inc(s_wtp, 1)

                    pe.wait_ge(s_gw, 16)
                    pe.wait_ge(s_ln, 1)
                    ln_transposes(0, 0).then_inc(s_lnt, 1)
                    for g in range(NG):
                        if g + 1 < NG:
                            pe.wait_ge(s_ln, g + 2)
                            if g:
                                pe.wait_ge(s_hhi, g)
                            ln_transposes(g + 1, 2 * ((g + 1) % 2)).then_inc(s_lnt, 1)
                        pe.wait_ge(s_h, g + 1)
                        if g >= 2:
                            pe.wait_ge(s_lgc, g - 1)
                        for i in range(4):
                            t = 4 * g + i
                            for k in range(KC):
                                last = nc.tensor.matmul(ps[:, 4 + g % 2, i * E2:(i + 1) * E2],
                                                        h_t[:, k, t * P:(t + 1) * P], gw[:, k, :],
                                                        start=k == 0, stop=k == KC - 1)
                        last.then_inc(s_lg, 1)
                        if g >= 2:
                            back(g - 2)
                    for g in range(NG - 2, NG):
                        back(g)

        def ffn(tag, layer, pairs, w_ap, weighted, raw_in, side=None):
            with ExitStack() as st:
                S = lambda n: sem(f"{tag}_{n}")
                units = 2 * pairs
                W = 3 * D
                w_hi = sb(st, f"{tag}_w_hi", [P, 3, W], F32R)
                w_lo = sb(st, f"{tag}_w_lo", [P, 3, W], F32R)
                wbc = sb(st, f"{tag}_wbc", [P, 3, SEQ]) if weighted else None
                sg = sb(st, f"{tag}_silu", [P, 3, GW])
                prod = sb(st, f"{tag}_prod", [P, 3, GW])
                inter = sb(st, f"{tag}_inter", [P, 3, GW]) if weighted else prod
                i_hi = sb(st, f"{tag}_i_hi", [P, 3, GW], F32R)
                i_lo = sb(st, f"{tag}_i_lo", [P, 3, GW], F32R)
                out_t = sb(st, f"{tag}_out", [P, KC, SEQ])
                wb_in = [S(f"wb{i}") for i in range(3)]
                s_whi, s_wlo, s_gu, s_silu, s_t, s_int, s_ihi, s_ilo, s_dn, s_acc, s_tr, s_add = [S(n) for n in
                    ("whi", "wlo", "gu", "silu", "t", "int", "ihi", "ilo", "dn", "acc", "tr", "add")]
                if not weighted:
                    s_int = s_t
                n_slot = [(pairs + 2 - i) // 3 for i in range(3)]
                HEAD = 4
                loops = (units - HEAD - 2) // 6 if side is None else 0

                def later(b, u, n):
                    return not isinstance(u, int) or b > 0 or u >= n

                def freed(b, u):
                    return b * units if isinstance(u, int) and u < 3 else u + (b * units - 2)

                def pairs_before(b, q):
                    return (b - 1) * pairs + 3 * (n_slot[q] - 1) + q + 1

                with nc.Block() as block:
                    @block.sync
                    def _(sp):
                        def load(b, q, slot):
                            fixed = isinstance(q, int)
                            first, rows_at = (q * P, q * 2) if fixed else (sp.snap(q * P), sp.snap(q * 2))
                            if not fixed or b or q >= 3:
                                sp.wait_ge(s_wlo, pairs_before(b, q) if fixed and q < 3 else
                                           q + (b * pairs - 2))
                            if not fixed or b or q >= 3:
                                sp.dma_start(raw[:, slot, :], w_ap[bass.ds(first, P), :]).then_inc(raw_in[slot], 16)
                            if weighted:
                                if fixed and b == 0 and q == 0:
                                    sp.wait_ge(s_wst, 16 * NG)
                                if not fixed or b or q >= 3:
                                    used = q * 2 + (b * units - 4)
                                    if fixed and b and q < 3:
                                        used = b * units
                                    sp.wait_ge(s_int, used)
                                rows = wt_dram[bass.ds(rows_at, 2), b * SEQ:(b + 1) * SEQ]
                                sp.dma_start(wbc[:, slot, :], bc(rows, 1, P // 2)).then_inc(wb_in[slot], 16)

                        for b in range(BATCH):
                            for q in range(3):
                                load(b, q, q)
                            with sp.Fori(0, (pairs - 3) // 3) as it:
                                for q in range(3):
                                    load(b, it * 3 + (3 + q), q)
                            for q in range(3 + 3 * ((pairs - 3) // 3), pairs):
                                load(b, q, q % 3)

                    @block.tensor
                    def _(pe):
                        def gate_up(b, u, s):
                            slot, g = s // 2, s % 2
                            cols = slice(b * SEQ + g * GW, b * SEQ + (g + 1) * GW)
                            if g == 0:
                                pe.wait_ge(s_wlo, b * pairs + u // 2 + 1 if isinstance(u, int) else pair_of(u, b))
                            if later(b, u, 2):
                                pe.wait_ge(s_t, u + (b * units - 1))
                            for m in range(2):
                                for n, (w, h) in enumerate(((w_hi, h_hi), (w_hi, h_lo), (w_lo, h_hi))):
                                    for k in range(KC):
                                        last = nc.tensor.matmul(ps[:, 2 * g + m, :],
                                                                w[:, slot, k * D + m * P:k * D + (m + 1) * P],
                                                                h[:, k, cols], start=n == 0 and k == 0,
                                                                stop=n == 2 and k == KC - 1)
                            last.then_inc(s_gu, 1)

                        def down(b, u, s):
                            slot, g = s // 2, s % 2
                            fixed = isinstance(u, int)
                            pe.wait_ge(s_ilo, u + (b * units + 1))
                            for c in range(KC):
                                for n, (w, i) in enumerate(((w_hi, i_hi), (w_hi, i_lo), (w_lo, i_hi))):
                                    last = nc.tensor.matmul(ps[:, 4 + 2 * c + g, :],
                                                            w[:, slot, 2 * D + c * P:2 * D + (c + 1) * P],
                                                            i[:, s % 3, :], start=fixed and u < 2 and n == 0,
                                                            stop=fixed and u >= units - 2 and n == 2)
                            last.then_inc(s_dn, 1)

                        pair = {}

                        def pair_of(u, b):
                            return pair["it"] * 3 + (b * pairs + pair["s"] // 2 + 1)

                        def flush(b):
                            pe.wait_ge(s_acc, 4 * b + 4)
                            for t in range(TB):
                                if t >= 4:
                                    pe.wait_ge(s_add, b * TB + t - 3)
                                for c in range(KC):
                                    last = nc.tensor.transpose(ps[:, 4 + t % 4, c * P:(c + 1) * P],
                                                               out_t[:, c, t * P:(t + 1) * P], ident)
                                last.then_inc(s_tr, 1)

                        for b in range(BATCH):
                            gate_up(b, 0, 0)
                            gate_up(b, 1, 1)
                            if b:
                                flush(b - 1)
                                pe.wait_ge(s_add, b * TB)
                            for u in range(2, HEAD):
                                gate_up(b, u, u)
                                down(b, u - 2, u - 2)
                            if loops:
                                with pe.Fori(0, loops) as it:
                                    pair["it"] = it
                                    for s in range(HEAD, HEAD + 6):
                                        pair["s"] = s
                                        gate_up(b, it * 6 + s, s % 6)
                                        down(b, it * 6 + (s - 2), (s - 2) % 6)
                            for u in range(HEAD + 6 * loops, units):
                                gate_up(b, u, u % 6)
                                down(b, u - 2, (u - 2) % 6)
                            for u in range(units - 2, units):
                                down(b, u, u % 6)
                        flush(BATCH - 1)

                    @block.scalar
                    def _(act):
                        def weights_hi(b, q, slot, loads, before):
                            act.wait_ge(raw_in[slot], loads)
                            if before is not None:
                                act.wait_ge(s_dn, before)
                            nc.scalar.copy(w_hi[:, slot, :], raw[:, slot, :]).then_inc(s_whi, 1)

                        def inter_hi(b, u, s):
                            act.wait_ge(s_int, u + (b * units + 1))
                            if later(b, u, 3):
                                act.wait_ge(s_dn, freed(b, u))
                            nc.scalar.copy(i_hi[:, s % 3, :], inter[:, s % 3, :]).then_inc(s_ihi, 1)

                        def step(b, u, s):
                            if s % 2 == 0:
                                slot = (s // 2 + 1) % 3
                                if isinstance(u, int):
                                    q = u // 2 + 1
                                    if q < pairs:
                                        weights_hi(b, q, slot, 16 * (b * n_slot[slot] + q // 3 + 1),
                                                   b * units + u - 2 if q >= 3 else
                                                   2 * pairs_before(b, q) if b else None)
                                else:
                                    first = loop_s[0] // 2 + 1
                                    weights_hi(b, None, slot, loop_it[0] * 16 + 16 * (b * n_slot[slot] + first // 3 + 1),
                                               u + (b * units - 2))
                            act.wait_ge(s_gu, u + (b * units + 1))
                            if later(b, u, 3):
                                act.wait_ge(s_t, freed(b, u))
                            nc.scalar.activation(sg[:, s % 3, :], ps[:, 2 * (s % 2), :], ACT.Silu).then_inc(s_silu, 1)
                            if not isinstance(u, int) or u >= 1:
                                inter_hi(b, u + (-1), (s - 1) % 6)

                        loop_it, loop_s = [None], [None]

                        def evacuate(b):
                            act.wait_ge(s_dn, (b + 1) * units)
                            for c in range(KC):
                                for g in range(GB):
                                    nc.scalar.activation(out_t[:, c, g * GW:(g + 1) * GW], ps[:, 4 + 2 * c + g, :],
                                                         ACT.Identity, scale=mod_col(layer, GATE_B, c, b))\
                                        .then_inc(s_acc, 1)

                        for b in range(BATCH):
                            weights_hi(b, 0, 0, 16 * (b * n_slot[0] + 1), 2 * pairs_before(b, 0) if b else None)
                            if b:
                                evacuate(b - 1)
                            for u in range(HEAD):
                                step(b, u, u)
                            if loops:
                                with act.Fori(0, loops) as it:
                                    loop_it[0] = it
                                    for s in range(HEAD, HEAD + 6):
                                        loop_s[0] = s
                                        step(b, it * 6 + s, s % 6)
                            for u in range(HEAD + 6 * loops, units):
                                step(b, u, u % 6)
                                if side:
                                    side[0](act, b * units + u)
                            inter_hi(b, units - 1, (units - 1) % 6)
                        evacuate(BATCH - 1)

                    @block.vector
                    def _(dve):
                        def inter_lo(b, u, s):
                            dve.wait_ge(s_ihi, u + (b * units + 1))
                            nc.vector.tensor_tensor(i_lo[:, s % 3, :], inter[:, s % 3, :],
                                                    i_hi[:, s % 3, :].bitcast(F32), ALU.subtract).then_inc(s_ilo, 1)

                        def step(b, u, s):
                            dve.wait_ge(s_silu, u + (b * units + 1))
                            if later(b, u, 3):
                                dve.wait_ge(s_int if weighted else s_ilo, freed(b, u))
                            nc.vector.tensor_tensor(prod[:, s % 3, :], sg[:, s % 3, :], ps[:, 2 * (s % 2) + 1, :],
                                                    ALU.mult).then_inc(s_t, 1)
                            if not isinstance(u, int) or u >= 1:
                                inter_lo(b, u + (-1), (s - 1) % 6)

                        def add_back(b):
                            for t in range(TB):
                                dve.wait_ge(s_tr, b * TB + t + 1)
                                nc.vector.tensor_tensor(x_tok[:, b * TB + t, :], ps[:, 4 + t % 4, 0:D],
                                                        x_tok[:, b * TB + t, :], ALU.add).then_inc(s_add, 1)

                        for b in range(BATCH):
                            for u in range(HEAD):
                                step(b, u, u)
                                if b and u == 1:
                                    add_back(b - 1)
                                if side:
                                    side[1](dve, b * units + u)
                            if loops:
                                with dve.Fori(0, loops) as it:
                                    for s in range(HEAD, HEAD + 6):
                                        step(b, it * 6 + s, s % 6)
                            for u in range(HEAD + 6 * loops, units):
                                step(b, u, u % 6)
                                if side:
                                    side[1](dve, b * units + u)
                            inter_lo(b, units - 1, (units - 1) % 6)
                        add_back(BATCH - 1)

                    @block.gpsimd
                    def _(pool):
                        def weights_lo(count, slot):
                            pool.wait_ge(s_whi, count)
                            nc.gpsimd.tensor_tensor(w_lo[:, slot, :], raw[:, slot, :], w_hi[:, slot, :].bitcast(F32),
                                                    ALU.subtract).then_inc(s_wlo, 1)

                        def weigh(b, u, s, loads):
                            if s % 2 == 0:
                                pool.wait_ge(wb_in[s // 2], loads)
                            pool.wait_ge(s_t, u + (b * units + 1))
                            if later(b, u, 3):
                                pool.wait_ge(s_ilo, freed(b, u))
                            nc.gpsimd.tensor_tensor(inter[:, s % 3, :], prod[:, s % 3, :],
                                                    wbc[:, s // 2, (s % 2) * GW:(s % 2 + 1) * GW],
                                                    ALU.mult).then_inc(s_int, 1)

                        def straight(b, u):
                            if u % 2 == 0 and u // 2 + 1 < pairs:
                                weights_lo(b * pairs + u // 2 + 2, (u // 2 + 1) % 3)
                            if weighted:
                                weigh(b, u, u % 6, 16 * (b * n_slot[(u // 2) % 3] + u // 6 + 1))

                        for b in range(BATCH):
                            weights_lo(b * pairs + 1, 0)
                            for u in range(HEAD):
                                straight(b, u)
                            if loops:
                                with pool.Fori(0, loops) as it:
                                    for s in range(HEAD, HEAD + 6):
                                        if s % 2 == 0:
                                            weights_lo(it * 3 + (b * pairs + s // 2 + 2), (s // 2 + 1) % 3)
                                        if weighted:
                                            weigh(b, it * 6 + s, s % 6,
                                                  it * 16 + 16 * (b * n_slot[(s // 2) % 3] + s // 6 + 1))
                            for u in range(HEAD + 6 * loops, units):
                                straight(b, u)

        ffn("d", 0, PAIRS0, a["moe"], True, raw_in_moe)

        recycle(kept)

        cxt0, cxl0 = h_t[:, :, SEQ:], h_t[:, :, 0:SEQ]
        z128, rz128 = [wqkv1[:, n].rearrange("p k n -> p (k n)")[:, 0:BATCH * P].rearrange("p (b n) -> p b n", b=BATCH)
                       for n in range(2)]
        wo = sb(ctx, "wo", [P, KC, D])
        bo = sb(ctx, "bo", [P, KC])
        s_wo, s_z0, s_rz0, s_rst0, s_c0, s_rzb0 = [sem(f"f_{n}") for n in ("wo", "z0", "rz0", "rst0", "ctx0", "rzb0")]

        def load_sums(sp, b, ready):
            rows = ctx_dram.rearrange("(u r) n -> u r n", r=CXR)[b * HEADS:(b + 1) * HEADS, HD, :]
            sp.dma_start(z128[:, b, :], rows.rearrange("u (a n) -> u a n", a=P // HEADS)).then_inc(ready, 16)

        def load_context(sp, b, high, low, ready):
            rows = ctx_dram.rearrange("(u r) n -> u r n", r=CXR)
            for k in range(KC):
                u = b * HEADS + k * P // HD
                for dst, r in ((high, 0), (low, 32)):
                    sp.dma_start(dst[:, k, :], rows[u:u + P // HD, r:r + HD, :]).then_inc(ready, 16)

        def store_inverse(sp, b, done):
            sp.dma_start(rz_dram[b * HEADS:(b + 1) * HEADS, :].rearrange("u (a n) -> (u a) n", a=P // HEADS),
                         rz128[:, b, :]).then_inc(done, 16)

        def spread_inverse(sp, b, dst, ready):
            for k in range(KC):
                u = b * HEADS + k * P // HD
                sp.dma_start(dst[:, k, :], bc(rz_dram[u:u + P // HD, :], 1, HD)).then_inc(ready, 16)

        with ExitStack() as vst:
            vs = sb(vst, "v_halves", [P, BATCH * HEADS, TB, CXR], F32R)
            ones = sb(vst, "ones", [P, BATCH * HEADS * TB])
            NS = 4
            qs = sb(vst, "qs", [P, NS, SEQ], BF16)
            ks = sb(vst, "ks", [P, NS, SEQ], BF16)
            mparts = sb(vst, "mparts", [P, P], BF16)
            parts = sb(vst, "parts", [P, 4, 3, GW], BF16)
            part1, part2, part3 = [parts[:, :, n, :] for n in range(3)]
            qk_in = [sem(f"f_qk{i}") for i in range(NS)]
            s_sts = [sem(f"e_st{i}") for i in range(4)]

            def load_qk(sp, row, slot):
                for r, n in ((0, 3), (3 * HD, 2), (5 * HD, 1)):
                    sp.dma_start(qs[r:r + n * HD, slot, :],
                                 qk_dram[0, 0:n, bass.ds(row, HD), :]).then_inc(qk_in[slot], 16)
                    sp.dma_start(ks[r:r + n * HD, slot, :],
                                 bc(qk_dram[1, 3 - n, bass.ds(row, HD), :], 0, n)).then_inc(qk_in[slot], 16)

            with ExitStack() as st:
                rest = rzb0[:, :, :].rearrange("p k (r n) -> p (k r) n", n=GW)
                wq_hi, wq_lo = wq1_hi, wq1_lo
                s_ln, s_lnt, s_h, s_hlo, s_proj, s_p1, s_rest, s_p2, s_p3, s_vhi, s_v, s_fill = [sem(f"e_{n}") for n in
                    ("ln", "lnt", "h", "h_lo", "proj", "p1", "rest", "p2", "p3", "vhi", "v", "fill")]
                gap = vs[:, :, :, HD:32].rearrange("p u t d -> p (u t) d")
                NJ = 4 * NG
                v_tile = lambda t: vs[:, (t // TB) * HEADS:(t // TB + 1) * HEADS, t % TB, :]
                v_bank = lambda t: ps[:, 6 + (t % 4) // 2, (t % 2) * D:(t % 2 + 1) * D]\
                    .rearrange("p (h d) -> p h d", h=HEADS)
                with nc.Block() as block:
                    @block.sync
                    def _(sp):
                        for j in range(NJ):
                            g, w, m = j // 4, (j // 2) % 2, j % 2
                            b, col = g // GB, (g % GB) * GW
                            if j == 8:
                                for i in range(4):
                                    sp.wait_ge(s_sts[i], 16 * 2)
                                sp.wait_ge(s_fill, 1)
                            if j in (8, 10):
                                load_qk(sp, (j - 8) // 2 * HD, (j - 8) // 2)
                            sp.wait_ge(s_p3, j + 1)
                            sp.dma_start(qk_dram[w, :, b * D + m * P:b * D + (m + 1) * P, col:col + GW]
                                         .rearrange("n p c -> p n c"), parts[:, j % 4]).then_inc(s_sts[j % 4], 16)

                    @block.scalar
                    def _(act):
                        def modulate(g):
                            act.wait_ge(s_lnt, g + 1)
                            ln_modulate(1, SHIFT_A, SCALE_A, g, 0)
                            high_h(1, SHIFT_A, SCALE_A, g, 0).then_inc(s_h, 1)

                        def second(j):
                            act.wait_ge(s_rest, j + 1)
                            nc.scalar.copy(part2[:, j % 4, :], rest[:, j % 4, :]).then_inc(s_p2, 1)

                        modulate(0)
                        for g in range(NG):
                            if g + 1 < NG:
                                modulate(g + 1)
                            for j in range(4 * g, 4 * g + 4):
                                act.wait_ge(s_proj, 6 * g + j % 4 + 1)
                                if j >= 4:
                                    act.wait_ge(s_sts[j % 4], 16 * (j // 4))
                                nc.scalar.copy(part1[:, j % 4, :], ps[:, 2 + j % 4, :]).then_inc(s_p1, 1)
                                if j % 4:
                                    second(j - 1)
                            second(4 * g + 3)
                            for t in range(4 * g, 4 * g + 4):
                                act.wait_ge(s_proj, 6 * g + 4 + (t % 4) // 2 + 1)
                                nc.scalar.copy(v_tile(t)[:, :, 0:HD], v_bank(t)).then_inc(s_vhi, 1)

                    @block.vector
                    def _(dve):
                        link = chain("e_dve", dve)
                        ln_stats(0, link)
                        ln_stats(1, link)
                        ln_rows(dve, 0, s_ln, 2)
                        ln_rows(dve, 1, s_ln, 2)
                        nc.vector.memset(ks[:, :, :], 1.0)
                        nc.vector.memset(qs[:, :, :], 0.0).then_inc(s_fill, 1)
                        link(nc.vector.memset(ones[:, :], 1.0))
                        nc.vector.memset(gap.bitcast(F32)[:, :, 1:], 0.0)
                        nc.vector.tensor_copy(gap[:, :, 0], ones[:, :])
                        for g in range(NG):
                            if g + 2 < NG:
                                ln_stats(g + 2, link)
                                ln_rows(dve, g + 2, s_ln, 2)
                            for j in range(4 * g, 4 * g + 4):
                                dve.wait_ge(s_p1, j + 1)
                                if j >= 4:
                                    dve.wait_ge(s_p3, j - 3)
                                nc.vector.tensor_tensor(rest[:, j % 4, :], ps[:, 2 + j % 4, :], part1[:, j % 4, :],
                                                        ALU.subtract).then_inc(s_rest, 1)
                            for t in range(4 * g, 4 * g + 4):
                                dve.wait_ge(s_vhi, t - t % 2 + 2)
                                last = nc.vector.tensor_tensor(v_tile(t)[:, :, 32:CXR], v_bank(t),
                                                               v_tile(t)[:, :, 0:HD].bitcast(F32), ALU.subtract)
                                if t % 2:
                                    last.then_inc(s_v, 1)

                    @block.gpsimd
                    def _(pool):
                        ln_pool(pool, 2, range(2))
                        low_h(pool, 0, s_h).then_inc(s_hlo, 1)
                        for g in range(NG):
                            if g + 2 < NG:
                                ln_pool(pool, 2, (g + 2,))
                            if g + 1 < NG:
                                low_h(pool, g + 1, s_h).then_inc(s_hlo, 1)
                            for j in range(4 * g, 4 * g + 4):
                                pool.wait_ge(s_p2, j + 1)
                                nc.gpsimd.tensor_tensor(part3[:, j % 4, :], rest[:, j % 4, :], part2[:, j % 4, :],
                                                        ALU.subtract).then_inc(s_p3, 1)
                        nc.gpsimd.memset(mparts[:, :], 0.0)

                    @block.tensor
                    def _(pe):
                        pe.wait_ge(s_ln, 1)
                        ln_transposes(0, 0).then_inc(s_lnt, 1)
                        for g in range(NG):
                            pe.wait_ge(s_h, g + 1)
                            for w in range(2):
                                for m in range(KC):
                                    if g:
                                        pe.wait_ge(s_p1, 4 * (g - 1) + 2 * w + m + 1)
                                        pe.wait_ge(s_rest, 4 * (g - 1) + 2 * w + m + 1)
                                    for n, wt in enumerate((wq_hi, wq_lo)):
                                        for k in range(KC):
                                            nc.tensor.matmul(ps[:, 2 + 2 * w + m, :], wt[:, w, k, m * P:(m + 1) * P],
                                                             h_hi[:, k, g * GW:(g + 1) * GW],
                                                             start=n == 0 and k == 0, stop=False)
                            if g + 1 < NG:
                                pe.wait_ge(s_ln, g + 2)
                                ln_transposes(g + 1, 0).then_inc(s_lnt, 1)
                            pe.wait_ge(s_hlo, g + 1)
                            for w in range(2):
                                for m in range(KC):
                                    for k in range(KC):
                                        last = nc.tensor.matmul(ps[:, 2 + 2 * w + m, :], wq_hi[:, w, k, m * P:(m + 1) * P],
                                                                h_lo[:, k, g * GW:(g + 1) * GW],
                                                                start=False, stop=k == KC - 1)
                                    last.then_inc(s_proj, 1)
                            for m in range(2):
                                if g:
                                    pe.wait_ge(s_v, 2 * (g - 1) + m + 1)
                                for i in range(2):
                                    t = 4 * g + 2 * m + i
                                    for n, (h, wt) in enumerate(((h_hi, wq_hi), (h_hi, wq_lo), (h_lo, wq_hi))):
                                        for k in range(KC):
                                            last = nc.tensor.matmul(ps[:, 6 + m, i * D:(i + 1) * D],
                                                                    h[:, k, t * P:(t + 1) * P], wt[:, 2, k, :],
                                                                    start=n == 0 and k == 0, stop=n == 2 and k == KC - 1)
                                last.then_inc(s_proj, 1)


            with ExitStack() as st:
                NU = BATCH * HEADS
                KR = 6 * HD
                KM = KR + 3 * TB
                tiles = [(0, j) for j in range(4)] + [(1, j) for j in range(8)]
                NTI = len(tiles)
                RING = 6
                EARLY = 4
                ITEMS = [[(1, EARLY + n)] if n < TB - EARLY else [(1, TB)] if n == 7 else
                         [(2, n - (NTI - EARLY))] if n >= NTI - EARLY else [] for n in range(NTI)]
                LAG = 5
                HI_DVE = (1, 4, 7, 10)
                LO_DVE = (5, 8)
                vnow = sb(st, "v_now", [P, 2, TB, CXR], F32R)
                ptile = xn[:, :, :].rearrange("p (r a) d -> p r (a d)", a=2)
                p_hi = h_hi[:, :, :].rearrange("p k (r n) -> p (k r) n", n=GW)
                p_lo = h_lo[:, :, :].rearrange("p k (r n) -> p (k r) n", n=GW)
                hmax = sb(st, "hmax", [P, 2, TB])
                hrest = sb(st, "hrest", [P, TB])
                blk = sb(st, "blk", [P, TB], BF16)
                cx = raw[0:CXR, :, :].rearrange("p q n -> p (q n)")[:, 0:2 * SEQ].rearrange("p (a n) -> p a n", a=2)
                s_v, s_si, s_mx, s_mp, s_row, s_st, s_exp, s_av, s_cx, s_hia, s_hid, s_lop, s_lod, s_dch = [
                    sem(f"f_{n}") for n in ("v", "s", "mx", "mp", "row", "st", "exp", "av", "cx", "hi_act",
                                            "hi_dve", "lo_pool", "lo_dve", "dve")]
                s_cst = [sem("f_cst0"), sem("f_cst1")]
                s_seen = sem("f_seen")

                def hi_count(u, n):
                    own = [m for m in range(NTI) if (m in HI_DVE) == (n in HI_DVE)]
                    return (s_hid if n in HI_DVE else s_hia), u * len(own) + (own.index(n) + 1)

                def lo_count(u, n):
                    own = [m for m in range(NTI) if (m in LO_DVE) == (n in LO_DVE)]
                    return (s_lod if n in LO_DVE else s_lop), u * len(own) + (own.index(n) + 1)

                def width(n):
                    g, j = tiles[n]
                    return (4 * g + 4 - max(4 * g, j)) * P

                def before(u, n, back):
                    if n >= back:
                        return u, n - back
                    return None if isinstance(u, int) and u == 0 else (u + (-1), n - back + NTI)

                with nc.Block() as block:
                    @block.sync
                    def _(sp):
                        def load(u, slot, used):
                            row = sp.snap(u * HD)
                            sp.wait_ge(s_st, used)
                            load_qk(sp, row, slot)

                        def store(u, par, count):
                            row = u * CXR if isinstance(u, int) else sp.snap(u * CXR)
                            sp.wait_ge(s_cx, count)
                            sp.sem_inc(s_seen, 1)
                            sp.dma_start(ctx_dram[bass.ds(row, CXR), :], cx[:, par, :]).then_inc(s_cst[par], 16)

                        for u in range(2, NS):
                            load_qk(sp, u * HD, u)
                        for i in range(4):
                            sp.wait_ge(s_sts[i], 16 * NG)
                        store(0, 0, 2)
                        with sp.Fori(0, (NU - 4) // 4) as it:
                            for s in range(4):
                                load(it * 4 + (4 + s), s, it * (4 * NTI) + NTI * (1 + s))
                                store(it * 4 + (1 + s), (1 + s) % 2, it * 8 + 2 * (2 + s))
                        for i in range(2):
                            sp.wait_ge(s_cst[i], 16 * (HEADS // 2))
                        load_sums(sp, 0, s_z0)
                        load_context(sp, 0, cxt0, cxl0, s_c0)
                        sp.dma_start(wo[:, :, :], a["wo1"].rearrange("(k p) n -> p k n", p=P)).then_inc(s_wo, 16)
                        sp.dma_start(bo[:, :], a["bo1"]).then_inc(s_wo, 16)
                        for u in range(NU - 3, NU):
                            store(u, u % 2, 2 * u + 2)
                            if u == NU - 2:
                                sp.wait_ge(s_rz0, 1)
                                store_inverse(sp, 0, s_rst0)
                                sp.wait_ge(s_rst0, 16)
                                spread_inverse(sp, 0, rzb0, s_rzb0)
                    @block.gpsimd
                    def _(pool):
                        def lows(u):
                            for n in range(NTI):
                                if n in LO_DVE:
                                    continue
                                pool.wait_ge(*hi_count(u, n))
                                w = width(n)
                                nc.gpsimd.tensor_tensor(p_lo[:, n % RING, 0:w], ptile[:, n % RING, 0:w],
                                                        p_hi[:, n % RING, 0:w].bitcast(F32), ALU.subtract).then_inc(s_lop, 1)

                        lows(0)
                        with pool.Fori(0, NU // 2 - 1) as it:
                            for s in range(2):
                                lows(it * 2 + (1 + s))
                        lows(NU - 1)

                    @block.tensor
                    def _(pe):
                        def s_item(w, u, sl, i):
                            half = (w * (TB + 1) + i) % 2
                            start = isinstance(u, int) and u == 0
                            if i < TB:
                                if i == 0:
                                    pe.wait_ge(qk_in[sl], (u - sl) * (96 // 4) + 96)
                                    if not start:
                                        pe.wait_ge(s_mx, u * TB)
                                elif i == 1:
                                    if not start:
                                        pe.wait_ge(s_row, u)
                                else:
                                    pe.wait_ge(s_mx, u * TB + (i - 1))
                                k = (i + 1) * P
                                for lo in range(0, k, GW):
                                    wd = min(GW, k - lo)
                                    diag = lo + wd == k
                                    out = ps[:, 2 * half + lo // GW, 0:wd]
                                    last = nc.tensor.matmul(out, qs[0:KR, sl, i * P:(i + 1) * P],
                                                            ks[0:KR, sl, lo:lo + wd], start=True, stop=not diag)
                                    if diag:
                                        last = nc.tensor.matmul(out[:, wd - P:wd], ident_b, mask_s, start=False, stop=True)
                                last.then_inc(s_si, 1)
                            else:
                                pe.wait_ge(s_mx, u * TB + TB)
                                pe.wait_ge(s_mp, u + 1)
                                nc.tensor.transpose(ps[:, 2 * half, 0:64].bitcast(BF16), mparts[:, :],
                                                    ident_b).then_inc(s_si, 1)

                        def st_tile(u, sl, n):
                            g, j = tiles[n]
                            q0 = max(4 * g, j)
                            wd = width(n)
                            if n == 0:
                                pe.wait_ge(s_row, u + 1)
                            if before(u, n, 2):
                                pe.wait_ge(s_exp, u * NTI + (n - 1))
                            diag = j >= 4 * g
                            out = ps[:, 4 + n % 2, 0:wd]
                            last = nc.tensor.matmul(out, ks[0:KM, sl, j * P:(j + 1) * P],
                                                    qs[0:KM, sl, q0 * P:q0 * P + wd], start=True, stop=not diag)
                            if diag:
                                last = nc.tensor.matmul(out[:, 0:P], ident_b, mask_t, start=False, stop=True)
                            last.then_inc(s_st, 1)

                        def av_tile(u, par, n):
                            g, j = tiles[n]
                            off = (max(4 * g, j) - 4 * g) * P
                            if n == 0:
                                pe.wait_ge(s_v, u + 1)
                            if j == 0 and not (isinstance(u, int) and u == 0):
                                pe.wait_ge(s_cx, u * 2 + (g - 1))
                            pe.wait_ge(*lo_count(u, n))
                            for i, part in enumerate((p_hi, p_lo)):
                                last = nc.tensor.matmul(ps[0:CXR, 6 + g, off:GW], vnow[:, par, j, :], part[:, n % RING, 0:GW - off],
                                                        start=j == 0 and i == 0, stop=j == 4 * g + 3 and i == 1)
                            last.then_inc(s_av, 1)

                        def unit(u, s):
                            for n in range(NTI):
                                st_tile(u, s % NS, n)
                                for v, i in ITEMS[n]:
                                    if not isinstance(u, int) or u + v < NU:
                                        s_item((s + v) % 4, u + v, (s + v) % NS, i)
                                at = before(u, n, LAG)
                                if at:
                                    av_tile(at[0], s % 2 if n >= LAG else (s + 1) % 2, at[1])

                        for i in range(TB + 1):
                            s_item(0, 0, 0, i)
                        for i in range(EARLY):
                            s_item(1, 1, 1, i)
                        unit(0, 0)
                        with pe.Fori(0, (NU - 4) // 4) as it:
                            for s in range(4):
                                unit(it * 4 + (1 + s), 1 + s)
                        for u in range(NU - 3, NU):
                            unit(u, u % 4)
                        for n in range(NTI - LAG, NTI):
                            av_tile(NU - 1, (NU - 1) % 2, n)

                    @block.scalar
                    def _(act):
                        def context(u, par, g):
                            act.wait_ge(s_av, u * NTI + (4 if g == 0 else NTI))
                            if g == 0 and not (isinstance(u, int) and u < 2):
                                act.wait_ge(s_cst[par], (u - par) * 8)
                            nc.scalar.copy(cx[:, par, g * GW:(g + 1) * GW], ps[0:CXR, 6 + g, :]).then_inc(s_cx, 1)

                        def values(u, slot):
                            at = u if isinstance(u, int) else act.snap(u)
                            if not isinstance(u, int) or u >= 2:
                                act.wait_ge(s_av, u * NTI - NTI)
                            nc.scalar.copy(vnow[:, slot, :, :].rearrange("p t d -> p (t d)"),
                                           vs[:, bass.ds(at, 1), :, :].rearrange("p a t d -> p (a t d)"))\
                                .then_inc(s_v, 1)

                        def high(u, n):
                            if n in HI_DVE:
                                return
                            if before(u, n, RING):
                                act.wait_ge(s_av, u * NTI + (n - RING + 1))
                            act.wait_ge(s_exp, u * NTI + (n + 1))
                            w = width(n)
                            nc.scalar.copy(p_hi[:, n % RING, 0:w], ptile[:, n % RING, 0:w]).then_inc(s_hia, 1)

                        def unit(u, s):
                            for n in range(NTI):
                                w = width(n)
                                act.wait_ge(s_st, u * NTI + (n + 1))
                                at = before(u, n, RING)
                                if at:
                                    act.wait_ge(*lo_count(*at))
                                nc.scalar.activation(ptile[:, n % RING, 0:w], ps[:, 4 + n % 2, 0:w], ACT.Exp,
                                                     scale=HD ** -0.5).then_inc(s_exp, 1)
                                at = before(u, n, 1)
                                if at:
                                    high(*at)
                                if n == LAG + 1 and not (isinstance(u, int) and u == 0):
                                    context(u + (-1), (s + 1) % 2, 1)
                                    if not (isinstance(u, int) and u == NU - 1):
                                        values(u + 1, (s + 1) % 2)
                                if n == LAG + 5:
                                    context(u, s % 2, 0)

                        for u in range(2):
                            values(u, u)
                        unit(0, 0)
                        with act.Fori(0, (NU - 2) // 2) as it:
                            for s in range(2):
                                unit(it * 2 + (1 + s), 1 + s)
                        unit(NU - 1, 1)
                        high(NU - 1, NTI - 1)
                        context(NU - 1, 1, 1)

                    @block.vector
                    def _(dve):
                        nc.vector.tensor_copy(blk[:, :], consts[:, C_BLK:C_BLK + TB]).then_inc(s_dch, 1)
                        dve.wait_ge(s_dch, 1)

                        def maxima(w, u, i):
                            half = (w * (TB + 1) + i) % 2
                            k = (i + 1) * P
                            dve.wait_ge(s_si, u * (TB + 1) + (i + 1))
                            nc.vector.reduce_max(hmax[:, w % 2, i:i + 1],
                                                 ps[:, 2 * half:2 * half + 2, :].rearrange("p a n -> p (a n)")[:, 0:k],
                                                 AX.X).then_inc(s_mx, 1)

                        def link(ins, u, k):
                            ins.then_inc(s_dch, 1)
                            dve.wait_ge(s_dch, u * 3 + (1 + k + 1))

                        def minus_max(w, u):
                            m = hmax[:, w % 2, :]
                            parts = [mparts[:, KR + n * TB:KR + (n + 1) * TB] for n in range(3)]
                            dve.wait_ge(s_mx, u * TB + TB)
                            if not (isinstance(u, int) and u == 0):
                                dve.wait_ge(s_row, u)
                            link(nc.vector.tensor_scalar(parts[0], m, -1.0, None, ALU.mult), u, 0)
                            link(nc.vector.scalar_tensor_tensor(hrest[:, :], m, -1.0, parts[0], ALU.mult, ALU.subtract), u, 1)
                            link(nc.vector.tensor_copy(parts[1], hrest[:, :]), u, 2)
                            nc.vector.tensor_tensor(parts[2], hrest[:, :], parts[1], ALU.subtract).then_inc(s_mp, 1)

                        def max_rows(w, u):
                            half = (w * (TB + 1) + TB) % 2
                            dve.wait_ge(s_si, u * (TB + 1) + (TB + 1))
                            rows = slice(KR, KM)
                            nc.vector.tensor_tensor(qs[rows, w % NS, :].rearrange("p (i q) -> p i q", i=TB),
                                                    bc(ps[rows, 2 * half, 0:64].bitcast(BF16), 1, TB),
                                                    bc(blk[rows, :], 2, P), ALU.mult).then_inc(s_row, 1)

                        def high(u, n):
                            if n not in HI_DVE:
                                return
                            if before(u, n, RING):
                                dve.wait_ge(s_av, u * NTI + (n - RING + 1))
                            dve.wait_ge(s_exp, u * NTI + (n + 1))
                            w = width(n)
                            nc.vector.tensor_copy(p_hi[:, n % RING, 0:w], ptile[:, n % RING, 0:w]).then_inc(s_hid, 1)

                        def low(u, n):
                            if n not in LO_DVE:
                                return
                            dve.wait_ge(*hi_count(u, n))
                            w = width(n)
                            nc.vector.tensor_tensor(p_lo[:, n % RING, 0:w], ptile[:, n % RING, 0:w],
                                                    p_hi[:, n % RING, 0:w].bitcast(F32), ALU.subtract).then_inc(s_lod, 1)

                        for i in range(TB):
                            maxima(0, 0, i)
                        minus_max(0, 0)
                        max_rows(0, 0)

                        for i in range(EARLY):
                            maxima(1, 1, i)

                        def unit(u, s):
                            for n in range(NTI):
                                for v, i in ITEMS[n]:
                                    if i < TB and (not isinstance(u, int) or u + v < NU):
                                        maxima((s + v) % 4, u + v, i)
                                if n == TB - EARLY and (not isinstance(u, int) or u + 1 < NU):
                                    minus_max((s + 1) % 4, u + 1)
                                if n == 7 and (not isinstance(u, int) or u + 1 < NU):
                                    max_rows((s + 1) % 4, u + 1)
                                at = before(u, n, 1)
                                if at:
                                    high(*at)
                                at = before(u, n, 2)
                                if at:
                                    low(*at)

                        unit(0, 0)
                        with dve.Fori(0, (NU - 4) // 4) as it:
                            for s in range(4):
                                unit(it * 4 + (1 + s), 1 + s)
                        for u in range(NU - 3, NU):
                            unit(u, u % 4)
                            if u == NU - 3:
                                dve.wait_ge(s_z0, 16)
                                nc.vector.reciprocal(rz128[:, 0, :], z128[:, 0, :]).then_inc(s_rz0, 1)
                        high(NU - 1, NTI - 1)
                        low(NU - 1, NTI - 2)
                        low(NU - 1, NTI - 1)

        with ExitStack() as keep:
            de = sb(keep, "de_t", [P, KC, NEXP])
            ue = sb(keep, "ue", [P, NEXP // P, D])
            us = sb(keep, "us", [P, NT, NA + NKEY + 1])
            ud = sb(keep, "ud", [P, NT, NA + NKEY])
            with ExitStack() as mid:
                rt = sb(mid, "rt", [P, NT, 2, NKEY])
                with ExitStack() as st:
                    wq = sb(st, "wq_r", [P, KC, R1])
                    keys = sb(st, "keys", [P, 2, NKEY])
                    qr = sb(st, "qr", [P, T])
                    out_t = sb(st, "att_out_t", [P, 2, KC, GW])
                    cxt1 = sb(st, "cxt1", [P, KC, SEQ])
                    cxl1 = sb(st, "cxl1", [P, KC, SEQ])
                    rzb1 = sb(st, "rzb1", [P, KC, SEQ])
                    bg = sb(st, "bias_gate", [P, KC, BATCH])
                    cxt, cxl, rzb = (cxt0, cxt1), (cxl0, cxl1), (rzb0, rzb1)
                    s_w, s_emb, s_z, s_rz, s_rst, s_c, s_bg, s_o, s_gate, s_tr, s_add, s_cs, s_cn, s_ln, s_lnt, \
                        s_h, s_hhi, s_q, s_qe, s_r, s_rea, s_red = [sem(f"g_{n}") for n in
                            ("w", "embed", "z", "rz", "rst", "ctx", "bias", "o", "gate", "tr", "add", "sum", "norm",
                             "ln", "lnt", "h", "h_hi", "q", "qe", "r", "re_act", "re_dve")]
                    s_rzb1 = sem("g_rzb")
                    score_bank = [0, 4, 0, 4, 0, 4, 2, 6]

                    def score_banks(n):
                        return ps[:, score_bank[n]:score_bank[n] + 2, 0:2 * NKEY].rearrange("p h (t k) -> p h t k", t=2)

                    raw_in_mlp = [sem(f"i_raw{i}") for i in range(3)]
                    with nc.Block() as block:
                        @block.sync
                        def _(sp):
                            for i in range(2):
                                sp.wait_ge(s_cst[i], 16 * (NU // 2))
                            load_sums(sp, 1, s_z)
                            load_context(sp, 1, cxt1, cxl1, s_c)
                            sp.dma_start(wq[:, :, :], a["wq_r"].rearrange("(k p) n -> p k n", p=P)).then_inc(s_w, 16)
                            for half in range(2):
                                sp.dma_start(keys[half * 64:(half + 1) * 64, :, :],
                                             a["keys"].rearrange("t d k -> d t k")).then_inc(s_w, 16)
                            sp.wait_ge(s_rz, 1)
                            store_inverse(sp, 1, s_rst)
                            sp.wait_ge(s_rst, 16)
                            spread_inverse(sp, 1, rzb1, s_rzb1)
                            sp.dma_start(de[:, :, :], a["de_t"].rearrange("(k p) e -> p k e", p=P)).then_inc(s_emb, 16)
                            sp.dma_start(ue[:, :, :], a["ue"].rearrange("(e p) h -> p e h", p=P)).then_inc(s_emb, 16)
                            for q in range(3):
                                sp.dma_start(raw[:, q, :], a["mlp"][q * P:(q + 1) * P, :]).then_inc(raw_in_mlp[q], 16)
                            sp.wait_ge(s_emb, 32)

                        @block.scalar
                        def _(act):
                            def routed(n):
                                act.wait_ge(s_r, n + 1)
                                nc.scalar.copy(rt[:, 2 * n:2 * n + 2, :, :], score_banks(n)).then_inc(s_rea, 1)

                            act.wait_ge(s_bg, 1)
                            for g in range(NG + 2):
                                if g < NG:
                                    act.wait_ge(s_o, g + 1)
                                    if g >= 2:
                                        act.wait_ge(s_tr, 2 * (g - 1))
                                    for m in range(KC):
                                        last = nc.scalar.activation(out_t[:, g % 2, m, :], ps[:, m, :], ACT.Identity,
                                                                    bias=bg[:, m, g // GB:g // GB + 1],
                                                                    scale=mod_col(1, GATE_A, m, g // GB))
                                    last.then_inc(s_gate, 1)
                                if g >= 2:
                                    act.wait_ge(s_q, g - 1)
                                    nc.scalar.copy(qr[:, (g - 2) * GW:(g - 1) * GW], ps[:, 2 + g % 2, :]).then_inc(s_qe, 1)
                                if g == NG:
                                    for n in range(TB // 2):
                                        routed(n)
                                if 1 <= g <= NG:
                                    act.wait_ge(s_lnt, g)
                                    ln_modulate(1, SHIFT_B, SCALE_B, g - 1, 6).then_inc(s_h, 1)
                                    high_h(1, SHIFT_B, SCALE_B, g - 1, 6).then_inc(s_hhi, 1)
                            for n in range(TB // 2 + 1, TB, 2):
                                routed(n)

                        @block.vector
                        def _(dve):
                            link = chain("g_dve", dve)

                            def normed(b, k):
                                if (b, k) != (0, 1):
                                    dve.wait_ge(s_cs, 1 if b == 0 else 2 + k)
                                dve.wait_ge(s_rzb[b], 16 * KC)
                                nc.vector.tensor_tensor(cxt[b][:, k, :], cxt[b][:, k, :], rzb[b][:, k, :],
                                                        ALU.mult).then_inc(s_cn, 1)

                            s_rzb = (s_rzb0, s_rzb1)
                            dve.wait_ge(s_wo, 32)
                            nc.vector.tensor_tensor(bg[:, :, :], modc[:, 1, GATE_A * KC:(GATE_A + 1) * KC, :],
                                                    bc(bo[:, :], 2, BATCH), ALU.mult).then_inc(s_bg, 1)
                            dve.wait_ge(s_c0, 16 * 2 * KC)
                            link(nc.vector.tensor_tensor(cxt0[:, 1, :], cxt0[:, 1, :], cxl0[:, 1, :], ALU.add))
                            normed(0, 1)
                            normed(0, 0)
                            dve.wait_ge(s_z, 16)
                            nc.vector.reciprocal(rz128[:, 1, :], z128[:, 1, :]).then_inc(s_rz, 1)
                            for g in range(NG):
                                for i in range(2):
                                    dve.wait_ge(s_tr, 2 * g + i + 1)
                                    t = 4 * g + 2 * i
                                    last = nc.vector.tensor_tensor(x_tok[:, t:t + 2, :],
                                                                   ps[:, 4 + i, :].rearrange("p (t d) -> p t d", t=2),
                                                                   x_tok[:, t:t + 2, :], ALU.add)
                                    last.then_inc(s_add, 1)
                                dve.wait_ge(s_add, 2 * g + 2)
                                ln_stats(g, link)
                                if g == 0:
                                    for k in range(KC):
                                        normed(1, k)
                                ln_rows(dve, g, s_ln, 3)
                            for n in range(TB // 2, TB, 2):
                                dve.wait_ge(s_r, n + 1)
                                nc.vector.tensor_copy(rt[:, 2 * n:2 * n + 2, :, :], score_banks(n)).then_inc(s_red, 1)

                        @block.gpsimd
                        def _(pool):
                            for b, k in ((0, 0), (1, 0), (1, 1)):
                                pool.wait_ge((s_c0, s_c)[b], 16 * 2 * KC)
                                nc.gpsimd.tensor_tensor(cxt[b][:, k, :], cxt[b][:, k, :], cxl[b][:, k, :],
                                                        ALU.add).then_inc(s_cs, 1)
                            for g in range(NG):
                                ln_pool(pool, 3, (g,))
                                low_h(pool, g, s_hhi)

                        @block.tensor
                        def _(pe):
                            def scores(n):
                                if 2 <= n < 6:
                                    pe.wait_ge(s_rea, n - 1)
                                for half in range(2):
                                    for w in range(2):
                                        r = slice(half * 64, half * 64 + 64)
                                        last = nc.tensor.matmul(
                                            ps[:, score_bank[n] + half, w * NKEY:(w + 1) * NKEY],
                                            qr[r, w * SEQ + n * P:w * SEQ + (n + 1) * P], keys[r, w, :],
                                            start=True, stop=True)
                                last.then_inc(s_r, 1)

                            pe.wait_ge(s_wo, 32)
                            for g in range(NG + 2):
                                if g < NG:
                                    if g % GB == 0:
                                        pe.wait_ge(s_cn, KC * (g // GB + 1))
                                    if g:
                                        pe.wait_ge(s_gate, g)
                                    for m in range(KC):
                                        for k in range(KC):
                                            last = nc.tensor.matmul(ps[:, m, :], wo[:, k, m * P:(m + 1) * P],
                                                                    cxt[g // GB][:, k, (g % GB) * GW:(g % GB + 1) * GW],
                                                                    start=k == 0, stop=k == KC - 1)
                                    last.then_inc(s_o, 1)
                                if g >= 2:
                                    if g == 2:
                                        pe.wait_ge(s_w, 48)
                                    pe.wait_ge(s_h, g - 1)
                                    if g >= 4:
                                        pe.wait_ge(s_qe, g - 3)
                                    for k in range(KC):
                                        last = nc.tensor.matmul(ps[:, 2 + g % 2, :], wq[:, k, :],
                                                                h_t[:, k, (g - 2) * GW:(g - 1) * GW],
                                                                start=k == 0, stop=k == KC - 1)
                                    last.then_inc(s_q, 1)
                                if g == NG:
                                    pe.wait_ge(s_qe, NG - 1)
                                    pe.wait_ge(s_add, 2 * NG)
                                    for n in range(TB // 2):
                                        scores(n)
                                if 1 <= g <= NG:
                                    pe.wait_ge(s_ln, g)
                                    if g >= 2:
                                        pe.wait_ge(s_hhi, g - 1)
                                    ln_transposes(g - 1, 6).then_inc(s_lnt, 1)
                                if g < NG:
                                    pe.wait_ge(s_gate, g + 1)
                                    for i in range(2):
                                        if g:
                                            pe.wait_ge(s_add, 2 * (g - 1) + i + 1)
                                        for t in range(2):
                                            for c in range(KC):
                                                at = (2 * i + t) * P
                                                last = nc.tensor.transpose(
                                                    ps[:, 4 + i, t * D + c * P:t * D + (c + 1) * P],
                                                    out_t[:, g % 2, c, at:at + P], ident)
                                        last.then_inc(s_tr, 1)
                            pe.wait_ge(s_qe, NG)
                            pe.wait_ge(s_hhi, NG)
                            for n in range(TB // 2, TB):
                                scores(n)

                s_u = sem("i_us")

                room = xn[:, :, :].rearrange("p t d -> p (t d)").rearrange("p (a t i j) -> p a t i j", a=4, t=NT, i=TOPK)
                cand, csel, cprob, eqa = [room[:, n] for n in range(4)]
                srt = sb(mid, "srt", [P, NT, 2, TOPK])
                ids = sb(mid, "ids", [P, NT, 2, TOPK], U32)
                idf = sb(mid, "idf", [P, NT, 2, TOPK])
                ctop = sb(mid, "ctop", [P, NT, TOPK])
                cntj = sb(mid, "cntj", [P, NT, TOPK])
                rowp = sb(mid, "rowp", [P, NT, TOPK])
                far = sb(mid, "far", [P, NT, TOPK])
                zc = sb(mid, "zc", [P, NT])
                lnz = sb(mid, "lnz", [P, NT])
                rzc = sb(mid, "rzc", [P, NT])
                far_s = sb(mid, "far_s", [P, NT])
                eq = sb(mid, "eq", [P, NKEY, TOPK])
                iota = consts[:, C_IOTA:C_IOTA + NKEY]
                rank = consts[:, C_RANK:C_RANK + TOPK]
                s_cd, s_ce, s_zd, s_lz = [sem(f"i_{n}") for n in ("cd", "ce", "zd", "lz")]
                routing = Tick(sem("i_routing"))
                RANKS = 12

                def route_act(act, k):
                    if k == 9:
                        act.wait_ge(s_cd, 1)
                        nc.scalar.activation(cprob, cand, ACT.Exp).then_inc(s_ce, 1)
                    if k == RANKS + NT:
                        act.wait_ge(s_zd, 1)
                        nc.scalar.activation(lnz[:, :], zc[:, :], ACT.Ln).then_inc(s_lz, 1)

                def route_dve(dve, k):
                    def link(ins):
                        routing.inc(ins)
                        dve.wait_ge(routing.sem, routing.n)

                    flat = lambda v: v.rearrange("p t i j -> p t (i j)")
                    if k < 4:
                        for t in range(4 * k, 4 * k + 4):
                            for w in range(2):
                                last = nc.vector.max(srt[:, t, w, :], rt[:, t, w, :])
                        link(last)
                        for t in range(4 * k, 4 * k + 4):
                            for w in range(2):
                                last = nc.vector.max_index(ids[:, t, w, :], srt[:, t, w, :], rt[:, t, w, :])
                        link(last)
                    elif k == 4:
                        nc.vector.tensor_copy(idf[:, :, :, :], ids[:, :, :, :])
                        for t in range(NT):
                            last = nc.vector.tensor_tensor(cand[:, t], bc(srt[:, t, 0, :], 2, TOPK),
                                                           bc(srt[:, t, 1, :], 1, TOPK), ALU.add)
                        link(last)
                    elif k == 5:
                        for t in range(NT):
                            last = nc.vector.max(ctop[:, t, :], cand[:, t].rearrange("p i j -> p (i j)"))
                        link(last)
                    elif k == 6:
                        for t in range(NT):
                            last = nc.vector.match_replace(csel[:, t].rearrange("p i j -> p (i j)"), ctop[:, t, :],
                                                           cand[:, t].rearrange("p i j -> p (i j)"), REPLACED)
                        link(last)
                    elif k == 7:
                        link(nc.vector.tensor_tensor(flat(csel), flat(csel), flat(cand), ALU.not_equal))
                        nc.vector.tensor_tensor(flat(cand), flat(cand), bc(ctop[:, :, 0], 2, TOPK * TOPK),
                                                ALU.subtract).then_inc(s_cd, 1)
                    elif k == 8:
                        link(nc.vector.tensor_reduce(cntj[:, :, :], csel, AX.X, ALU.add))
                    elif k == 9:
                        for t in range(NT):
                            last = nc.vector.tensor_tensor(eqa[:, t], bc(idf[:, t, 0, :], 1, NA),
                                                           bc(iota[:, 0:NA], 2, TOPK), ALU.is_equal)
                        link(last)
                    elif k == 10:
                        for t in range(NT):
                            last = nc.vector.tensor_tensor(eqa[:, t], eqa[:, t], bc(cntj[:, t, :], 1, NA), ALU.mult)
                        link(last)
                    elif k == 11:
                        link(nc.vector.tensor_reduce(ud[:, :, 0:NA], eqa, AX.X, ALU.add))
                    elif k < RANKS + NT:
                        t = k - RANKS
                        link(nc.vector.tensor_tensor(eq[:, :, :], bc(idf[:, t, 1, :], 1, NKEY), bc(iota, 2, TOPK),
                                                     ALU.is_equal))
                        link(nc.vector.tensor_tensor(eq[:, :, :], eq[:, :, :], bc(rank, 1, NKEY), ALU.mult))
                        link(nc.vector.tensor_reduce(ud[:, t, NA:], eq[:, :, :], AX.X, ALU.add))
                        if t == NT - 1:
                            dve.wait_ge(s_ce, 1)
                            link(nc.vector.tensor_tensor(flat(cprob), flat(cprob), flat(csel), ALU.mult))
                            link(nc.vector.tensor_reduce(rowp[:, :, :], cprob, AX.X, ALU.add))
                            nc.vector.tensor_reduce(zc[:, :], rowp[:, :, :], AX.X, ALU.add).then_inc(s_zd, 1)
                    elif k == RANKS + NT:
                        dve.wait_ge(s_zd, 1)
                        nc.vector.reciprocal(rzc[:, :], zc[:, :])
                        link(nc.vector.tensor_scalar(far[:, :, :], idf[:, :, 0, :], float(NA), None, ALU.is_ge))
                        link(nc.vector.tensor_tensor(far[:, :, :], far[:, :, :], rowp[:, :, :], ALU.mult))
                        link(nc.vector.tensor_reduce(far_s[:, :], far[:, :, :], AX.X, ALU.add))
                        nc.vector.tensor_tensor(us[:, :, NA + NKEY], far_s[:, :], rzc[:, :], ALU.mult)
                    elif k == RANKS + NT + 1:
                        nc.vector.tensor_tensor(us[:, :, NA:NA + NKEY], rt[:, :, 1, :], bc(srt[:, :, 1, 0], 2, NKEY),
                                                ALU.subtract)
                        link(nc.vector.tensor_tensor(us[:, :, 0:NA], rt[:, :, 0, 0:NA], bc(srt[:, :, 0, 0], 2, NA),
                                                     ALU.subtract))
                        dve.wait_ge(s_lz, 1)
                        nc.vector.tensor_tensor(us[:, :, 0:NA], us[:, :, 0:NA], bc(lnz[:, :], 2, NA),
                                                ALU.subtract).then_inc(s_u, 1)

                ffn("i", 1, PAIRS1, a["mlp"], False, raw_in_mlp, (route_act, route_dve))

            with ExitStack() as st:
                NE = NEXP // P
                units = NE * NG
                SELW = C_SELR + P - C_SEL
                sel = sb(st, "sel_r", [P, SELW], F32R)
                sel_b = wqkv1[:, :, :, :].rearrange("p w k n -> p (w k n)")[:, 0:NEXP // 2].bitcast(BF16)
                de_hi, de_lo = [sb(st, n, [P, KC, NEXP], F32R) for n in ("de_hi", "de_lo")]
                ue_hi, ue_lo = [sb(st, n, [P, NEXP // P, D], F32R) for n in ("ue_hi", "ue_lo")]
                us_hi, us_lo = [sb(st, n, [NA + NKEY + 1, T], F32R) for n in ("us_t_hi", "us_t_lo")]
                ud_t = rzb0[:, :, :].rearrange("p k n -> p (k n)")[0:NA + NKEY, 0:T // 2].bitcast(BF16)
                pexp = sb(st, "pexp", [P, NEXP // P, T])
                room = xn[:, :, :].rearrange("p (r a) d -> p r (a d)", a=2)
                score, coef, pex = room[:, 0:2, :], room[:, 2:5, :], room[:, 5:8, :]
                c_hi, c_lo = [w[:, :, :, :].rearrange("p w k n -> p w (k n)") for w in (wq1_hi, wq1_lo)]
                out_t = h_t
                s_selr, s_whi, s_wlo, s_ut, s_uhi, s_ulo, s_ex, s_px, s_pe, s_far = [sem(f"j_{n}") for n in
                    ("selr", "whi", "wlo", "ut", "uhi", "ulo", "ex", "px", "pe", "far")]
                s_sc, s_silu, s_cf, s_chi, s_clo, s_up, s_oe, s_tr, s_add, s_store = [sem(f"j_{n}") for n in
                    ("sc", "silu", "cf", "chi", "clo", "up", "oe", "tr", "add", "store")]
                ROWS = NA + NKEY + 1
                with nc.Block() as block:
                    @block.sync
                    def _(sp):
                        for t in range(NT):
                            sp.wait_ge(s_add, t + 1)
                            sp.dma_start(a["out"][t // TB, (t % TB) * P:(t % TB + 1) * P, :], x_tok[:, t, :])\
                                .then_inc(s_store, 16)
                        sp.wait_ge(s_store, 16 * NT)

                    @block.scalar
                    def _(act):
                        for n in range(NT // 2):
                            act.wait_ge(s_ut, n + 1)
                            nc.scalar.copy(us_hi[:, n * 256:(n + 1) * 256].rearrange("p (s h) -> p h s", h=2),
                                           ps[0:ROWS, 2 * (n % 2), 0:256].rearrange("p (h s) -> p h s", h=2))\
                                .then_inc(s_uhi, 1)
                        for j in range(units):
                            act.wait_ge(s_ex, 2 * j + 1)
                            if j >= 3:
                                act.wait_ge(s_pe, j - 2)
                            nc.scalar.activation(pex[:, j % 3, :], ps[:, 2 * (j % 3), :], ACT.Exp).then_inc(s_px, 1)

                        def high(u):
                            act.wait_ge(s_cf, u + 1)
                            if u >= 3:
                                act.wait_ge(s_up, u - 2)
                            nc.scalar.copy(c_hi[:, u % 3, :], coef[:, u % 3, :]).then_inc(s_chi, 1)

                        for u in range(units):
                            act.wait_ge(s_sc, u + 1)
                            if u >= 2:
                                act.wait_ge(s_cf, u - 1)
                            nc.scalar.activation(score[:, u % 2, :], ps[:, u % 2, :], ACT.Silu).then_inc(s_silu, 1)
                            if u:
                                high(u - 1)
                        high(units - 1)

                    @block.gpsimd
                    def _(pool):
                        nc.gpsimd.tensor_copy(de_hi[:, :, :], de[:, :, :]).then_inc(s_whi, 1)
                        nc.gpsimd.tensor_copy(ue_hi[:, :, :], ue[:, :, :]).then_inc(s_whi, 1)
                        pool.wait_ge(s_whi, 2)
                        nc.gpsimd.tensor_tensor(de_lo[:, :, :], de[:, :, :], de_hi[:, :, :].bitcast(F32),
                                                ALU.subtract).then_inc(s_wlo, 1)
                        nc.gpsimd.tensor_tensor(ue_lo[:, :, :], ue[:, :, :], ue_hi[:, :, :].bitcast(F32),
                                                ALU.subtract).then_inc(s_wlo, 1)

                    @block.vector
                    def _(dve):
                        link = chain("j_dve", dve)
                        nc.vector.tensor_copy(sel[:, :], consts[:, C_SEL:C_SEL + SELW]).then_inc(s_selr, 1)
                        nc.vector.tensor_copy(sel_b, consts[:, C_SEL:C_SEL + NEXP]).then_inc(s_selr, 1)
                        for n in range(NT // 2):
                            cols = slice(n * 256, (n + 1) * 256)
                            view = lambda v: v.rearrange("p (s h) -> p h s", h=2)
                            dve.wait_ge(s_ut, n + 1)
                            nc.vector.tensor_copy(view(ud_t[:, cols]),
                                                  ps[0:NA + NKEY, 2 * (n % 2) + 1, 0:256]
                                                  .rearrange("p (h s) -> p h s", h=2))
                            dve.wait_ge(s_uhi, n + 1)
                            nc.vector.tensor_tensor(view(us_lo[:, cols]),
                                                    ps[0:ROWS, 2 * (n % 2), 0:256].rearrange("p (h s) -> p h s", h=2),
                                                    view(us_hi[:, cols].bitcast(F32)), ALU.subtract).then_inc(s_ulo, 1)
                        for j in range(units):
                            g, e = divmod(j, NE)
                            cols = slice(g * GW, (g + 1) * GW)
                            dve.wait_ge(s_ex, 2 * j + 2)
                            dve.wait_ge(s_px, j + 1)
                            ins = nc.vector.scalar_tensor_tensor(pexp[:, e, cols], ps[:, 2 * (j % 3) + 1, :],
                                                                 float(TOPK) + 0.5, pex[:, j % 3, :],
                                                                 ALU.is_gt, ALU.mult)
                            ins.then_inc(s_pe, 1)
                            if e == NE - 1:
                                dve.wait_ge(s_pe, j - 2)
                                nc.vector.tensor_tensor(pexp[:, 0, cols], ps[:, 6 + g % 2, :], pexp[:, 0, cols],
                                                        ALU.add).then_inc(s_far, 1)
                        dve.wait_ge(s_far, NG)

                        def low(u):
                            dve.wait_ge(s_chi, u + 1)
                            nc.vector.tensor_tensor(c_lo[:, u % 3, :], coef[:, u % 3, :],
                                                    c_hi[:, u % 3, :].bitcast(F32), ALU.subtract).then_inc(s_clo, 1)

                        def finish(g):
                            dve.wait_ge(s_up, NE * (g + 1))
                            for c in range(KC):
                                nc.vector.tensor_scalar(out_t[:, c, g * GW:(g + 1) * GW], ps[:, 2 + 2 * (g % 2) + c, :],
                                                        mod_col(1, GATE_B, c, g // GB), None, ALU.mult).then_inc(s_oe, 1)

                        def add(g):
                            for t in range(4 * g, 4 * g + 4):
                                dve.wait_ge(s_tr, t + 1)
                                nc.vector.tensor_tensor(x_tok[:, t, :], ps[:, 6 + t % 2, 0:D], x_tok[:, t, :],
                                                        ALU.add).then_inc(s_add, 1)

                        for u in range(units):
                            g, e = divmod(u, NE)
                            dve.wait_ge(s_silu, u + 1)
                            if u >= 3:
                                dve.wait_ge(s_clo, u - 2)
                            nc.vector.tensor_tensor(coef[:, u % 3, :], score[:, u % 2, :],
                                                    pexp[:, e, g * GW:(g + 1) * GW], ALU.mult).then_inc(s_cf, 1)
                            if u:
                                low(u - 1)
                            if e == 2 and g:
                                finish(g - 1)
                            if e == 3 and g:
                                add(g - 1)
                        low(units - 1)
                        finish(NG - 1)
                        add(NG - 1)

                    @block.tensor
                    def _(pe):
                        pe.wait_ge(s_u, 1)
                        for n in range(NT // 2):
                            if n >= 2:
                                pe.wait_ge(s_ulo, n - 1)
                            for v, (src, rows) in enumerate(((us, ROWS), (ud, NA + NKEY))):
                                for half in range(2):
                                    last = nc.tensor.transpose(ps[0:rows, 2 * (n % 2) + v, half * P:(half + 1) * P],
                                                               src[:, 2 * n + half, :], ident)
                            last.then_inc(s_ut, 1)
                        pe.wait_ge(s_selr, 2)
                        pe.wait_ge(s_ulo, NT // 2)
                        for j in range(units):
                            g, e = divmod(j, NE)
                            cols = slice(g * GW, (g + 1) * GW)
                            if j >= 3:
                                pe.wait_ge(s_pe, j - 2)
                            if e == 0:
                                if g >= 2:
                                    pe.wait_ge(s_far, g - 1)
                                for n, part in enumerate((us_hi, us_lo)):
                                    nc.tensor.matmul(ps[:, 6 + g % 2, :], sel[0:ROWS, NEXP:NEXP + P], part[:, cols],
                                                     start=n == 0, stop=n == 1)
                            w = sel[0:NA + NKEY, e * P:(e + 1) * P]
                            for n, part in enumerate((us_hi, us_lo)):
                                last = nc.tensor.matmul(ps[:, 2 * (j % 3), :], w, part[0:NA + NKEY, cols],
                                                        start=n == 0, stop=n == 1)
                            last.then_inc(s_ex, 1)
                            nc.tensor.matmul(ps[:, 2 * (j % 3) + 1, :], sel_b[0:NA + NKEY, e * P:(e + 1) * P],
                                             ud_t[:, cols],
                                             start=True, stop=True).then_inc(s_ex, 1)

                        def up(u):
                            g, e = divmod(u, NE)
                            pe.wait_ge(s_clo, u + 1)
                            if e == 0 and g >= 2:
                                pe.wait_ge(s_oe, 2 * (g - 1))
                            for c in range(KC):
                                for n, (w, i) in enumerate(((ue_hi, c_hi), (ue_hi, c_lo), (ue_lo, c_hi))):
                                    last = nc.tensor.matmul(ps[:, 2 + 2 * (g % 2) + c, :], w[:, e, c * P:(c + 1) * P],
                                                            i[:, u % 3, :], start=e == 0 and n == 0,
                                                            stop=e == NE - 1 and n == 2)
                            last.then_inc(s_up, 1)

                        def back(g):
                            pe.wait_ge(s_oe, 2 * g + 2)
                            for t in range(4 * g, 4 * g + 4):
                                if t >= 2:
                                    pe.wait_ge(s_add, t - 1)
                                for c in range(KC):
                                    last = nc.tensor.transpose(ps[:, 6 + t % 2, c * P:(c + 1) * P],
                                                               out_t[:, c, t * P:(t + 1) * P], ident)
                                last.then_inc(s_tr, 1)

                        pe.wait_ge(s_wlo, 2)
                        pe.wait_ge(s_far, NG)
                        LATE = 2
                        for u in range(units + LATE):
                            if u < units:
                                g, e = divmod(u, NE)
                                if u >= 2:
                                    pe.wait_ge(s_silu, u - 1)
                                for n, (w, h) in enumerate(((de_hi, h_hi), (de_hi, h_lo), (de_lo, h_hi))):
                                    for k in range(KC):
                                        last = nc.tensor.matmul(ps[:, u % 2, :], w[:, k, e * P:(e + 1) * P],
                                                                h[:, k, g * GW:(g + 1) * GW],
                                                                start=n == 0 and k == 0, stop=n == 2 and k == KC - 1)
                                last.then_inc(s_sc, 1)
                            if u >= LATE:
                                up(u - LATE)
                            if u >= LATE and u % NE == 0 and u > NE:
                                back(u // NE - 2)
                        back(NG - 1)


def constants():
    import numpy as np
    c = np.zeros((P, C_N), np.float32)
    p = np.arange(P)
    c[:, C_ID:C_ID + P] = np.eye(P)
    c[:, C_MS:C_MS + P] = np.where(p[None, :] > p[:, None], MASKED, 0.0)
    c[:, C_MT:C_MT + P] = np.where(p[:, None] > p[None, :], MASKED, 0.0)
    for r in range(3 * TB):
        c[6 * HD + r, C_BLK + r % TB] = 1.0
    c[:, C_IOTA:C_IOTA + NKEY] = np.arange(NKEY)
    c[:, C_RANK:C_RANK + TOPK] = TOPK - np.arange(TOPK)
    for e in range(NEXP):
        i = NEXP - 1 - e
        c[i // NKEY, C_SEL + e] = 1.0
        c[NA + i % NKEY, C_SEL + e] = 1.0
    c[NA + NKEY, C_SELR] = 1.0
    return c


def laid_out(inputs):
    import numpy as np
    x = {k: np.asarray(v) for k, v in inputs.items()}

    def pack(gates, ups, downs):
        n = gates.shape[0] // P
        g = gates.reshape(n, P, KC, P).transpose(0, 3, 2, 1)
        u = ups.reshape(n, P, KC, P).transpose(0, 3, 2, 1)
        gu = np.concatenate([g, u], axis=3).reshape(n, P, KC * 2 * P)
        return np.ascontiguousarray(np.concatenate([gu, downs.reshape(n, P, D)], axis=2).reshape(n * P, 3 * D))

    zero = np.zeros((I0, D), np.float32)
    gu = x["L0_ffn_gu_w"]
    moe = pack(np.concatenate([gu[:, :I0].reshape(-1, D), x["L0_ffn_sh_gate_w"], zero]),
               np.concatenate([gu[:, I0:].reshape(-1, D), x["L0_ffn_sh_up_w"], zero]),
               np.concatenate([x["L0_ffn_dp_w"].transpose(0, 2, 1).reshape(-1, D),
                               x["L0_ffn_sh_down_w"].T, zero]))
    mlp = pack(x["L1_ffn_gate_w"].T, x["L1_ffn_up_w"].T, x["L1_ffn_down_w"])
    gate0 = np.concatenate([x["L0_ffn_gate_w"], x["L0_ffn_sh_gate1_w"], np.zeros((1, D), np.float32)]).T

    def col(v):
        return v.reshape(KC, P).T

    cond = np.stack([x["L0_c"], x["L1_c"]]).transpose(0, 2, 1).reshape(2, KC, P, BATCH).transpose(2, 0, 1, 3)
    out = {
        "x": x["L0_attn_x"], "cond": cond, "consts": constants(), "wmod0": x["L0_wmod"], "wmod1": x["L1_wmod"],
        "wq0": x["L0_attn_Wq"], "wk0": x["L0_attn_Wk"], "wv0": x["L0_attn_Wv"],
        "bq0": col(x["L0_attn_bq"]), "bk0": col(x["L0_attn_bk"]), "bv0": x["L0_attn_bv"],
        "gate0": gate0, "moe": moe, "mlp": mlp,
        "wq1": x["L1_attn_W_query"], "wk1": x["L1_attn_W_key"], "wv1": x["L1_attn_W_value"],
        "wo1": x["L1_attn_W_out"], "bo1": col(x["L1_attn_b_out"]),
        "wq_r": x["L1_ffn_W_q"], "keys": x["L1_ffn_keys"],
        "de_t": x["L1_ffn_down_embed"][::-1].T, "ue": x["L1_ffn_up_embed"][::-1],
    }
    return {k: np.ascontiguousarray(v) for k, v in out.items()}


def kernel(**inputs):
    import concourse.bacc as bacc
    from concourse.bass_utils import run_bass_kernel_spmd

    nc = bacc.Bacc("TRN2", target_bir_lowering=False, num_devices=1)
    arrays = laid_out(inputs)
    aps = {k: nc.dram_tensor(f"in_{k}", v.shape, F32, kind="ExternalInput").ap() for k, v in arrays.items()}
    aps["out"] = nc.dram_tensor("out_x", (BATCH, SEQ, D), F32, kind="ExternalOutput").ap()
    build(nc, aps)
    r = run_bass_kernel_spmd(nc, [{f"in_{k}": v for k, v in arrays.items()}], core_ids=[0])
    return r.results[0]["out_x"]
```
